# Optimizing a Trainium2 kernel written in Bass

```python
import numpy as np
import jax
import jax.numpy as jnp

def _softmax(x, axis=-1):
    return jax.nn.softmax(x, axis=axis)

def _gelu(x):
    return jax.nn.gelu(x, approximate=True)

def _silu(x):
    return jax.nn.silu(x)

def _sigmoid(x):
    return jax.nn.sigmoid(x)

def _layernorm(x, axis=-1, eps=1e-05):
    m = jnp.mean(x, axis=axis, keepdims=True)
    v = jnp.var(x, axis=axis, keepdims=True)
    return (x - m) / jnp.sqrt(v + eps)

def _scatter_add(tgt, idx, src, axis=0):
    return tgt.at[idx].add(src)

def _segment_sum(src, seg, n):
    return jax.ops.segment_sum(src, seg, n)
kernel_name = 'mk_seq_preln_d1_jaxref_r4_7b0c52'

def setup_inputs(seed: int=0):
    np.random.seed(seed)
    _w = jnp.asarray

    def _L0_attn_setup():
        import jax, jax.numpy as jnp
        import numpy as np
        HID = 256
        NH = 4
        HD = HID // NH
        KS = 4
        C = 64
        EPS = 1e-05
        B = 4
        L = 1024

        def _causal_dwconv(x, w):
            xc = jnp.moveaxis(x, 1, 2)
            y = jax.lax.conv_general_dilated(xc, w, window_strides=(1,), padding=[(w.shape[-1] - 1, 0)], dimension_numbers=('NCH', 'OIH', 'NCH'), feature_group_count=w.shape[0])
            return jnp.moveaxis(jax.nn.silu(y), 1, 2)

        def _forward(x, Wq, Wk, Wv, Wb, conv_q, conv_k, conv_v, g, Wo):
            Bx, Lx, _ = x.shape
            N = Lx // C
            q = _causal_dwconv(x @ Wq, conv_q).reshape(Bx, Lx, NH, HD)
            k = _causal_dwconv(x @ Wk, conv_k).reshape(Bx, Lx, NH, HD)
            v = _causal_dwconv(x @ Wv, conv_v).reshape(Bx, Lx, NH, HD)
            q = q / jnp.linalg.norm(q, axis=-1, keepdims=True)
            k = k / jnp.linalg.norm(k, axis=-1, keepdims=True)
            beta = jax.nn.sigmoid(x @ Wb)
            Q = q.reshape(Bx, N, C, NH, HD)
            K = k.reshape(Bx, N, C, NH, HD)
            V = v.reshape(Bx, N, C, NH, HD)
            bta = beta.reshape(Bx, N, C, NH, 1)
            Kb = K * bta
            Vb = V * bta
            A = jnp.einsum('bnihd,bnjhd->bnij', Kb, K)
            T0 = jnp.eye(C, dtype=x.dtype) - jnp.tril(A, -1)
            col = jnp.arange(C)

            def body(i, T):
                row = jax.lax.dynamic_slice_in_dim(T, i, 1, axis=2)[:, :, 0]
                acc = jnp.einsum('bnj,bnjc->bnc', row, T)
                new_row = jnp.where(col < i, row + acc, row)
                return jax.lax.dynamic_update_slice_in_dim(T, new_row[:, :, None, :], i, axis=2)
            T = jax.lax.fori_loop(1, C, body, T0)
            W = jnp.einsum('bnij,bnjhd->bnihd', T, Kb)
            U = jnp.einsum('bnij,bnjhd->bnihd', T, Vb)

            def chunk_step(S, inp):
                q_i, k_i, w_i, u0 = inp
                Sd = jnp.diagonal(S, axis1=-2, axis2=-1)
                u_i = u0 - w_i * Sd[:, None]
                o_inter = q_i * Sd[:, None]
                A_i = jnp.tril(jnp.einsum('bchd,bchd->bc', q_i, k_i))
                o_intra = A_i[:, :, None, None] * u_i
                S = S + jnp.einsum('bchd,bche->bhde', k_i, u_i)
                return (S, o_inter + o_intra)
            xs = tuple((jnp.moveaxis(a, 1, 0) for a in (Q, K, W, U)))
            S0 = jnp.zeros((Bx, NH, HD, HD), x.dtype)
            S, O = jax.lax.scan(chunk_step, S0, xs)
            o = jnp.moveaxis(O, 0, 1).reshape(Bx, Lx, NH, HD)
            o = o * jax.lax.rsqrt(jnp.mean(o * o, axis=-1, keepdims=True) + EPS) * g
            out = o.reshape(Bx, Lx, NH * HD) @ Wo
            return (out, S)

        def _reference_tuple_inner(x, Wq, Wk, Wv, Wb, conv_q, conv_k, conv_v, g, Wo):
            return _forward(x, Wq, Wk, Wv, Wb, conv_q, conv_k, conv_v, g, Wo)
        key = jax.random.key(seed)
        ks = jax.random.split(key, 9)
        return {'x': jax.random.normal(ks[0], (B, L, HID), jnp.float32), 'Wq': jax.random.normal(ks[1], (HID, HID), jnp.float32) * 0.02, 'Wk': jax.random.normal(ks[2], (HID, HID), jnp.float32) * 0.02, 'Wv': jax.random.normal(ks[3], (HID, HID), jnp.float32) * 0.02, 'Wb': jax.random.normal(ks[4], (HID, NH), jnp.float32) * 0.02, 'conv_q': jax.random.normal(ks[5], (HID, 1, KS), jnp.float32) * 0.5, 'conv_k': jax.random.normal(ks[6], (HID, 1, KS), jnp.float32) * 0.5, 'conv_v': jax.random.normal(ks[7], (HID, 1, KS), jnp.float32) * 0.5, 'g': jnp.ones((HD,), jnp.float32), 'Wo': jax.random.normal(ks[8], (HID, HID), jnp.float32) * 0.02}
    _L0_attn_in = _L0_attn_setup()

    def _L0_ffn_setup():
        import jax, jax.numpy as jnp
        import numpy as np
        D = 256
        F = 4 * D
        E = 8
        NS = 2
        TOP_K = 2
        B, S = (2, 256)
        key = jax.random.key(seed)
        ks = jax.random.split(key, 7)
        w = 1.0 / np.sqrt(D)
        wf = 1.0 / np.sqrt(F)
        return {'x': jax.random.normal(ks[0], (B, S, D), jnp.float32), 'centroids': jax.random.normal(ks[1], (E, D), jnp.float32) * w, 'routing_bias': jnp.zeros((E,), jnp.float32), 'Wfc_r': jax.random.normal(ks[2], (E, F, D), jnp.float32) * w, 'Wproj_r': jax.random.normal(ks[3], (E, D, F), jnp.float32) * wf, 'Wfc_sh': jax.random.normal(ks[4], (NS, F, D), jnp.float32) * w, 'Wproj_sh': jax.random.normal(ks[5], (NS, D, F), jnp.float32) * wf}
    _L0_ffn_in = _L0_ffn_setup()
    _d = {'L0_attn_x': _L0_attn_in['x'], 'L0_attn_Wq': _L0_attn_in['Wq'], 'L0_attn_Wk': _L0_attn_in['Wk'], 'L0_attn_Wv': _L0_attn_in['Wv'], 'L0_attn_Wb': _L0_attn_in['Wb'], 'L0_attn_conv_q': _L0_attn_in['conv_q'], 'L0_attn_conv_k': _L0_attn_in['conv_k'], 'L0_attn_conv_v': _L0_attn_in['conv_v'], 'L0_attn_g': _L0_attn_in['g'], 'L0_attn_Wo': _L0_attn_in['Wo'], 'L0_ffn_centroids': _L0_ffn_in['centroids'], 'L0_ffn_routing_bias': _L0_ffn_in['routing_bias'], 'L0_ffn_Wfc_r': _L0_ffn_in['Wfc_r'], 'L0_ffn_Wproj_r': _L0_ffn_in['Wproj_r'], 'L0_ffn_Wfc_sh': _L0_ffn_in['Wfc_sh'], 'L0_ffn_Wproj_sh': _L0_ffn_in['Wproj_sh']}
    _x0 = _d['L0_attn_x']
    _d['L0_attn_x'] = jax.random.normal(jax.random.fold_in(jax.random.key(seed), 1), (2, 2048, 256), dtype=_x0.dtype)
    del _x0
    return _d

def reference(L0_attn_x, L0_attn_Wq, L0_attn_Wk, L0_attn_Wv, L0_attn_Wb, L0_attn_conv_q, L0_attn_conv_k, L0_attn_conv_v, L0_attn_g, L0_attn_Wo, L0_ffn_centroids, L0_ffn_routing_bias, L0_ffn_Wfc_r, L0_ffn_Wproj_r, L0_ffn_Wfc_sh, L0_ffn_Wproj_sh):

    def _L0_attn_ref(x, Wq, Wk, Wv, Wb, conv_q, conv_k, conv_v, g, Wo):
        import jax, jax.numpy as jnp
        import numpy as np
        HID = 256
        NH = 4
        HD = HID // NH
        KS = 4
        C = 64
        EPS = 1e-05
        B = 4
        L = 1024

        def _causal_dwconv(x, w):
            xc = jnp.moveaxis(x, 1, 2)
            y = jax.lax.conv_general_dilated(xc, w, window_strides=(1,), padding=[(w.shape[-1] - 1, 0)], dimension_numbers=('NCH', 'OIH', 'NCH'), feature_group_count=w.shape[0])
            return jnp.moveaxis(jax.nn.silu(y), 1, 2)

        def _forward(x, Wq, Wk, Wv, Wb, conv_q, conv_k, conv_v, g, Wo):
            Bx, Lx, _ = x.shape
            N = Lx // C
            q = _causal_dwconv(x @ Wq, conv_q).reshape(Bx, Lx, NH, HD)
            k = _causal_dwconv(x @ Wk, conv_k).reshape(Bx, Lx, NH, HD)
            v = _causal_dwconv(x @ Wv, conv_v).reshape(Bx, Lx, NH, HD)
            q = q / jnp.linalg.norm(q, axis=-1, keepdims=True)
            k = k / jnp.linalg.norm(k, axis=-1, keepdims=True)
            beta = jax.nn.sigmoid(x @ Wb)
            Q = q.reshape(Bx, N, C, NH, HD)
            K = k.reshape(Bx, N, C, NH, HD)
            V = v.reshape(Bx, N, C, NH, HD)
            bta = beta.reshape(Bx, N, C, NH, 1)
            Kb = K * bta
            Vb = V * bta
            A = jnp.einsum('bnihd,bnjhd->bnij', Kb, K)
            T0 = jnp.eye(C, dtype=x.dtype) - jnp.tril(A, -1)
            col = jnp.arange(C)

            def body(i, T):
                row = jax.lax.dynamic_slice_in_dim(T, i, 1, axis=2)[:, :, 0]
                acc = jnp.einsum('bnj,bnjc->bnc', row, T)
                new_row = jnp.where(col < i, row + acc, row)
                return jax.lax.dynamic_update_slice_in_dim(T, new_row[:, :, None, :], i, axis=2)
            T = jax.lax.fori_loop(1, C, body, T0)
            W = jnp.einsum('bnij,bnjhd->bnihd', T, Kb)
            U = jnp.einsum('bnij,bnjhd->bnihd', T, Vb)

            def chunk_step(S, inp):
                q_i, k_i, w_i, u0 = inp
                Sd = jnp.diagonal(S, axis1=-2, axis2=-1)
                u_i = u0 - w_i * Sd[:, None]
                o_inter = q_i * Sd[:, None]
                A_i = jnp.tril(jnp.einsum('bchd,bchd->bc', q_i, k_i))
                o_intra = A_i[:, :, None, None] * u_i
                S = S + jnp.einsum('bchd,bche->bhde', k_i, u_i)
                return (S, o_inter + o_intra)
            xs = tuple((jnp.moveaxis(a, 1, 0) for a in (Q, K, W, U)))
            S0 = jnp.zeros((Bx, NH, HD, HD), x.dtype)
            S, O = jax.lax.scan(chunk_step, S0, xs)
            o = jnp.moveaxis(O, 0, 1).reshape(Bx, Lx, NH, HD)
            o = o * jax.lax.rsqrt(jnp.mean(o * o, axis=-1, keepdims=True) + EPS) * g
            out = o.reshape(Bx, Lx, NH * HD) @ Wo
            return (out, S)

        def _reference_tuple_inner(x, Wq, Wk, Wv, Wb, conv_q, conv_k, conv_v, g, Wo):
            return _forward(x, Wq, Wk, Wv, Wb, conv_q, conv_k, conv_v, g, Wo)
        return _reference_tuple_inner(x, Wq, Wk, Wv, Wb, conv_q, conv_k, conv_v, g, Wo)[0]

    def _L0_ffn_ref(x, centroids, routing_bias, Wfc_r, Wproj_r, Wfc_sh, Wproj_sh):
        import jax, jax.numpy as jnp
        import numpy as np
        D = 256
        F = 4 * D
        E = 8
        NS = 2
        TOP_K = 2
        B, S = (2, 256)
        raw = jnp.einsum('bsd,ed->bse', x, centroids)
        routing_scores = jax.nn.sigmoid(raw)
        balanced = jax.nn.sigmoid(raw + routing_bias)
        _, top_idx = jax.lax.top_k(balanced, TOP_K)
        gathered = jnp.take_along_axis(routing_scores, top_idx, axis=-1)
        top_w = jax.nn.softmax(gathered, axis=-1)
        combine = jnp.sum(jax.nn.one_hot(top_idx, E, dtype=x.dtype) * top_w[..., None], axis=-2)
        h_sh = jax.nn.gelu(jnp.einsum('bsd,nfd->bsnf', x, Wfc_sh), approximate=False)
        shared_out = jnp.einsum('bsnf,ndf->bsd', h_sh, Wproj_sh)
        h_r = jax.nn.gelu(jnp.einsum('bsd,efd->bsef', x, Wfc_r), approximate=False)
        expert_out = jnp.einsum('bsef,edf->bsed', h_r, Wproj_r)
        routed_out = jnp.einsum('bsed,bse->bsd', expert_out, combine)
        return x + shared_out + routed_out
    x = L0_attn_x
    x = x + _L0_attn_ref(_layernorm(x, axis=-1), L0_attn_Wq, L0_attn_Wk, L0_attn_Wv, L0_attn_Wb, L0_attn_conv_q, L0_attn_conv_k, L0_attn_conv_v, L0_attn_g, L0_attn_Wo)
    x = x + _L0_ffn_ref(_layernorm(x, axis=-1), L0_ffn_centroids, L0_ffn_routing_bias, L0_ffn_Wfc_r, L0_ffn_Wproj_r, L0_ffn_Wfc_sh, L0_ffn_Wproj_sh)
    return x

_drawn_inputs = setup_inputs


def setup_inputs(seed=0):
    import zlib

    import numpy as np

    out = dict(_drawn_inputs(seed))
    spreads = {'L0_attn_g': (1.0, 0.2), 'L0_ffn_routing_bias': (0.0, 0.1)}
    factors = {}
    for name, (base, spread) in spreads.items():
        noise = np.random.default_rng([zlib.crc32(name.encode()), seed]).standard_normal(out[name].shape)
        drawn = base * np.exp(spread * noise) if base else spread * noise
        out[name] = jnp.asarray(drawn.astype(out[name].dtype))
    for name, factor in factors.items():
        out[name] = (out[name] * factor).astype(out[name].dtype)
    return out
```

```python
from contextlib import ExitStack

import numpy as np

import concourse.bass as bass
from concourse import mybir

ALU = mybir.AluOpType
ACT = mybir.ActivationFunctionType
F32 = mybir.dt.float32
F16 = mybir.dt.float16
I32 = mybir.dt.int32
AX_X = mybir.AxisListType.X

P = 128
BATCH, SEQ, D = 2, 2048, 256
TOK = BATCH * SEQ
NH, HD = 4, 64
CH = 64
TAPS = 4
EPS = 1e-5
DB = D // P

GRP = 512
GT = GRP // P
GROUPS = TOK // GRP
ROUNDS = GROUPS // BATCH
GCH = GRP // CH
LEVELS = 6

FF = 1024
FB = FF // P
N_SH, N_RT, TOPK = 2, 8, 2
SLOTS = N_SH + N_RT
PIECE = 1024
PIECES = 2 * DB * FF // PIECE
XT = 256
XB = XT // P
X_TILES = TOK // XT
R_TILES = TOK * TOPK // XT + N_RT
TTOK = TOK // P
IDX_COLS = R_TILES * XB
X_SCALE = 256.0
W_SCALE = 256.0
H_SCALE = 64.0


class Ring:

    def __init__(self, banks, fills, sem_full, sem_empty):
        self.banks, self.fills = banks, fills
        self.at = {name: i for i, (name, _) in enumerate(fills)}
        self.sem_full, self.sem_empty = sem_full, sem_empty
        self.count = {e: sum(o == e for _, o in fills) for e in sem_empty}
        self.rank = [sum(o == e for _, o in fills[:i]) for i, (_, e) in enumerate(fills)]

    def bank(self, name):
        return self.banks[self.at[name] % len(self.banks)]

    def full(self, n, name):
        return self.sem_full, n * len(self.fills) + self.at[name] + 1

    def empty(self, n, name):
        i = self.at[name]
        e = self.fills[i][1]
        return self.sem_empty[e], n * self.count[e] + self.rank[i] + 1

    def free(self, n, name):
        i = self.at[name]
        if i >= len(self.banks):
            return self.empty(n, self.fills[i - len(self.banks)][0])
        last = [k for k in range(len(self.fills)) if k % len(self.banks) == i % len(self.banks)][-1]
        e = self.fills[last][1]
        return self.sem_empty[e], n * self.count[e]


FRONT_FILLS = (
    [(f"xnT{d}", "act") for d in range(DB)]
    + [(f"proj{m}", "act") for m in range(3 * DB)]
    + [(f"tok{c}{h}", "act" if c < 2 else "dve") for c in range(3) for h in range(2)]
    + [(f"{c}T{d}", "dve" if c == "Q" else "act") for c in ("K", "Kb", "Q") for d in range(DB)]
    + [("AT", "act"), ("X", "dve")]
)
BACK_FILLS = (
    [(f"{w}{s}", "act" if w == "Y" else "dve")
     for s in range(1, LEVELS) for w in ("Y", "Z", "ZT") if (w, s) != ("Z", LEVELS - 1)]
    + [(f"{w}T{d}", "dve") for w in ("W", "U") for d in range(DB)]
    + [(f"otok{h}", "act") for h in range(2)]
    + [(f"oT{d}", "act") for d in range(DB)]
    + [(f"attn{h}", "dve") for h in range(2)]
    + [(f"x2nT{d}", "act") for d in range(DB)]
)


def has(n, k):
    n = val(n)
    return not isinstance(n, int) or n >= k


class Num:

    def __init__(self, v, par, half=None, routed=False):
        self.v, self.par, self.half, self.routed = v, par, half, routed


def val(n):
    return n.v if isinstance(n, Num) else n


def parity(n):
    return n.par if isinstance(n, Num) else n % 2


def half(n):
    return n.half if isinstance(n, Num) else n // 2


def is_routed(n):
    return isinstance(n, Num) and n.routed


def unit_of_routed(i):
    return i + N_SH * X_TILES


def units_through(t, routed):
    return t - X_TILES + N_SH * X_TILES + 1 if routed else N_SH * (t + 1)


def expert_stages(eng, turn, unit, weights, y_shared=None, y_routed=None):
    turn(0)
    unit(0)
    weights(0)

    def shared_tile(t, last=False):
        n, par, h = val(t), parity(t), half(t)
        if not last:
            turn(Num(n + 1, 1 - par, h + par))
        unit(Num(2 * n + 1, 1))
        weights(Num(2 * n + 1, 1, n))
        if y_shared:
            y_shared(Num(2 * n, 0), t)
        if not last:
            unit(Num(2 * n + 2, 0))
            weights(Num(2 * n + 2, 0, n + 1))
        if y_shared:
            y_shared(Num(2 * n + 1, 1), t)

    shared_tile(0)
    shared_tile(1)
    with eng.Fori(1, X_TILES // 2 - 1) as k:
        for j in range(2):
            shared_tile(Num(2 * k + j, j, k))
    shared_tile(X_TILES - 2)
    shared_tile(X_TILES - 1, last=True)

    def routed_up(i, par, h):
        turn(Num(i + X_TILES, par, h, routed=True))
        unit(Num(unit_of_routed(i), par))

    def routed_y(i, par, h):
        if y_routed:
            y_routed(Num(unit_of_routed(i), par), Num(i, par, h))

    routed_up(0, 0, 0)
    with eng.Fori(0, R_TILES // 2 - 1) as k:
        for j in range(2):
            routed_up(2 * k + j + 1, 1 - j, k + j)
            routed_y(2 * k + j, j, k)
    i = R_TILES - 2
    routed_up(i + 1, 1, R_TILES // 2 - 1)
    routed_y(i, 0, i // 2)
    routed_y(i + 1, 1, i // 2)


def weave(front, back):
    going = [front, back]
    while going:
        going = [g for g in going if next(g, StopIteration) is not StopIteration]


def build(nc, x, w_qkv, w_beta, conv_w, g_col, w_o, cent, bias, w_ffn,
          ident, lvl_masks, eye2, block_tri, row_iota, tile_iota, pref, tok_id, out):
    ctx = ExitStack()
    with ctx:
        def sb(name, shape, dt=F32):
            return ctx.enter_context(nc.sbuf_tensor(name, shape, dt))

        def sem(name):
            return ctx.enter_context(nc.semaphore(name))

        base_d = nc.dram_tensor("base_d", (TOK, D), F32).ap()
        x2n_d = nc.dram_tensor("x2n_d", (TOK, D), F32).ap()
        acc_d = nc.dram_tensor("acc_d", (TOK, D), F32).ap()
        ys_d = nc.dram_tensor("ys_d", (R_TILES * XT, D), F32).ap()
        rows_d = nc.dram_tensor("rows_d", (P * IDX_COLS, 1), I32).ap()

        W = sb("W", [P, SLOTS * PIECES, 2, PIECE], F16)
        arena = W[:, N_SH * PIECES:, :, :].rearrange("p a b c -> p (a b c)").bitcast(F32)
        late_room = sb("late_room", [P, 8192])
        rooms = [[arena, 0, N_RT * PIECES * PIECE], [late_room[:], 0, 8192]]

        def early(*shape):
            n = int(np.prod(shape))
            room = next(r for r in rooms if r[1] + n <= r[2])
            a = room[0][:, room[1]:room[1] + n]
            room[1] += n
            if len(shape) == 1:
                return a
            names = "abcd"[:len(shape)]
            return a.rearrange(f"p ({' '.join(names)}) -> p {' '.join(names)}",
                               **{k: s for k, s in zip(names[1:], shape[1:])})

        idt = sb("idt", [P, P])
        wstage = sb("wstage", [P, 2, PIECE])
        logits = sb("logits", [P, TTOK, N_RT])

        def carve(room, start, shape, dt=F32):
            n = int(np.prod(shape)) // (2 if dt == F16 else 1)
            a = room[:, start:start + n]
            a = a.bitcast(dt) if dt != F32 else a
            if len(shape) > 1:
                names = "abcd"[:len(shape)]
                a = a.rearrange(f"p ({' '.join(names)}) -> p {' '.join(names)}",
                                **{k: z for k, z in zip(names[1:], shape[1:])})
            return a, start + n

        late = 0
        xg, bt, yo, xs, hs = [], [], [], [], []
        for tiles, shape, dt in ((xg, (XB, D), F32), (bt, (XB, D), F32), (yo, (XB, D), F32),
                                 (xs, (2, DB, XT), F16), (hs, (2, FB, XT), F16)):
            for _ in range(2):
                tile, late = carve(late_room[:], late, shape, dt)
                tiles.append(tile)
        assert late <= 8192

        at = (N_RT - 1) * PIECES * PIECE
        scr = {}
        for name, shape in (("rc", (2, P)), ("prefc", (N_RT,)), ("biasc", (N_RT,)), ("kc", (X_TILES,)),
                            ("tc", (R_TILES,)), ("onec", (TTOK,)), ("z", (TTOK, N_RT)), ("sc", (TTOK, N_RT)),
                            ("bl", (TTOK, N_RT)), ("oh1", (TTOK, N_RT)), ("oh2", (TTOK, N_RT)),
                            ("mask", (TTOK, N_RT)), ("tmp", (TTOK, N_RT)), ("inc", (TTOK, N_RT)),
                            ("pos", (TTOK, N_RT)), ("m", (TTOK,)), ("mx", (TTOK,)), ("s12", (2, TTOK)),
                            ("p12", (2, TTOK)), ("cmp", (N_RT, X_TILES)), ("nb", (N_RT,)), ("tb", (N_RT,)),
                            ("start", (N_RT,)), ("cmpt", (R_TILES, N_RT)), ("es", (R_TILES,)), ("dd", (TTOK,))):
            scr[name], at = carve(arena, at, shape)
        assert at <= N_RT * PIECES * PIECE
        eid = sb("eid", [P, R_TILES], I32)
        pos_i = sb("pos_i", [P, 2, TTOK], I32)
        lane = sb("lane", [P, 2, TTOK], I32)
        adr = sb("adr", [P, 2, TTOK], I32)
        tid = sb("tid", [P, TTOK], I32)
        wtop = sb("wtop", [P, 2, TTOK])
        idx = sb("idx", [P, IDX_COLS], I32)
        scat = sb("scat", [P, 2, 3], I32)
        gath = sb("gath", [P, 2, XB], I32)

        at = 0
        acc, yrow = [], []
        for _ in range(4):
            tile, at = carve(arena, at, (D,))
            acc.append(tile)
            tile, at = carve(arena, at, (TOPK, D))
            yrow.append(tile)
        lastidx = sb("lastidx", [P, 4, TOPK], I32)

        wqkv = early(DB, 3 * D)
        wo = early(DB, D)
        wb = early(DB, NH)
        cen = early(DB, N_RT)
        cw = early(3 * DB, TAPS)
        gcol = early(DB)
        masks = early(LEVELS, P)
        minus2i = early(P)
        ones = early(P)
        half_neg = early(32)
        xt = [early(GT, D) for _ in range(BATCH)]
        sq = early(2, GT, D)
        xn = sq[:, 0]
        xnT = sq[:, 1].rearrange("p k d -> p (k d)").rearrange("p (d t) -> p d t", d=DB)
        pre = [early(3 * DB, GRP + TAPS - 1) for _ in range(BATCH)]
        qkvT = early(3 * DB, GRP)
        raw = early(3, GT, D)
        KbT = sq[:, 0].rearrange("p k d -> p (k d)").rearrange("p (d t) -> p d t", d=DB)
        KT = [early(DB, GRP) for _ in range(BATCH)]
        QT = [early(DB, GRP) for _ in range(BATCH)]
        Kb = [early(GT, D) for _ in range(BATCH)]
        Vb = [early(GT, D) for _ in range(BATCH)]
        AT = sq[:, 1, 0:2].rearrange("p k d -> p (k d)").rearrange("p (k t) -> p k t", k=GT)
        CT = [early(LEVELS - 1, GT, P) for _ in range(BATCH)]
        X = [early(GT, P) for _ in range(BATCH)]
        XTr = [early(GT, P) for _ in range(BATCH)]
        Y = early(GT, P)
        prod = early(4, GRP)
        Wc = early(2, DB, GCH, BATCH)
        PR = early(2, DB, GCH)
        Sd = [early(DB, GCH + 1) for _ in range(BATCH)]
        qk = early(DB, GCH, BATCH)
        wu = early(DB, GCH, BATCH)
        oT = early(DB, GRP)
        ob = early(GT, D)
        osq = prod[:, 0:2].rearrange("p a t -> p (a t)").rearrange("p (k d) -> p k d", k=GT)
        x2n = ob
        x2nT = oT
        bn = early(GT, 6)
        mv = early(GT, 2)
        rstd = early(GT)
        bn2 = early(GT, 6)
        mv2 = early(GT, 2)
        rstd2 = early(GT)
        ssq = early(2, GT, NH)
        th = early(GT, NH)
        beta = early(GT, NH)
        oss = early(GT, NH)

        ps = ctx.enter_context(nc.psum_tensor("ps", [P, 8, 512], F32))
        small = ps[:, 7, :]
        beta_ps = small[:, 0:GT * NH]
        corr_ps = small[:, 32:32 + GCH * BATCH]
        logit_ps = small[:, 64:64 + GT * N_RT]

        const_in = sem("const_in")
        consts_made = sem("consts_made")
        wo_scaled = sem("wo_scaled")
        x_in = [sem(f"x_in{b}") for b in range(BATCH)]
        stats = sem("stats")
        moments = sem("moments")
        var_eps = sem("var_eps")
        rstd_ready = sem("rstd_ready")
        xn_ready = sem("xn_ready")
        history = sem("history")
        beta_mm = sem("beta_mm")
        beta_tanh = sem("beta_tanh")
        beta_ready = sem("beta_ready")
        pre_ready = sem("pre_ready")
        conv_step = sem("conv_step")
        silu_done = sem("silu_done")
        squares = sem("squares")
        sumsq = sem("sumsq")
        rnorm = sem("rnorm")
        normed = sem("normed")
        normed_v = sem("normed_v")
        masked = sem("masked")
        x0t_ready = sem("x0t_ready")
        inv_sum = sem("inv_sum")
        tt_ready = sem("tt_ready")
        edge_cols = sem("edge_cols")
        chunk_sums = sem("chunk_sums")
        carry = sem("carry")
        one_minus = sem("one_minus")
        scanned = sem("scanned")
        qk_ready = sem("qk_ready")
        corr_mm = sem("corr_mm")
        edge_u = sem("edge_u")
        o_ready = sem("o_ready")
        o_sq = sem("o_sq")
        o_sum = sem("o_sum")
        o_rms = sem("o_rms")
        o_normed = sem("o_normed")
        x2_ready = sem("x2_ready")
        stats2 = sem("stats2")
        rstd2_ready = sem("rstd2_ready")
        x2n_ready = sem("x2n_ready")
        base_ready = sem("base_ready")
        logit_mm = sem("logit_mm")
        logits_kept = sem("logits_kept")
        tokens_out = [sem(f"tokens_out{b}") for b in range(BATCH)]
        w_in = sem("w_in")
        w_scaled = sem("w_scaled")
        w_split = sem("w_split")

        route_in = sem("route_in")
        x_loaded = [sem(f"x_loaded{b}") for b in range(2)]
        base_in = [sem(f"base_in{b}") for b in range(2)]
        x_turned = sem("x_turned")
        x_high = sem("x_high")
        x_low = sem("x_low")
        up_done = sem("up_done")
        gelu_done = sem("gelu_done")
        h_high = sem("h_high")
        h_low = sem("h_low")
        down_done = sem("down_done")
        y_out = sem("y_out")
        y_stored = [sem(f"y_stored{b}") for b in range(2)]
        rw_in = [sem(f"rw_in{b}") for b in range(2)]
        rw_high = sem("rw_high")
        rw_low = sem("rw_low")
        scored = sem("scored")
        route = sem("route")
        mask_ready = sem("mask_ready")
        ranked = sem("ranked")
        picked = sem("picked")
        tops_ready = sem("tops_ready")
        routed = sem("routed")
        rows_zeroed = sem("rows_zeroed")
        rows_out = sem("rows_out")
        x_gathered = [sem(f"x_gathered{b}") for b in range(2)]
        scat_copied = sem("scat_copied")
        scattered = [sem(f"scattered{b}") for b in range(2)]
        idx_in = sem("idx_in")
        gath_copied = sem("gath_copied")
        acc_in = [sem(f"acc_in{b}") for b in range(4)]
        y_in = [sem(f"y_in{b}") for b in range(4)]
        combined = sem("combined")
        out_done = [sem(f"out_done{b}") for b in range(4)]

        fr = Ring([ps[:, b, :] for b in range(3)], FRONT_FILLS, sem("front_full"),
                  {"act": sem("front_act"), "dve": sem("front_dve")})
        bk = Ring([ps[:, b, :] for b in range(3, 7)], BACK_FILLS, sem("back_full"),
                  {"act": sem("back_act"), "dve": sem("back_dve")})

        SH_PIECES = N_SH * PIECES
        assert SH_PIECES == GROUPS
        N_CONST = 10

        def tokens(ap, b, it):
            return ap[bass.ds(b * SEQ + it * GRP, GRP), :].rearrange("(k p) d -> p k d", p=P)

        passed = sem("passed")
        kept, pe_idle, act_idle = sem("kept"), sem("pe_idle"), sem("act_idle")

        def rows_of(ap, t):
            return ap[bass.ds(val(t) * XT, XT), :].rearrange("(k p) d -> p k d", p=P)

        def piece(n, half):
            return W[:, n:n + 1, half, :] if isinstance(n, int) else W[:, bass.ds(n, 1), half, :]

        def weight(slot, k, half, cols):
            if isinstance(slot, int):
                return W[:, slot * PIECES + k, half, cols]
            return W[:, bass.ds(slot + k, 1), half, cols].rearrange("p a n -> p (a n)")

        def x_there(t):
            if is_routed(t):
                return x_gathered[parity(t)], 16 * XB * (half(t) + 1)
            return x_loaded[parity(t)], 16 * (half(t) + 1)

        def settled(eng, s, value):
            eng.wait_ge(s, value)
            eng.sem_inc(passed, 1)

        block = ctx.enter_context(nc.Block())

        @block.sync
        def _(sp):
            sp.dma_start(idt[:], ident).then_inc(const_in, 16)
            sp.dma_start(wqkv, w_qkv).then_inc(const_in, 16)

            def load_x(b, it):
                sp.dma_start(xt[b], tokens(x, b, it)).then_inc(x_in[b], 16)

            load_x(0, 0)
            for dst, src in ((cw, conv_w), (wb, w_beta), (masks, lvl_masks), (minus2i, eye2),
                             (wo, w_o), (gcol, g_col), (cen, cent)):
                sp.dma_start(dst, src).then_inc(const_in, 16)
            sp.dma_start(wstage[:, 0, :], w_ffn[0]).then_inc(w_in, 16)
            load_x(1, 0)

            def store(b, it, more):
                n = 2 * it + b
                sp.wait_ge(base_ready, n + 1)
                sp.dma_start(tokens(base_d, b, it), xt[b]).then_inc(tokens_out[b], 16)
                sp.wait_ge(x2n_ready, GT * (n + 1))
                sp.dma_start(tokens(x2n_d, b, it), x2n).then_inc(tokens_out[b], 16)
                if more:
                    sp.wait_ge(tokens_out[b], 32 * (it + 1))
                    load_x(b, it + 1)
                    sp.wait_ge(w_split, n + 1)
                    sp.dma_start(wstage[:, 0, :], w_ffn[bass.ds(n + 1, 1)].rearrange("a p n -> p (a n)")).then_inc(w_in, 16)
                elif b == 0:
                    sp.wait_ge(w_split, n + 1)
                    sp.dma_start(wstage[:, 0, :], w_ffn[n + 1]).then_inc(w_in, 16)

            with sp.Fori(0, ROUNDS - 1) as it:
                for b in range(BATCH):
                    store(b, it, True)
            for b in range(BATCH):
                store(b, ROUNDS - 1, False)
            for b in range(BATCH):
                sp.wait_ge(tokens_out[b], 32 * ROUNDS)

            for e in (kept, pe_idle, act_idle):
                sp.wait_ge(e, 1)
            for dst, src in ((scr["rc"], block_tri), (scr["prefc"], pref), (scr["biasc"], bias),
                             (scr["kc"], row_iota), (scr["tc"], tile_iota), (tid[:], tok_id)):
                sp.dma_start(dst, src).then_inc(route_in, 16)

            def load_tile(t):
                b = parity(t)
                if has(t, 2):
                    sp.wait_ge(x_turned, val(t) - 1)
                sp.dma_start(xg[b], rows_of(x2n_d, t)).then_inc(x_loaded[b], 16)
                if has(t, 2):
                    sp.wait_ge(y_out, 2 * val(t) - 2)
                sp.dma_start(bt[b], rows_of(base_d, t)).then_inc(base_in[b], 16)

            def load_weights(u):
                b = parity(u)
                if has(u, 2):
                    sp.wait_ge(rw_low, val(u) - 1)
                src = w_ffn[bass.ds(val(u) + SH_PIECES, 1)].rearrange("a p n -> p (a n)")
                sp.dma_start(wstage[:, b, :], src).then_inc(rw_in[b], 16)

            def store_tile(t):
                b = parity(t)
                sp.wait_ge(y_out, 2 * val(t) + 2)
                sp.dma_start(rows_of(acc_d, t), yo[b]).then_inc(y_stored[b], 16)

            sp.wait_ge(w_split, SH_PIECES)
            for t in range(2):
                load_tile(t)
                load_weights(t)
            with sp.Fori(0, X_TILES // 2 - 1) as k:
                for j in range(2):
                    t = Num(2 * k + j, j)
                    load_weights(Num(2 * t.v + 2, 0))
                    load_weights(Num(2 * t.v + 3, 1))
                    store_tile(t)
                    load_tile(Num(t.v + 2, j))
            for t in range(X_TILES - 2, X_TILES):
                if t == X_TILES - 2:
                    load_weights(2 * t + 2)
                    load_weights(2 * t + 3)
                store_tile(t)

            for b in range(2):
                sp.wait_ge(scattered[b], 16 * TOPK * TTOK // 2)
            sp.dma_start(idx[:], rows_d.rearrange("(p c) a -> p (c a)", p=P)).then_inc(idx_in, 16)

            def store_routed(i):
                t = i + X_TILES if isinstance(i, int) else Num(i.v + X_TILES, i.par)
                b = parity(i)
                sp.wait_ge(y_out, unit_of_routed(val(i)) + 1)
                dst = ys_d[bass.ds(val(i) * XT, XT), :].rearrange("(k p) d -> p k d", p=P)
                sp.dma_start(dst, yo[b]).then_inc(y_stored[b], 16)

            with sp.Fori(0, R_TILES // 2) as k:
                for j in range(2):
                    store_routed(Num(2 * k + j, j))
            for b in range(2):
                sp.wait_ge(y_stored[b], 16 * (X_TILES + R_TILES) // 2)

            def load_acc(t, b):
                sp.dma_start(acc[b], acc_d[bass.ds(t * P, P), :]).then_inc(acc_in[b], 16)

            for b in range(4):
                load_acc(b, b)
            with sp.Fori(0, TTOK // 4 - 1) as k:
                for b in range(4):
                    sp.wait_ge(combined, 2 * (4 * k + b) + 2)
                    sp.dma_start(out[bass.ds((4 * k + b) * P, P), :], acc[b]).then_inc(out_done[b], 16)
                    sp.wait_ge(out_done[b], 16 * (k + 1))
                    load_acc(4 * k + b + 4, b)
            for b in range(4):
                t = TTOK - 4 + b
                sp.wait_ge(combined, 2 * t + 2)
                sp.dma_start(out[t * P:(t + 1) * P, :], acc[b]).then_inc(out_done[b], 16)
            for b in range(4):
                sp.wait_ge(out_done[b], 16 * TTOK // 4)

        @block.gpsimd
        def _(pool):
            pool.memset(ones, 1.0).then_inc(consts_made, 1)
            pool.memset(half_neg, -0.5).then_inc(consts_made, 1)
            for b in range(BATCH):
                pool.memset(pre[b], 0.0).then_inc(consts_made, 1)
                pool.memset(Sd[b], 0.0).then_inc(consts_made, 1)
            pool.wait_ge(consts_made, 6)
            pool.wait_ge(const_in, 16 * 9)

            def front(b, it):
                n = 2 * it + b
                pool.wait_ge(var_eps, n + 1)
                pool.tensor_tensor(rstd, rstd, half_neg[:, 0:GT], ALU.pow).then_inc(rstd_ready, 1)
                yield
                yield
                yield
                yield
                pool.wait_ge(*fr.empty(n, "tok11"))
                pool.tensor_tensor(sq, raw[:, 0:2], raw[:, 0:2], ALU.mult).then_inc(squares, 1)
                pool.wait_ge(sumsq, n + 1)
                ss = ssq.rearrange("p a k h -> p (a k h)")
                pool.tensor_tensor(ss, ss, half_neg[:, 0:2 * GT * NH], ALU.pow).then_inc(rnorm, 1)
                yield
                yield
                pool.wait_ge(*fr.empty(n, "AT"))
                if has(n, 2):
                    pool.wait_ge(*bk.full(n - 2, f"Y{LEVELS - 1}"))
                for s in range(LEVELS):
                    dst = XTr[b] if s == 0 else CT[b][:, s - 1]
                    m = masks[:, s].unsqueeze(1).to_broadcast([P, GT, P])
                    if s == 0:
                        if has(n, 2):
                            pool.wait_ge(*bk.full(n - 2, "UT1"))
                    pool.tensor_tensor(dst, AT, m, ALU.mult).then_inc(masked, 1)
                yield

            def back(b, it):
                n = 2 * it + b
                for _ in range(LEVELS + 1):
                    yield
                pool.wait_ge(*bk.empty(n, "otok1"))
                pool.tensor_tensor(osq, ob, ob, ALU.mult).then_inc(o_sq, 1)
                pool.wait_ge(o_sum, 2 * n + 2)
                pool.tensor_tensor(oss.rearrange("p k h -> p (k h)"), oss.rearrange("p k h -> p (k h)"),
                                   half_neg[:, 0:GT * NH], ALU.pow).then_inc(o_rms, 1)
                yield
                pool.wait_ge(stats2, 3 * n + 3)
                pool.tensor_tensor(rstd2, rstd2, half_neg[:, 0:GT], ALU.pow).then_inc(rstd2_ready, 1)
                pool.wait_ge(x2n_ready, GT * n + GT)
                pool.tensor_tensor(xt[b], xt[b], x2n, ALU.add).then_inc(base_ready, 1)
                settled(pool, w_in, 16 * (n + 1))
                wsplit = wstage[:, 0, :]
                pool.tensor_scalar(wsplit, wsplit, W_SCALE, None, ALU.mult).then_inc(w_scaled, 1)
                pool.wait_ge(w_scaled, 2 * n + 1)
                hi = W[:, bass.ds(n, 1), 0, :]
                lo = W[:, bass.ds(n, 1), 1, :]
                f32 = wsplit.rearrange("p (a n) -> p a n", a=1)
                pool.tensor_copy(hi, f32).then_inc(w_scaled, 1)
                pool.wait_ge(w_scaled, 2 * n + 2)
                pool.tensor_tensor(lo, f32, hi, ALU.subtract).then_inc(w_split, 1)
                yield

            run_stages(pool, front, back)

            pool.memset(idx[:], 0).then_inc(rows_zeroed, 1)
            pool.wait_ge(rows_zeroed, 1)
            pool.dma_start(rows_d.rearrange("(p c) a -> p (c a)", p=P), idx[:]).then_inc(rows_out, 16)
            pool.wait_ge(rows_out, 16)
            pool.wait_ge(routed, 1)
            pool.wait_ge(route_in, 96)

            def scatter(t, b, first):
                if not first:
                    pool.wait_ge(scattered[b], 16 * TOPK * t.half)
                for c in range(TOPK):
                    pool.tensor_copy(scat[:, b, c:c + 1], adr[:, c, bass.ds(t.v, 1)]).then_inc(scat_copied, 1)
                pool.tensor_copy(scat[:, b, TOPK:], tid[:, bass.ds(t.v, 1)]).then_inc(scat_copied, 1)
                settled(pool, scat_copied, 3 * t.v + 3)
                for c in range(TOPK):
                    pool.indirect_dma_start(
                        out=rows_d, out_offset=bass.IndirectOffsetOnAxis(ap=scat[:, b, c:c + 1], axis=0),
                        in_=scat[:, b, TOPK:], in_offset=None).then_inc(scattered[b], 16)

            for b in range(2):
                scatter(Num(b, b, 0), b, True)
            with pool.Fori(1, TTOK // 2) as k:
                for b in range(2):
                    scatter(Num(2 * k + b, b, k), b, False)

            def gather(i, b, h):
                pool.wait_ge(x_turned, i + X_TILES - 1)
                if has(h, 1):
                    pool.wait_ge(x_gathered[b], 16 * XB * h)
                pool.tensor_copy(gath[:, b, :], idx[:, bass.ds(i * XB, XB)]).then_inc(gath_copied, 1)
                settled(pool, gath_copied, i + 1)
                for c in range(XB):
                    pool.indirect_dma_start(
                        out=xg[b][:, c], out_offset=None, in_=x2n_d,
                        in_offset=bass.IndirectOffsetOnAxis(ap=gath[:, b, c:c + 1], axis=0)).then_inc(x_gathered[b], 16)

            pool.wait_ge(idx_in, 16)
            for b in range(2):
                gather(b, b, 0)
            with pool.Fori(1, R_TILES // 2) as k:
                for b in range(2):
                    gather(2 * k + b, b, k)

            for b in range(2):
                pool.wait_ge(y_stored[b], 16 * (X_TILES + R_TILES) // 2)

            def fetch(t, b, first):
                if not first:
                    pool.wait_ge(combined, 2 * t - 6)
                pool.tensor_copy(lastidx[:, b, :], pos_i[:, :, bass.ds(t, 1)].rearrange("p a b -> p (a b)")).then_inc(gath_copied, 1)
                settled(pool, gath_copied, R_TILES + t + 1)
                for c in range(TOPK):
                    pool.indirect_dma_start(
                        out=yrow[b][:, c], out_offset=None, in_=ys_d,
                        in_offset=bass.IndirectOffsetOnAxis(ap=lastidx[:, b, c:c + 1], axis=0)).then_inc(y_in[b], 16)

            for b in range(4):
                fetch(b, b, True)
            with pool.Fori(1, TTOK // 4) as k:
                for b in range(4):
                    fetch(4 * k + b, b, False)

        @block.scalar
        def _(act):
            act.wait_ge(consts_made, 6)
            act.wait_ge(const_in, 16 * 9)

            def front(b, it):
                n = 2 * it + b
                yield
                if has(n, 1):
                    act.wait_ge(masked, LEVELS * n)
                for d in range(DB):
                    act.wait_ge(*fr.full(n, f"xnT{d}"))
                    act.copy(xnT[:, d], fr.bank(f"xnT{d}")).then_inc(fr.empty(n, f"xnT{d}")[0], 1)
                act.wait_ge(beta_mm, n + 1)
                if has(n, 1):
                    act.wait_ge(beta_ready, n)
                act.activation(th.rearrange("p k h -> p (k h)"), beta_ps, ACT.Tanh, scale=0.5).then_inc(beta_tanh, 1)
                act.wait_ge(history, n + 1)
                for m in range(3 * DB):
                    act.wait_ge(*fr.full(n, f"proj{m}"))
                    act.copy(pre[b][:, m, TAPS - 1:], fr.bank(f"proj{m}")).then_inc(pre_ready, 1)
                    act.activation(qkvT[:, m], fr.bank(f"proj{m}"), ACT.Copy,
                                   scale=cw[:, m, TAPS - 1:TAPS]).then_inc(fr.empty(n, f"proj{m}")[0], 1)
                yield
                for m in range(3 * DB):
                    act.wait_ge(conv_step, n * 3 * DB * (TAPS - 1) + conv_order(m, TAPS - 2))
                    act.activation(qkvT[:, m], qkvT[:, m], ACT.Silu).then_inc(silu_done, 1)
                yield
                if has(n, 1):
                    act.wait_ge(*fr.full(n - 1, "QT1"))
                for c in range(2):
                    for h in range(2):
                        name = f"tok{c}{h}"
                        act.wait_ge(*fr.full(n, name))
                        act.copy(raw[:, c, 2 * h:2 * h + 2].rearrange("p k d -> p (k d)"),
                                 fr.bank(name)).then_inc(fr.empty(n, name)[0], 1)
                yield
                yield
                act.wait_ge(sumsq, n + 1)
                if has(n, 2):
                    act.wait_ge(qk_ready, n - 1)
                for c, dst in (("K", KT[b]), ("Kb", KbT)):
                    for d in range(DB):
                        name = f"{c}T{d}"
                        act.wait_ge(*fr.full(n, name))
                        act.copy(dst[:, d], fr.bank(name)).then_inc(fr.empty(n, name)[0], 1)
                yield
                act.wait_ge(*fr.full(n, "AT"))
                act.copy(AT.rearrange("p k t -> p (k t)"), fr.bank("AT")).then_inc(fr.empty(n, "AT")[0], 1)
                yield

            def back(b, it):
                n = 2 * it + b
                for s in range(1, LEVELS):
                    act.wait_ge(*bk.full(n, f"Y{s}"))
                    act.copy(Y.rearrange("p k t -> p (k t)"), bk.bank(f"Y{s}")).then_inc(bk.empty(n, f"Y{s}")[0], 1)
                    yield
                yield
                yield
                if has(n, 1):
                    act.wait_ge(*bk.full(n - 1, "x2nT1"))
                    act.wait_ge(base_ready, n)
                    act.wait_ge(tokens_out[1 - b], 32 * (it + b))
                for h in range(2):
                    act.wait_ge(*bk.full(n, f"otok{h}"))
                    act.copy(ob[:, 2 * h:2 * h + 2].rearrange("p k d -> p (k d)"),
                             bk.bank(f"otok{h}")).then_inc(bk.empty(n, f"otok{h}")[0], 1)
                yield
                for d in range(DB):
                    act.wait_ge(*bk.full(n, f"oT{d}"))
                    act.copy(oT[:, d], bk.bank(f"oT{d}")).then_inc(bk.empty(n, f"oT{d}")[0], 1)
                yield
                for d in range(DB):
                    act.wait_ge(*bk.full(n, f"x2nT{d}"))
                    act.copy(x2nT[:, d], bk.bank(f"x2nT{d}")).then_inc(bk.empty(n, f"x2nT{d}")[0], 1)
                yield

            run_stages(act, front, back)
            act.drain().then_inc(act_idle, 1)

            act.wait_ge(kept, 1)
            act.activation(scr["sc"], logits[:], ACT.Sigmoid).then_inc(scored, 1)
            act.wait_ge(route, 1)
            act.activation(scr["bl"], scr["z"], ACT.Sigmoid).then_inc(scored, 1)
            act.wait_ge(picked, 1)
            for c in range(TOPK):
                act.activation(wtop[:, c], scr["dd"], ACT.Sigmoid, scale=1.0 - 2.0 * c).then_inc(tops_ready, 1)

            def x_high_half(t):
                b = parity(t)
                act.wait_ge(x_turned, val(t) + 1)
                if has(t, 2):
                    act.wait_ge(up_done, 4 * units_through(val(t) - 2, is_routed(t)))
                act.activation(xs[b][:, 0].rearrange("p d t -> p (d t)"), ps[:, 6, :], ACT.Copy,
                               scale=X_SCALE).then_inc(x_high, 1)

            def unit(u):
                b = parity(u)
                n = val(u)

                def gelu(c):
                    act.wait_ge(up_done, 4 * n + c + 1)
                    act.activation(ps[:, c, :], ps[:, c, :], ACT.Gelu,
                                   scale=1.0 / (X_SCALE * W_SCALE)).then_inc(gelu_done, 1)

                def high(c):
                    act.wait_ge(gelu_done, 4 * n + c + 1)
                    act.activation(hs[b][:, 0, 2 * c:2 * c + 2].rearrange("p f t -> p (f t)"), ps[:, c, :],
                                   ACT.Copy, scale=H_SCALE).then_inc(h_high, 1)

                gelu(0)
                if has(u, 2):
                    act.wait_ge(down_done, n - 1)
                for c in range(1, 4):
                    gelu(c)
                    high(c - 1)
                high(3)

            def weights_high(u):
                b = parity(u)
                act.wait_ge(rw_in[b], 16 * (half(u) + 1))
                act.activation(piece(val(u) + SH_PIECES, 0), wstage[:, b:b + 1, :], ACT.Copy,
                               scale=W_SCALE).then_inc(rw_high, 1)

            expert_stages(act, turn=x_high_half, unit=unit, weights=weights_high)

        @block.tensor
        def _(pe):
            pe.wait_ge(consts_made, 6)
            pe.wait_ge(const_in, 16 * 9)

            def fill(ring, n, name):
                if has(n, 1) or ring.at[name] >= len(ring.banks):
                    pe.wait_ge(*ring.free(n, name))
                return ring.bank(name)

            def front(b, it):
                n = 2 * it + b
                yield
                pe.wait_ge(xn_ready, GT * (n + 1))
                for d in range(DB):
                    to = fill(fr, n, f"xnT{d}")
                    for k in range(GT):
                        last = pe.transpose(to[:, k * P:(k + 1) * P], xn[:, k, d * P:(d + 1) * P], idt[:])
                    last.then_inc(fr.sem_full, 1)
                for d in range(DB):
                    pe.wait_ge(*fr.empty(n, f"xnT{d}"))
                if has(n, 1):
                    pe.wait_ge(beta_tanh, n)
                for k in range(GT):
                    for d in range(DB):
                        last = pe.matmul(beta_ps[:, k * NH:(k + 1) * NH], xnT[:, d, k * P:(k + 1) * P], wb[:, d],
                                         start=(d == 0), stop=(d == DB - 1))
                last.then_inc(beta_mm, 1)
                for m in range(3 * DB):
                    to = fill(fr, n, f"proj{m}")
                    for d in range(DB):
                        last = pe.matmul(to, wqkv[:, d, m * P:(m + 1) * P], xnT[:, d],
                                         start=(d == 0), stop=(d == DB - 1))
                    last.then_inc(fr.sem_full, 1)
                yield
                yield
                for c in range(3):
                    pe.wait_ge(silu_done, n * 3 * DB + DB * c + DB)
                    for h in range(2):
                        to = fill(fr, n, f"tok{c}{h}")
                        for k in range(2):
                            for d in range(DB):
                                last = pe.transpose(to[:, k * D + d * P:k * D + (d + 1) * P],
                                                    qkvT[:, DB * c + d, (2 * h + k) * P:(2 * h + k + 1) * P], idt[:])
                        last.then_inc(fr.sem_full, 1)
                yield
                yield
                for i, (c, src) in enumerate((("K", raw[:, 1]), ("Kb", Kb[b]), ("Q", raw[:, 0]))):
                    pe.wait_ge(normed, 4 * n + i + 1)
                    for d in range(DB):
                        to = fill(fr, n, f"{c}T{d}")
                        for k in range(GT):
                            last = pe.transpose(to[:, k * P:(k + 1) * P], src[:, k, d * P:(d + 1) * P], idt[:])
                        last.then_inc(fr.sem_full, 1)
                yield
                pe.wait_ge(*fr.empty(n, "KbT1"))
                to = fill(fr, n, "AT")
                for k in range(GT):
                    for d in range(DB):
                        last = pe.matmul(to[:, k * P:(k + 1) * P], KT[b][:, d, k * P:(k + 1) * P],
                                         KbT[:, d, k * P:(k + 1) * P], start=(d == 0), stop=(d == DB - 1))
                last.then_inc(fr.sem_full, 1)
                pe.wait_ge(x0t_ready, n + 1)
                to = fill(fr, n, "X")
                for k in range(GT):
                    last = pe.transpose(to[:, k * P:(k + 1) * P], XTr[b][:, k], idt[:])
                last.then_inc(fr.sem_full, 1)
                yield

            def back(b, it):
                n = 2 * it + b
                pe.wait_ge(masked, LEVELS * (n + 1))
                pe.wait_ge(*fr.empty(n, "X"))
                for s in range(1, LEVELS):
                    if s > 1:
                        pe.wait_ge(*bk.empty(n, f"Z{s - 1}"))
                        pe.wait_ge(*bk.empty(n, f"ZT{s - 1}"))
                    to = fill(bk, n, f"Y{s}")
                    for k in range(GT):
                        last = pe.matmul(to[:, k * P:(k + 1) * P], CT[b][:, s - 1, k], X[b][:, k], start=True, stop=True)
                    last.then_inc(bk.sem_full, 1)
                    pe.wait_ge(*bk.empty(n, f"Y{s}"))
                    if s < LEVELS - 1:
                        to = fill(bk, n, f"Z{s}")
                        for k in range(GT):
                            last = pe.matmul(to[:, k * P:(k + 1) * P], XTr[b][:, k], Y[:, k], start=True, stop=True)
                        last.then_inc(bk.sem_full, 1)
                    to = fill(bk, n, f"ZT{s}")
                    for k in range(GT):
                        last = pe.matmul(to[:, k * P:(k + 1) * P], Y[:, k], XTr[b][:, k], start=True, stop=True)
                    last.then_inc(bk.sem_full, 1)
                    yield
                pe.wait_ge(tt_ready, n + 1)
                for w, src in (("W", Kb[b]), ("U", Vb[b])):
                    for d in range(DB):
                        to = fill(bk, n, f"{w}T{d}")
                        for k in range(GT):
                            last = pe.matmul(to[:, k * P:(k + 1) * P], src[:, k, d * P:(d + 1) * P], XTr[b][:, k],
                                             start=True, stop=True)
                        last.then_inc(bk.sem_full, 1)
                yield
                pe.wait_ge(qk_ready, n + 1)
                for d in range(DB):
                    last = pe.matmul(corr_ps[:, 0:GCH * (b + 1)], ones, qk[:, d, :, 0:b + 1].rearrange("p a b -> p (a b)") if b + 1 == BATCH else qk[:, d, :, 0],
                                     start=(d == 0), stop=(d == DB - 1))
                last.then_inc(corr_mm, 1)
                yield
                pe.wait_ge(o_ready, n + 1)
                for h in range(2):
                    to = fill(bk, n, f"otok{h}")
                    for k in range(2):
                        for d in range(DB):
                            last = pe.transpose(to[:, k * D + d * P:k * D + (d + 1) * P],
                                                oT[:, d, (2 * h + k) * P:(2 * h + k + 1) * P], idt[:])
                    last.then_inc(bk.sem_full, 1)
                yield
                pe.wait_ge(o_normed, n + 1)
                for d in range(DB):
                    to = fill(bk, n, f"oT{d}")
                    for k in range(GT):
                        last = pe.transpose(to[:, k * P:(k + 1) * P], ob[:, k, d * P:(d + 1) * P], idt[:])
                    last.then_inc(bk.sem_full, 1)
                for d in range(DB):
                    pe.wait_ge(*bk.empty(n, f"oT{d}"))
                pe.wait_ge(wo_scaled, DB)
                for h in range(2):
                    to = fill(bk, n, f"attn{h}")
                    for k in range(2):
                        for d in range(DB):
                            last = pe.matmul(to[:, k * D:(k + 1) * D], oT[:, d, (2 * h + k) * P:(2 * h + k + 1) * P],
                                             wo[:, d], start=(d == 0), stop=(d == DB - 1))
                    last.then_inc(bk.sem_full, 1)
                yield
                pe.wait_ge(x2n_ready, GT * (n + 1))
                for d in range(DB):
                    to = fill(bk, n, f"x2nT{d}")
                    for k in range(GT):
                        last = pe.transpose(to[:, k * P:(k + 1) * P], x2n[:, k, d * P:(d + 1) * P], idt[:])
                    last.then_inc(bk.sem_full, 1)
                for d in range(DB):
                    pe.wait_ge(*bk.empty(n, f"x2nT{d}"))
                if has(n, 1):
                    pe.wait_ge(logits_kept, n)
                for k in range(GT):
                    for d in range(DB):
                        last = pe.matmul(logit_ps[:, k * N_RT:(k + 1) * N_RT], x2nT[:, d, k * P:(k + 1) * P], cen[:, d],
                                         start=(d == 0), stop=(d == DB - 1))
                last.then_inc(logit_mm, 1)
                yield

            run_stages(pe, front, back)
            pe.drain().then_inc(pe_idle, 1)

            pe.wait_ge(mask_ready, 1)
            pe.wait_ge(route_in, 96)
            maskf = scr["mask"].rearrange("p t e -> p (t e)")
            pe.matmul(ps[:, 7, 0:TTOK * N_RT], scr["rc"][:, 0], maskf, start=True, stop=True)
            pe.matmul(ps[:, 7, TTOK * N_RT:2 * TTOK * N_RT], scr["rc"][:, 1], maskf,
                      start=True, stop=True).then_inc(ranked, 1)

            def turn(t):
                b = parity(t)
                pe.wait_ge(*x_there(t))
                if has(t, 1):
                    pe.wait_ge(x_low, val(t))
                for d in range(DB):
                    for c in range(XB):
                        last = pe.transpose(ps[:, 6, d * XT + c * P:d * XT + (c + 1) * P],
                                            xg[b][:, c, d * P:(d + 1) * P], idt[:])
                last.then_inc(x_turned, 1)

            def up(u, t, slot):
                n, b = val(u), parity(t)
                pe.wait_ge(x_low, val(t) + 1)
                for c in range(4):
                    if has(u, 1):
                        pe.wait_ge(h_low, 4 * n - 3 + c)
                    for f in range(2):
                        cols = slice((2 * c + f) * P, (2 * c + f + 1) * P)
                        parts = [(d, hw, hx) for d in range(DB) for hw, hx in ((0, 0), (0, 1), (1, 0))]
                        for q, (d, hw, hx) in enumerate(parts):
                            last = pe.matmul(ps[:, c, f * XT:(f + 1) * XT], weight(slot, d, hw, cols), xs[b][:, hx, d],
                                             start=(q == 0), stop=(q == len(parts) - 1))
                    last.then_inc(up_done, 1)

            def down(u, slot):
                n, b = val(u), parity(u)
                pe.wait_ge(h_low, 4 * n + 4)
                if has(u, 2):
                    pe.wait_ge(y_out, n - 1)
                for c in range(XB):
                    parts = [(f, hh, hw) for f in range(FB) for hh, hw in ((0, 0), (0, 1), (1, 0))]
                    for q, (f, hh, hw) in enumerate(parts):
                        cols = slice(f % 4 * D, (f % 4 + 1) * D)
                        last = pe.matmul(ps[:, 4 + b, c * D:(c + 1) * D], hs[b][:, hh, f, c * P:(c + 1) * P],
                                         weight(slot, DB + f // 4, hw, cols), start=(q == 0), stop=(q == len(parts) - 1))
                last.then_inc(down_done, 1)

            turn(0)
            pe.wait_ge(w_split, SH_PIECES)
            up(0, 0, 0)

            def shared_tile(t, last=False):
                n, par = val(t), parity(t)
                if not last:
                    turn(Num(n + 1, 1 - par, half=half(t) + parity(t)))
                up(Num(2 * n + 1, 1), Num(n, par), 1)
                down(Num(2 * n, 0), 0)
                if not last:
                    up(Num(2 * n + 2, 0), Num(n + 1, 1 - par), 0)
                down(Num(2 * n + 1, 1), 1)

            shared_tile(0)
            shared_tile(1)
            with pe.Fori(1, X_TILES // 2 - 1) as k:
                for j in range(2):
                    shared_tile(Num(2 * k + j, j, k))
            shared_tile(X_TILES - 2)
            shared_tile(X_TILES - 1, last=True)

            pe.wait_ge(routed, 2)
            pe.wait_ge(rw_low, N_RT * PIECES)

            def expert_of(i):
                return pe.value_load(eid[0:1, bass.ds(i, 1)], min_val=N_SH * PIECES, max_val=(SLOTS - 1) * PIECES)

            def routed_up(i, par, h):
                turn(Num(i + X_TILES, par, h, routed=True))
                up(Num(unit_of_routed(i), par), Num(i + X_TILES, par), expert_of(i))

            routed_up(0, 0, 0)
            with pe.Fori(0, R_TILES // 2 - 1) as k:
                for j in range(2):
                    i = 2 * k + j
                    routed_up(i + 1, 1 - j, k + j)
                    down(Num(unit_of_routed(i), j), expert_of(i))
            i = R_TILES - 2
            routed_up(i + 1, 1, R_TILES // 2 - 1)
            down(Num(unit_of_routed(i), 0), expert_of(i))
            down(Num(unit_of_routed(i + 1), 1), expert_of(i + 1))

        @block.vector
        def _(dve):
            dve.wait_ge(consts_made, 6)
            dve.wait_ge(const_in, 16 * 9)
            for d in range(DB):
                dve.tensor_scalar(wo[:, d], wo[:, d], gcol[:, d:d + 1], None, ALU.mult).then_inc(wo_scaled, 1)

            def layer_norm(n, src, dst, b6, m2, rs, s_stats, s_rstd, s_out):
                for k in range(GT):
                    last = dve.bn_stats(b6[:, k], src[:, k])
                last.then_inc(s_stats, 1)
                settled(dve, s_stats, 3 * n + 1)
                for k in range(GT):
                    last = dve.bn_aggr(m2[:, k], b6[:, k])
                last.then_inc(s_stats, 1)
                dve.wait_ge(s_stats, 3 * n + 2)
                dve.tensor_scalar(rs, m2[:, :, 1], EPS, None, ALU.add).then_inc(s_stats, 1)

            def front(b, it):
                n = 2 * it + b
                dve.tensor_copy(pre[b][:, :, 0:TAPS - 1], pre[b][:, :, GRP:GRP + TAPS - 1]).then_inc(history, 1)
                dve.wait_ge(x_in[b], 16 * (it + 1))
                for k in range(GT):
                    last = dve.bn_stats(bn[:, k], xt[b][:, k])
                last.then_inc(stats, 1)
                settled(dve, stats, n + 1)
                for k in range(GT):
                    last = dve.bn_aggr(mv[:, k], bn[:, k])
                last.then_inc(moments, 1)
                dve.wait_ge(moments, n + 1)
                dve.tensor_scalar(rstd, mv[:, :, 1], EPS, None, ALU.add).then_inc(var_eps, 1)
                dve.wait_ge(rstd_ready, n + 1)
                if has(n, 1):
                    dve.wait_ge(*fr.full(n - 1, "AT"))
                for k in range(GT):
                    dve.tensor_scalar(xn[:, k], xt[b][:, k], mv[:, k, 0:1], rstd[:, k:k + 1],
                                      ALU.subtract, ALU.mult).then_inc(xn_ready, 1)
                yield
                yield
                base = n * 3 * DB * (TAPS - 1)
                for pair in range(3):
                    for t in range(TAPS - 1):
                        for m in (DB * pair, DB * pair + 1):
                            if t == 0:
                                dve.wait_ge(*fr.empty(n, f"proj{m}"))
                            else:
                                dve.wait_ge(conv_step, base + conv_order(m, t - 1))
                            dve.scalar_tensor_tensor(qkvT[:, m], pre[b][:, m, t:t + GRP], cw[:, m, t:t + 1],
                                                     qkvT[:, m], ALU.mult, ALU.add).then_inc(conv_step, 1)
                yield
                dve.wait_ge(beta_tanh, n + 1)
                dve.tensor_scalar(beta, th, 0.5, 0.5, ALU.mult, ALU.add).then_inc(beta_ready, 1)
                for h in range(2):
                    name = f"tok2{h}"
                    dve.wait_ge(*fr.full(n, name))
                    dve.tensor_copy(raw[:, 2, 2 * h:2 * h + 2].rearrange("p k d -> p (k d)"),
                                    fr.bank(name)).then_inc(fr.empty(n, name)[0], 1)
                yield
                bt = beta.rearrange("p k h -> p (k h)").unsqueeze(2).to_broadcast([P, GT * NH, HD])

                def heads(a):
                    return a.rearrange("p k (h e) -> p (k h) e", h=NH)

                dve.wait_ge(beta_ready, n + 1)
                dve.wait_ge(*fr.empty(n, "tok21"))
                if has(n, 2):
                    dve.wait_ge(*bk.full(n - 2, "UT1"))
                dve.tensor_tensor(heads(Vb[b]), heads(raw[:, 2]), bt, ALU.mult).then_inc(normed_v, 1)
                dve.wait_ge(squares, n + 1)
                dve.tensor_reduce(ssq.rearrange("p a k h -> p (a k h)"),
                                  sq.rearrange("p a k (h e) -> p (a k h) e", h=NH), AX_X, ALU.add).then_inc(sumsq, 1)
                dve.wait_ge(rnorm, n + 1)

                def rn(c):
                    return ssq[:, c].rearrange("p k h -> p (k h)").unsqueeze(2).to_broadcast([P, GT * NH, HD])

                dve.tensor_tensor(heads(raw[:, 1]), heads(raw[:, 1]), rn(1), ALU.mult).then_inc(normed, 1)
                dve.wait_ge(normed, 4 * n + 1)
                dve.tensor_tensor(heads(Kb[b]), heads(raw[:, 1]), bt, ALU.mult).then_inc(normed, 1)
                dve.tensor_tensor(heads(raw[:, 0]), heads(raw[:, 0]), rn(0), ALU.mult).then_inc(normed, 2)
                yield
                for d in range(DB):
                    name = f"QT{d}"
                    dve.wait_ge(*fr.full(n, name))
                    dve.tensor_copy(QT[b][:, d], fr.bank(name)).then_inc(fr.empty(n, name)[0], 1)
                yield
                dve.wait_ge(masked, LEVELS * n + 1)
                dve.tensor_tensor(XTr[b], XTr[b], idt[:].unsqueeze(1).to_broadcast([P, GT, P]), ALU.add).then_inc(x0t_ready, 1)
                dve.wait_ge(*fr.full(n, "X"))
                dve.tensor_copy(X[b].rearrange("p k t -> p (k t)"), fr.bank("X")).then_inc(fr.empty(n, "X")[0], 1)
                yield

            def back(b, it):
                n = 2 * it + b
                flat = lambda a: a.rearrange("p k t -> p (k t)")
                for s in range(1, LEVELS):
                    if s < LEVELS - 1:
                        dve.wait_ge(*bk.full(n, f"Z{s}"))
                        dve.tensor_tensor(flat(X[b]), flat(X[b]), bk.bank(f"Z{s}"), ALU.add).then_inc(bk.empty(n, f"Z{s}")[0], 1)
                    dve.wait_ge(*bk.full(n, f"ZT{s}"))
                    dve.tensor_tensor(flat(XTr[b]), flat(XTr[b]), bk.bank(f"ZT{s}"), ALU.add).then_inc(bk.empty(n, f"ZT{s}")[0], 1)
                    if s == LEVELS - 1:
                        dve.wait_ge(*bk.empty(n, f"ZT{s}"))
                        dve.scalar_tensor_tensor(XTr[b], XTr[b], 3.0, minus2i.unsqueeze(1).to_broadcast([P, GT, P]),
                                                 ALU.mult, ALU.add).then_inc(tt_ready, 1)
                    yield
                edge_k, edge_q = (m[b].rearrange("p d (c t) -> p d c t", t=CH)[:, :, :, 0:b + 1] for m in (KT, QT))
                if has(n, 1):
                    dve.wait_ge(corr_mm, n)
                dve.tensor_tensor(qk[:, :, :, 0:b + 1], edge_q, edge_k, ALU.mult).then_inc(qk_ready, 1)
                for i, w in enumerate(("W", "U")):
                    for d in range(DB):
                        name = f"{w}T{d}"
                        dve.wait_ge(*bk.full(n, name))
                        dve.tensor_tensor(prod[:, DB * i + d], bk.bank(name), KT[b][:, d], ALU.mult).then_inc(edge_cols, 1)
                        dve.tensor_copy(Wc[:, i, d, :, 0:b + 1],
                                        bk.bank(name).rearrange("p (c t) -> p c t", t=CH)[:, :, 0:b + 1]).then_inc(bk.empty(n, name)[0], 1)
                dve.wait_ge(edge_cols, 4 * n + 4)
                dve.tensor_reduce(PR.rearrange("p a d c -> p (a d c)"),
                                  prod.rearrange("p a (c t) -> p (a c) t", t=CH), AX_X, ALU.add).then_inc(chunk_sums, 1)
                yield
                dve.tensor_copy(Sd[b][:, :, 0:1], Sd[b][:, :, GCH:GCH + 1]).then_inc(carry, 1)
                dve.wait_ge(chunk_sums, n + 1)
                dve.tensor_scalar(PR[:, 0], PR[:, 0], -1.0, 1.0, ALU.mult, ALU.add).then_inc(one_minus, 1)
                dve.wait_ge(one_minus, n + 1)
                dve.wait_ge(carry, n + 1)
                for d in range(DB):
                    dve.tensor_tensor_scan(Sd[b][:, d, 1:GCH + 1], PR[:, 0, d], PR[:, 1, d], Sd[b][:, d, 0:1],
                                           ALU.mult, ALU.add).then_inc(scanned, 1)
                dve.wait_ge(scanned, DB * (n + 1))
                if has(n, 1):
                    dve.wait_ge(logit_mm, n)
                before = Sd[b][:, :, 0:GCH].unsqueeze(3)
                oc = oT.rearrange("p d (c t) -> p d c t", t=CH)
                dve.tensor_tensor(oc, QT[b].rearrange("p d (c t) -> p d c t", t=CH),
                                  before.to_broadcast([P, DB, GCH, CH]), ALU.mult).then_inc(edge_u, 1)
                e = b + 1
                dve.wait_ge(*bk.empty(n, "UT1"))
                dve.tensor_tensor(wu[:, :, :, 0:e], Wc[:, 0, :, :, 0:e], before.to_broadcast([P, DB, GCH, e]),
                                  ALU.mult).then_inc(edge_u, 1)
                dve.wait_ge(edge_u, 4 * n + 2)
                dve.tensor_tensor(wu[:, :, :, 0:e], Wc[:, 1, :, :, 0:e], wu[:, :, :, 0:e], ALU.subtract).then_inc(edge_u, 1)
                dve.wait_ge(edge_u, 4 * n + 3)
                dve.wait_ge(corr_mm, n + 1)
                a = corr_ps[:, 0:GCH * e].rearrange("p (c t) -> p c t", t=e).unsqueeze(1).to_broadcast([P, DB, GCH, e])
                dve.tensor_tensor(wu[:, :, :, 0:e], wu[:, :, :, 0:e], a, ALU.mult).then_inc(edge_u, 1)
                dve.wait_ge(edge_u, 4 * n + 4)
                dve.tensor_tensor(oc[:, :, :, 0:e], oc[:, :, :, 0:e], wu[:, :, :, 0:e], ALU.add).then_inc(o_ready, 1)
                yield
                dve.wait_ge(o_sq, n + 1)
                oss_f = oss.rearrange("p k h -> p (k h)")
                dve.tensor_reduce(oss_f, osq.rearrange("p k (h e) -> p (k h) e", h=NH), AX_X, ALU.add).then_inc(o_sum, 1)
                dve.wait_ge(o_sum, 2 * n + 1)
                dve.tensor_scalar(oss_f, oss_f, 1.0 / HD, EPS, ALU.mult, ALU.add).then_inc(o_sum, 1)
                dve.wait_ge(o_rms, n + 1)
                ov = ob.rearrange("p k (h e) -> p (k h) e", h=NH)
                dve.tensor_tensor(ov, ov, oss_f.unsqueeze(2).to_broadcast([P, GT * NH, HD]), ALU.mult).then_inc(o_normed, 1)
                yield
                for h in range(2):
                    name = f"attn{h}"
                    dve.wait_ge(*bk.full(n, name))
                    part = xt[b][:, 2 * h:2 * h + 2].rearrange("p k d -> p (k d)")
                    dve.tensor_tensor(part, part, bk.bank(name), ALU.add).then_inc(bk.empty(n, name)[0], 1)
                dve.wait_ge(*bk.empty(n, "attn1"))
                layer_norm(n, xt[b], x2n, bn2, mv2, rstd2, stats2, rstd2_ready, x2n_ready)
                dve.wait_ge(rstd2_ready, n + 1)
                dve.wait_ge(*bk.full(n, "oT1"))
                for k in range(GT):
                    dve.tensor_scalar(x2n[:, k], xt[b][:, k], mv2[:, k, 0:1], rstd2[:, k:k + 1],
                                      ALU.subtract, ALU.mult).then_inc(x2n_ready, 1)
                yield
                dve.wait_ge(logit_mm, n + 1)
                dve.tensor_copy(logits[:, bass.ds(b * (TTOK // BATCH) + GT * it, GT), :],
                                logit_ps.rearrange("p (k e) -> p k e", e=N_RT)).then_inc(logits_kept, 1)
                yield

            run_stages(dve, front, back)
            dve.wait_ge(logits_kept, GROUPS)
            dve.drain().then_inc(kept, 1)
            dve.wait_ge(route_in, 96)
            r = scr
            step = [0]

            def then(ins, s=route):
                step[0] += 1
                ins.then_inc(route, 1)
                dve.wait_ge(route, step[0])

            def over_tiles(a):
                return a.unsqueeze(1).to_broadcast([P, TTOK, a.shape[-1]])

            def over_experts(a):
                return a.unsqueeze(2).to_broadcast([P, a.shape[-1], N_RT])

            then(dve.tensor_tensor(r["z"], logits[:], over_tiles(r["biasc"]), ALU.add))
            then(dve.memset(r["onec"], 1.0))
            dve.wait_ge(scored, 2)

            def pick(hot):
                then(dve.tensor_reduce(r["m"], r["bl"], AX_X, ALU.max))
                then(dve.tensor_tensor(r["tmp"], r["bl"], over_experts(r["m"]), ALU.is_equal))
                then(dve.tensor_tensor(r["tmp"], r["tmp"], over_tiles(r["prefc"]), ALU.mult))
                then(dve.tensor_reduce(r["mx"], r["tmp"], AX_X, ALU.max))
                then(dve.tensor_tensor(hot, r["tmp"], over_experts(r["mx"]), ALU.is_equal))

            pick(r["oh1"])
            then(dve.scalar_tensor_tensor(r["bl"], r["oh1"], -2.0, r["bl"], ALU.mult, ALU.add))
            pick(r["oh2"])
            then(dve.tensor_tensor(r["mask"], r["oh1"], r["oh2"], ALU.add))
            dve.nop().then_inc(mask_ready, 1)
            for c, hot in enumerate(("oh1", "oh2")):
                then(dve.tensor_tensor(r["tmp"], r[hot], r["sc"], ALU.mult))
                then(dve.tensor_reduce(r["s12"][:, c], r["tmp"], AX_X, ALU.add))
            then(dve.tensor_tensor(r["dd"], r["s12"][:, 0], r["s12"][:, 1], ALU.subtract))
            dve.nop().then_inc(picked, 1)
            dve.wait_ge(ranked, 1)
            rank = ps[:, 7, 0:TTOK * N_RT].rearrange("p (t e) -> p t e", e=N_RT)
            count = ps[:, 7, TTOK * N_RT:2 * TTOK * N_RT].rearrange("p (t e) -> p t e", e=N_RT)
            for e in range(N_RT):
                then(dve.tensor_tensor_scan(r["inc"][:, :, e], r["onec"], count[:, :, e], 0.0, ALU.mult, ALU.add))
            whole = r["inc"][:, TTOK - 1, :].unsqueeze(2).to_broadcast([P, N_RT, X_TILES])
            steps = r["kc"].unsqueeze(1).to_broadcast([P, N_RT, X_TILES])
            then(dve.tensor_tensor(r["cmp"], whole, steps, ALU.is_gt))
            then(dve.tensor_reduce(r["nb"], r["cmp"], AX_X, ALU.add))
            then(dve.tensor_tensor_scan(r["tb"], r["onec"][:, 0:N_RT], r["nb"], 0.0, ALU.mult, ALU.add))
            then(dve.tensor_tensor(r["start"], r["tb"], r["nb"], ALU.subtract))
            then(dve.tensor_scalar(r["start"], r["start"], float(XT), None, ALU.mult))
            then(dve.tensor_tensor(r["pos"], r["inc"], count, ALU.subtract))
            then(dve.tensor_tensor(r["pos"], r["pos"], rank, ALU.add))
            then(dve.tensor_tensor(r["pos"], r["pos"], over_tiles(r["start"]), ALU.add))
            for c, hot in enumerate(("oh1", "oh2")):
                then(dve.tensor_tensor(r["tmp"], r[hot], r["pos"], ALU.mult))
                then(dve.tensor_reduce(r["p12"][:, c], r["tmp"], AX_X, ALU.add))
            then(dve.tensor_copy(pos_i[:], r["p12"]))
            then(dve.tensor_scalar(lane[:], pos_i[:], P - 1, None, ALU.bitwise_and))
            then(dve.tensor_scalar(adr[:], pos_i[:], 7, None, ALU.logical_shift_right))
            dve.scalar_tensor_tensor(adr[:], lane[:], float(IDX_COLS), adr[:], ALU.mult, ALU.add).then_inc(routed, 1)
            tiles = r["tc"].unsqueeze(2).to_broadcast([P, R_TILES, N_RT])
            ends = r["tb"].unsqueeze(1).to_broadcast([P, R_TILES, N_RT])
            then(dve.tensor_tensor(r["cmpt"], ends, tiles, ALU.is_le))
            then(dve.tensor_reduce(r["es"], r["cmpt"], AX_X, ALU.add))
            then(dve.tensor_scalar(r["es"], r["es"], float(N_RT - 1), None, ALU.min))
            dve.tensor_scalar(eid[:], r["es"], float(PIECES), float(SH_PIECES), ALU.mult, ALU.add).then_inc(routed, 1)

            def x_low_half(t):
                b = parity(t)
                dve.wait_ge(x_high, val(t) + 1)
                dve.scalar_tensor_tensor(xs[b][:, 1].rearrange("p d t -> p (d t)"), ps[:, 6, :], X_SCALE,
                                         xs[b][:, 0].rearrange("p d t -> p (d t)"), ALU.mult, ALU.subtract).then_inc(x_low, 1)

            def unit(u):
                n, b = val(u), parity(u)
                for c in range(4):
                    dve.wait_ge(h_high, 4 * n + c + 1)
                    hi, lo = (hs[b][:, q, 2 * c:2 * c + 2].rearrange("p f t -> p (f t)") for q in range(2))
                    dve.scalar_tensor_tensor(lo, ps[:, c, :], H_SCALE, hi, ALU.mult, ALU.subtract).then_inc(h_low, 1)

            def weights_low(u):
                n = val(u)
                dve.wait_ge(rw_high, n + 1)
                dve.scalar_tensor_tensor(piece(n + SH_PIECES, 1), wstage[:, parity(u):parity(u) + 1, :], W_SCALE,
                                         piece(n + SH_PIECES, 0), ALU.mult, ALU.subtract).then_inc(rw_low, 1)

            def y_shared(u, t):
                n, b, e = val(u), parity(t), parity(u)
                dve.wait_ge(down_done, n + 1)
                if e == 0:
                    dve.wait_ge(base_in[b], 16 * (half(t) + 1))
                    if has(t, 2):
                        dve.wait_ge(y_stored[b], 16 * half(t))
                else:
                    dve.wait_ge(y_out, n)
                flat = lambda a: a.rearrange("p k d -> p (k d)")
                dve.scalar_tensor_tensor(flat(yo[b]), ps[:, 4 + e, :], 1.0 / (H_SCALE * W_SCALE),
                                         flat(bt[b] if e == 0 else yo[b]), ALU.mult, ALU.add).then_inc(y_out, 1)

            def y_routed(u, i):
                n, b = val(u), parity(u)
                dve.wait_ge(down_done, n + 1)
                dve.wait_ge(y_stored[b], 16 * (X_TILES // 2 + half(i)))
                dve.tensor_scalar(yo[b].rearrange("p k d -> p (k d)"), ps[:, 4 + b, :],
                                  1.0 / (H_SCALE * W_SCALE), None, ALU.mult).then_inc(y_out, 1)

            expert_stages(dve, turn=x_low_half, unit=unit, weights=weights_low, y_shared=y_shared, y_routed=y_routed)

            dve.wait_ge(tops_ready, TOPK)

            def combine(t, b, k):
                dve.wait_ge(acc_in[b], 16 * (k + 1))
                dve.wait_ge(y_in[b], 32 * (k + 1))
                for c in range(TOPK):
                    if c:
                        dve.wait_ge(combined, 2 * t + c)
                    dve.scalar_tensor_tensor(acc[b], yrow[b][:, c], wtop[:, c, bass.ds(t, 1)], acc[b],
                                             ALU.mult, ALU.add).then_inc(combined, 1)

            with dve.Fori(0, TTOK // 4) as k:
                for b in range(4):
                    combine(4 * k + b, b, k)


def conv_order(m, t):
    pair, odd = divmod(m, DB)
    return pair * DB * (TAPS - 1) + t * DB + odd + 1


def run_stages(eng, front, back):
    for _ in front(0, 0):
        pass
    weave(front(1, 0), back(0, 0))
    with eng.Fori(0, ROUNDS - 1) as it:
        weave(front(0, it + 1), back(1, it))
        weave(front(1, it + 1), back(0, it + 1))
    for _ in back(1, ROUNDS - 1):
        pass


def constants():
    i = np.arange(P)
    same = (i[:, None] // CH) == (i[None, :] // CH)
    masks = np.zeros((P, LEVELS, P), np.float32)
    for s in range(LEVELS):
        w = 1 << s
        joined = same & (i[:, None] // (2 * w) == i[None, :] // (2 * w))
        joined &= ((i[:, None] // w) % 2 == 0) & ((i[None, :] // w) % 2 == 1)
        masks[:, s][joined] = -1.0
    eye = np.eye(P, dtype=np.float32)
    before = np.stack([(i[:, None] < i[None, :]), np.ones((P, P))], axis=1).astype(np.float32)

    def row(a):
        return np.ascontiguousarray(np.broadcast_to(np.asarray(a, np.float32), (P, len(a))))

    return {
        "ident": eye, "lvl_masks": masks, "eye2": -2.0 * eye, "block_tri": before,
        "row_iota": row(XT * np.arange(X_TILES)), "tile_iota": row(np.arange(R_TILES)),
        "pref": row(N_RT - np.arange(N_RT)),
        "tok_id": (P * np.arange(TTOK)[None, :] + i[:, None]).astype(np.int32),
    }


def laid_out(i):
    def split(w):
        return np.ascontiguousarray(np.asarray(w).reshape(-1, P, w.shape[-1]).transpose(1, 0, 2))

    conv = np.concatenate([i[f"L0_attn_conv_{c}"].reshape(D, TAPS) for c in "qkv"])
    up = np.concatenate([i["L0_ffn_Wfc_sh"], i["L0_ffn_Wfc_r"]]).transpose(0, 2, 1)
    down = np.concatenate([i["L0_ffn_Wproj_sh"], i["L0_ffn_Wproj_r"]]).transpose(0, 2, 1)
    up = up.reshape(SLOTS, DB, P, PIECE)
    down = down.reshape(SLOTS, FB, P, D).transpose(0, 2, 1, 3).reshape(SLOTS, P, PIECES // 2, PIECE).transpose(0, 2, 1, 3)
    return {
        "x": i["L0_attn_x"].reshape(TOK, D),
        "w_qkv": split(np.concatenate([i[f"L0_attn_W{c}"] for c in "qkv"], axis=1)),
        "w_beta": split(i["L0_attn_Wb"]),
        "conv_w": split(conv),
        "g_col": split(np.tile(i["L0_attn_g"], NH)[:, None])[:, :, 0],
        "w_o": split(i["L0_attn_Wo"]),
        "cent": split(i["L0_ffn_centroids"].T),
        "bias": np.ascontiguousarray(np.broadcast_to(i["L0_ffn_routing_bias"], (P, N_RT))),
        "w_ffn": np.concatenate([up, down], axis=1).reshape(SLOTS * PIECES, P, PIECE),
    }


_ORDER = ["x", "w_qkv", "w_beta", "conv_w", "g_col", "w_o", "cent", "bias", "w_ffn",
          "ident", "lvl_masks", "eye2", "block_tri", "row_iota", "tile_iota", "pref", "tok_id"]


def kernel(**inputs):
    import concourse.bacc as bacc
    from concourse.bass_utils import run_bass_kernel_spmd

    arrays = {**laid_out({k: np.asarray(v) for k, v in inputs.items()}), **constants()}
    nc = bacc.Bacc("TRN2", target_bir_lowering=False, num_devices=1)
    args = [nc.dram_tensor(f"in_{n}", arrays[n].shape, mybir.dt.from_np(arrays[n].dtype), kind="ExternalInput").ap()
            for n in _ORDER]
    out = nc.dram_tensor("out", (TOK, D), F32, kind="ExternalOutput").ap()
    build(nc, *args, out)
    feed = {f"in_{n}": np.ascontiguousarray(arrays[n]) for n in _ORDER}
    r = run_bass_kernel_spmd(nc, [feed], core_ids=[0])
    return r.results[0]["out"].reshape(BATCH, SEQ, D)
```

```python
from contextlib import ExitStack

import numpy as np

import concourse.bass as bass
from concourse import mybir

ALU = mybir.AluOpType
ACT = mybir.ActivationFunctionType
F32 = mybir.dt.float32
F16 = mybir.dt.float16
I32 = mybir.dt.int32
AX_X = mybir.AxisListType.X

P = 128
BATCH, SEQ, D = 2, 2048, 256
TOK = BATCH * SEQ
NH, HD = 4, 64
CH = 64
TAPS = 4
EPS = 1e-5
DB = D // P

GRP = 512
GT = GRP // P
GROUPS = TOK // GRP
ROUNDS = GROUPS // BATCH
GCH = GRP // CH
LEVELS = 6

FF = 1024
FB = FF // P
N_SH, N_RT, TOPK = 2, 8, 2
SLOTS = N_SH + N_RT
PIECE = 1024
PIECES = 2 * DB * FF // PIECE
CONSTS_MADE = 2 + 2 * BATCH
CONSTS_IN = 16 * 10
XT = 256
XB = XT // P
X_TILES = TOK // XT
R_TILES = TOK * TOPK // XT + N_RT - 1
TTOK = TOK // P
IDX_COLS = R_TILES * XB
PEELED = 4
X_SCALE = 256.0
W_SCALE = 256.0
H_SCALE = 64.0


class Ring:

    def __init__(self, banks, fills, sem_full, sem_empty):
        self.banks, self.fills = banks, fills
        self.at = {name: i for i, (name, _) in enumerate(fills)}
        self.sem_full, self.sem_empty = sem_full, sem_empty
        self.count = {e: sum(o == e for _, o in fills) for e in sem_empty}
        self.rank = [sum(o == e for _, o in fills[:i]) for i, (_, e) in enumerate(fills)]

    def bank(self, name):
        return self.banks[self.at[name] % len(self.banks)]

    def full(self, n, name):
        return self.sem_full, n * len(self.fills) + self.at[name] + 1

    def empty(self, n, name):
        i = self.at[name]
        e = self.fills[i][1]
        return self.sem_empty[e], n * self.count[e] + self.rank[i] + 1

    def free(self, n, name):
        i = self.at[name]
        if i >= len(self.banks):
            return self.empty(n, self.fills[i - len(self.banks)][0])
        last = [k for k in range(len(self.fills)) if k % len(self.banks) == i % len(self.banks)][-1]
        e = self.fills[last][1]
        return self.sem_empty[e], n * self.count[e]


FRONT_FILLS = (
    [(f"proj{m}", "act") for m in range(3 * DB)]
    + [(f"tok{c}{h}", "dve") for c in "KQV" for h in range(2)]
    + [(f"{c}T{d}", "act") for c in ("K", "Kb", "Q") for d in range(DB)]
    + [("AT", "act"), ("X", "dve")]
)
BACK_FILLS = (
    [(f"{w}{s}", "act" if w == "Y" else "dve")
     for s in range(1, LEVELS) for w in ("Y", "Z", "ZT") if (w, s) != ("Z", LEVELS - 1)]
    + [(f"{w}T{d}", "dve") for w in ("W", "U") for d in range(DB)]
    + [(f"otok{h}", "dve") for h in range(2)]
    + [(f"oT{d}", "act") for d in range(DB)]
    + [(f"attn{h}", "dve") for h in range(2)]
    + [(f"x2nT{d}", "act") for d in range(DB)]
)
AHEAD_FILLS = [(f"xnT{d}", "act") for d in range(DB)] + [("beta", "act")]
SLOTS_A = 20
W_SLOT = 11


class Num:

    def __init__(self, v, par, half=None, routed=False):
        self.v, self.par, self.half, self.routed = v, par, half, routed


def val(n):
    return n.v if isinstance(n, Num) else n


def parity(n):
    return n.par if isinstance(n, Num) else n % 2


def half(n):
    return n.half if isinstance(n, Num) else n // 2


def is_routed(n):
    return isinstance(n, Num) and n.routed


def unit_of_routed(i):
    return i + N_SH * X_TILES


def routed_on(b):
    return (R_TILES + 1 - b) // 2


def units_through(t, routed):
    return t - X_TILES + N_SH * X_TILES + 1 if routed else N_SH * (t + 1)


def shared_order(turn, up, down, between=None):
    def tile(t, last=False):
        n, par, h = val(t), parity(t), half(t)
        after = Num(n + 1, 1 - par, h + par)
        if not last:
            turn(after)
        up(Num(2 * n + 1, 1, n), t)
        down(Num(2 * n, 0, n), t)
        if isinstance(t, int) and between:
            between(2 * t)
        if not last:
            up(Num(2 * n + 2, 0, n + 1), after)
        down(Num(2 * n + 1, 1, n), t)
        if isinstance(t, int) and between:
            between(2 * t + 1)

    def run(eng):
        turn(0)
        up(0, 0)
        for t in range(PEELED):
            tile(t)
        with eng.Fori(PEELED // 2, X_TILES // 2 - 1) as k:
            for j in range(2):
                tile(Num(2 * k + j, j, k))
        tile(X_TILES - 2)
        tile(X_TILES - 1, last=True)

    return run


def routed_order(eng, turn, up, down):
    def routed(t):
        return Num(t.v + X_TILES, t.par, t.half, routed=True)

    def step(i, j, h, left):
        if left >= 1:
            up(Num(i + 1, 1 - j, h + j))
        if left >= 2:
            turn(routed(Num(i + 2, j, h + 1)))
        down(Num(i, j, h))

    turn(routed(Num(0, 0, 0)))
    up(Num(0, 0, 0))
    turn(routed(Num(1, 1, 0)))
    pairs = (R_TILES - 2) // 2
    with eng.Fori(0, pairs) as k:
        for j in range(2):
            step(2 * k + j, j, k, 2)
    for i in range(2 * pairs, R_TILES):
        step(i, i % 2, i // 2, R_TILES - 1 - i)


def has(n, k):
    n = val(n)
    return not isinstance(n, int) or n >= k


def build(nc, x, w_qkv, w_beta, conv_w, g_col, w_o, cent, bias, w_ffn,
          ident, lvl_masks, eye2, head_sel, block_tri, row_iota, tile_iota, pref, tok_id, out):
    ctx = ExitStack()
    with ctx:
        def sb(name, shape, dt=F32):
            return ctx.enter_context(nc.sbuf_tensor(name, shape, dt))

        def sem(name):
            return ctx.enter_context(nc.semaphore(name))

        base_d = nc.dram_tensor("base_d", (TOK, D), F32).ap()
        x2n_d = nc.dram_tensor("x2n_d", (TOK, D), F32).ap()
        acc_d = nc.dram_tensor("acc_d", (TOK, D), F32).ap()
        ys_d = nc.dram_tensor("ys_d", (R_TILES * XT, D), F32).ap()
        rows_d = nc.dram_tensor("rows_d", (P * IDX_COLS, 1), I32).ap()

        W = sb("W", [P, SLOTS * PIECES, 2, PIECE], F16)
        arena = W[:, N_SH * PIECES:, :, :].rearrange("p a b c -> p (a b c)").bitcast(F32)
        late_room = sb("late_room", [P, 8192])
        rooms = [[arena, 0, N_RT * PIECES * PIECE], [late_room[:], 0, 8192]]

        def early(*shape):
            n = int(np.prod(shape))
            room = next(r for r in rooms if r[1] + n <= r[2])
            a = room[0][:, room[1]:room[1] + n]
            room[1] += n
            if len(shape) == 1:
                return a
            names = "abcd"[:len(shape)]
            return a.rearrange(f"p ({' '.join(names)}) -> p {' '.join(names)}",
                               **{k: s for k, s in zip(names[1:], shape[1:])})

        idt = sb("idt", [P, P])
        wstage = sb("wstage", [P, 2, PIECE])
        logits = sb("logits", [P, TTOK, N_RT])

        def carve(room, start, shape, dt=F32):
            n = int(np.prod(shape)) // (2 if dt == F16 else 1)
            a = room[:, start:start + n]
            a = a.bitcast(dt) if dt != F32 else a
            if len(shape) > 1:
                names = "abcd"[:len(shape)]
                a = a.rearrange(f"p ({' '.join(names)}) -> p {' '.join(names)}",
                                **{k: z for k, z in zip(names[1:], shape[1:])})
            return a, start + n

        late = 0
        xg, bt, yo, xs, hs = [], [], [], [], []
        for tiles, shape, dt in ((xg, (XB, D), F32), (bt, (XB, D), F32), (yo, (XB, D), F32),
                                 (xs, (2, DB, XT), F16), (hs, (2, FB, XT), F16)):
            for _ in range(2):
                tile, late = carve(late_room[:], late, shape, dt)
                tiles.append(tile)
        assert late <= 8192

        at = (N_RT - 1) * PIECES * PIECE
        scr = {}
        for name, shape in (("rc", (2, P)), ("prefc", (N_RT,)), ("biasc", (N_RT,)), ("kc", (X_TILES,)),
                            ("tc", (R_TILES,)), ("onec", (TTOK,)), ("z", (TTOK, N_RT)), ("sc", (TTOK, N_RT)),
                            ("bl", (TTOK, N_RT)), ("oh1", (TTOK, N_RT)), ("oh2", (TTOK, N_RT)),
                            ("mask", (TTOK, N_RT)), ("tmp", (TTOK, N_RT)), ("inc", (TTOK, N_RT)),
                            ("pos", (TTOK, N_RT)), ("m", (TTOK,)), ("mx", (TTOK,)), ("s12", (2, TTOK)),
                            ("p12", (2, TTOK)), ("cmp", (N_RT, X_TILES)), ("nb", (N_RT,)), ("tb", (N_RT,)),
                            ("start", (N_RT,)), ("cmpt", (R_TILES, N_RT)), ("es", (R_TILES,))):
            scr[name], at = carve(arena, at, shape)
        assert at <= N_RT * PIECES * PIECE
        score_diff = sb("score_diff", [P, TTOK])
        eid = sb("eid", [P, R_TILES], I32)
        pos_i = sb("pos_i", [P, 2, TTOK], I32)
        lane = sb("lane", [P, 2, TTOK], I32)
        adr = sb("adr", [P, 2, TTOK], I32)
        tid = sb("tid", [P, TTOK], I32)
        wtop = sb("wtop", [P, 2, TTOK])
        idx = sb("idx", [P, IDX_COLS], I32)
        scat = sb("scat", [P, 2, 3], I32)
        gath = sb("gath", [P, 2, XB], I32)

        at = 0
        acc, yrow = [], []
        for _ in range(4):
            tile, at = carve(arena, at, (D,))
            acc.append(tile)
            tile, at = carve(arena, at, (TOPK, D))
            yrow.append(tile)
        lastidx = sb("lastidx", [P, 4, TOPK], I32)

        wqkv = early(DB, 3 * D)
        wo = early(DB, D)
        wb = early(DB, NH)
        cen = early(DB, N_RT)
        cw = early(3 * DB, TAPS)
        gcol = early(DB)
        masks = early(LEVELS, P)
        minus2i = early(P)
        headsel = early(P // HD)
        ones = early(P)
        minus_half = early(16)
        xl = early(GT, D)
        xr = early(GT, D)
        xnT = early(DB, GRP)
        pre = early(3 * DB, GRP + TAPS - 1)
        hist = [early(3 * DB, TAPS - 1) for _ in range(BATCH)]
        qkvT = early(3 * DB, GRP)
        sqT = early(2 * DB, GRP)
        osqT = early(DB, GRP)
        xn = early(GT, D)
        Qt = early(GT, D)
        Kt = early(GT, D)
        Kb = early(GT, D)
        Vb = early(GT, D)
        KT = early(DB, GRP)
        KbT = early(DB, GRP)
        QT = early(DB, GRP)
        AT = early(GT, P)
        CT = early(LEVELS - 1, GT, P)
        X = early(GT, P)
        XTr = early(GT, P)
        Y = early(GT, P)
        prod = early(2 * DB, GRP)
        Wc = early(2, DB, GCH, BATCH)
        PR = early(2, DB, GCH)
        Sd = [early(DB, GCH + 1) for _ in range(BATCH)]
        qk = early(DB, GCH, BATCH)
        wu = early(DB, GCH, BATCH)
        oT = early(DB, GRP)
        ob = early(GT, D)
        x2n = ob
        x2nT = oT
        bn = early(GT, 6)
        mv = early(GT, 2)
        rstd = early(GT)
        nmr = early(GT)
        bn2 = early(GT, 6)
        mv2 = early(GT, 2)
        rstd2 = early(GT)
        nmr2 = early(GT)
        ssq = early(2, GT * NH)
        th = early(GT * NH)
        beta = [early(GT * NH) for _ in range(BATCH)]
        oss = early(GT * NH)

        ps = ctx.enter_context(nc.psum_tensor("ps", [P, 8, 512], F32))
        small = ps[:, 7, :]
        corr_ps = small[:, 32:32 + GCH * BATCH]
        logit_ps = small[:, 64:64 + GT * N_RT]
        ssq_ps = small[:, 128:128 + 2 * GT * NH].rearrange("p (a t) -> p a t", a=2)
        oss_ps = small[:, 192:192 + GT * NH]

        const_in = sem("const_in")
        consts_made = sem("consts_made")
        wo_scaled = sem("wo_scaled")
        xl_in = [sem(f"xl_in{b}") for b in range(BATCH)]
        xr_in = [sem(f"xr_in{b}") for b in range(BATCH)]
        stats = sem("stats")
        rstd_ready = sem("rstd_ready")
        nmr_ready = sem("nmr_ready")
        xn_ready = sem("xn_ready")
        hist_saved = sem("hist_saved")
        hist_set = sem("hist_set")
        beta_ready = sem("beta_ready")
        pre_ready = sem("pre_ready")
        conv_step = sem("conv_step")
        silu_done = sem("silu_done")
        squares = sem("squares")
        sumsq = sem("sumsq")
        sumsq_kept = sem("sumsq_kept")
        rnorm = sem("rnorm")
        kb_ready = sem("kb_ready")
        masked = sem("masked")
        x0t_ready = sem("x0t_ready")
        tt_ready = sem("tt_ready")
        products = sem("products")
        chunk_sums = sem("chunk_sums")
        carry = sem("carry")
        one_minus = sem("one_minus")
        scanned = sem("scanned")
        qk_ready = sem("qk_ready")
        corr_mm = sem("corr_mm")
        edge_u = sem("edge_u")
        o_ready = sem("o_ready")
        o_sq = sem("o_sq")
        o_sum = sem("o_sum")
        o_mean = sem("o_mean")
        o_rms = sem("o_rms")
        stats2 = sem("stats2")
        rstd2_ready = sem("rstd2_ready")
        nmr2_ready = sem("nmr2_ready")
        x2n_ready = sem("x2n_ready")
        base_ready = sem("base_ready")
        logit_mm = sem("logit_mm")
        logits_kept = sem("logits_kept")
        tokens_out = [sem(f"tokens_out{b}") for b in range(BATCH)]
        w_in = sem("w_in")
        w_scaled = sem("w_scaled")
        w_split = sem("w_split")
        route_in = sem("route_in")
        x_loaded = [sem(f"x_loaded{b}") for b in range(2)]
        base_in = [sem(f"base_in{b}") for b in range(2)]
        x_turned = sem("x_turned")
        x_high = sem("x_high")
        x_low = sem("x_low")
        up_done = sem("up_done")
        gelu_done = sem("gelu_done")
        h_high = sem("h_high")
        h_low = sem("h_low")
        down_done = sem("down_done")
        y_out = sem("y_out")
        y_stored = [sem(f"y_stored{b}") for b in range(2)]
        rw_in = [sem(f"rw_in{b}") for b in range(2)]
        rw_high = sem("rw_high")
        rw_low = sem("rw_low")
        scored = sem("scored")
        route = sem("route")
        mask_ready = sem("mask_ready")
        ranked = sem("ranked")
        picked = sem("picked")
        tops_ready = sem("tops_ready")
        routed = sem("routed")
        rows_zeroed = sem("rows_zeroed")
        rows_out = sem("rows_out")
        x_gathered = [sem(f"x_gathered{b}") for b in range(2)]
        scat_copied = sem("scat_copied")
        scattered = [sem(f"scattered{b}") for b in range(2)]
        idx_in = sem("idx_in")
        gath_copied = sem("gath_copied")
        acc_in = [sem(f"acc_in{b}") for b in range(4)]
        y_in = [sem(f"y_in{b}") for b in range(4)]
        combined = sem("combined")
        out_done = [sem(f"out_done{b}") for b in range(4)]

        fr = Ring([ps[:, b, :] for b in range(3)], FRONT_FILLS, sem("front_full"),
                  {"act": sem("front_act"), "dve": sem("front_dve")})
        bk = Ring([ps[:, b, :] for b in range(3, 6)], BACK_FILLS, sem("back_full"),
                  {"act": sem("back_act"), "dve": sem("back_dve")})
        ah = Ring([ps[:, 6, :]], AHEAD_FILLS, sem("ahead_full"), {"act": sem("ahead_act")})
        SH_PIECES = N_SH * PIECES
        assert SH_PIECES == GROUPS

        def tokens(ap, b, it):
            return ap[bass.ds(b * SEQ + it * GRP, GRP), :].rearrange("(k p) d -> p k d", p=P)

        passed = sem("passed")
        kept, pe_idle, act_idle = sem("kept"), sem("pe_idle"), sem("act_idle")

        def rows_of(ap, t):
            return ap[bass.ds(val(t) * XT, XT), :].rearrange("(k p) d -> p k d", p=P)

        def piece(n, half):
            return W[:, n:n + 1, half, :] if isinstance(n, int) else W[:, bass.ds(n, 1), half, :]

        def weight(slot, k, half, cols):
            if isinstance(slot, int):
                return W[:, slot * PIECES + k, half, cols]
            return W[:, bass.ds(slot + k, 1), half, cols].rearrange("p a n -> p (a n)")

        def x_there(t):
            if is_routed(t):
                return x_gathered[parity(t)], 16 * XB * (half(t) + 1)
            return x_loaded[parity(t)], 16 * (half(t) + 1)

        def settled(eng, s, value):
            eng.wait_ge(s, value)
            eng.sem_inc(passed, 1)

        block = ctx.enter_context(nc.Block())

        @block.sync
        def _(sp):
            def load_ahead(b, it):
                n = 2 * it + b
                if has(n, 1):
                    sp.wait_ge(xn_ready, GT * n)
                sp.dma_start(xl, tokens(x, b, it)).then_inc(xl_in[b], 16)

            load_ahead(0, 0)
            for dst, src in ((idt[:], ident), (wqkv, w_qkv), (cw, conv_w), (wb, w_beta), (masks, lvl_masks),
                             (minus2i, eye2), (wo, w_o), (gcol, g_col), (cen, cent), (headsel, head_sel)):
                sp.dma_start(dst, src).then_inc(const_in, 16)
            load_ahead(1, 0)

            def tick(b, it, ahead=True):
                n = 2 * it + b
                if ahead:
                    load_ahead(b, it + 1)
                if has(n, 1):
                    sp.wait_ge(tokens_out[1 - b], 32 * (it + b))
                    sp.wait_ge(w_split, n)
                sp.dma_start(xr, tokens(x, b, it)).then_inc(xr_in[b], 16)
                sp.dma_start(wstage[:, 0, :], w_ffn[bass.ds(n, 1)].rearrange("a p n -> p (a n)")).then_inc(w_in, 16)
                sp.wait_ge(x2n_ready, GT * (n + 1))
                sp.dma_start(tokens(x2n_d, b, it), x2n).then_inc(tokens_out[b], 16)
                sp.wait_ge(base_ready, n + 1)
                sp.dma_start(tokens(base_d, b, it), xr).then_inc(tokens_out[b], 16)

            tick(0, 0)
            with sp.Fori(0, ROUNDS - 2) as it:
                tick(1, it)
                tick(0, it + 1)
            tick(1, ROUNDS - 2)
            for b in range(BATCH):
                tick(b, ROUNDS - 1, ahead=False)
            for b in range(BATCH):
                sp.wait_ge(tokens_out[b], 32 * ROUNDS)

            for e in (kept, pe_idle, act_idle):
                sp.wait_ge(e, 1)
            for dst, src in ((scr["rc"], block_tri), (scr["prefc"], pref), (scr["biasc"], bias),
                             (scr["kc"], row_iota), (scr["tc"], tile_iota), (tid[:], tok_id)):
                sp.dma_start(dst, src).then_inc(route_in, 16)

            def load_tile(t):
                b = parity(t)
                if has(t, 2):
                    sp.wait_ge(x_turned, val(t) - 1)
                sp.dma_start(xg[b], rows_of(x2n_d, t)).then_inc(x_loaded[b], 16)

            def load_base(t):
                b = parity(t)
                if has(t, 2):
                    sp.wait_ge(y_out, 2 * val(t) - 3)
                sp.dma_start(bt[b], rows_of(base_d, t)).then_inc(base_in[b], 16)

            def load_weights(u):
                b = parity(u)
                if has(u, 2):
                    sp.wait_ge(rw_low, val(u) - 1)
                src = w_ffn[bass.ds(val(u) + SH_PIECES, 1)].rearrange("a p n -> p (a n)")
                sp.dma_start(wstage[:, b, :], src).then_inc(rw_in[b], 16)

            def store_tile(t):
                b = parity(t)
                sp.wait_ge(y_out, 2 * val(t) + 2)
                sp.dma_start(rows_of(acc_d, t), yo[b]).then_inc(y_stored[b], 16)

            sp.wait_ge(w_split, SH_PIECES)
            for t in range(2):
                load_tile(t)
                load_base(t)
                load_weights(t)
            with sp.Fori(0, X_TILES // 2 - 1) as k:
                for j in range(2):
                    t = Num(2 * k + j, j)
                    load_tile(Num(t.v + 2, j))
                    load_weights(Num(2 * t.v + 2, 0))
                    load_weights(Num(2 * t.v + 3, 1))
                    load_base(Num(t.v + 2, j))
                    store_tile(t)
            for t in range(X_TILES - 2, X_TILES):
                if t == X_TILES - 2:
                    load_weights(2 * t + 2)
                    load_weights(2 * t + 3)
                store_tile(t)

            for b in range(2):
                sp.wait_ge(scattered[b], 16 * TOPK * TTOK // 2)
            sp.dma_start(idx[:], rows_d.rearrange("(p c) a -> p (c a)", p=P)).then_inc(idx_in, 16)

            def store_routed(i):
                b = parity(i)
                sp.wait_ge(y_out, unit_of_routed(val(i)) + 1)
                dst = ys_d[bass.ds(val(i) * XT, XT), :].rearrange("(k p) d -> p k d", p=P)
                sp.dma_start(dst, yo[b]).then_inc(y_stored[b], 16)

            with sp.Fori(0, R_TILES // 2) as k:
                for j in range(2):
                    store_routed(Num(2 * k + j, j))
            for i in range(R_TILES // 2 * 2, R_TILES):
                store_routed(i)
            for b in range(2):
                sp.wait_ge(y_stored[b], 16 * (X_TILES // 2 + routed_on(b)))

            def load_acc(t, b):
                sp.dma_start(acc[b], acc_d[bass.ds(t * P, P), :]).then_inc(acc_in[b], 16)

            for b in range(4):
                load_acc(b, b)
            with sp.Fori(0, TTOK // 4 - 1) as k:
                for b in range(4):
                    sp.wait_ge(combined, 2 * (4 * k + b) + 2)
                    sp.dma_start(out[bass.ds((4 * k + b) * P, P), :], acc[b]).then_inc(out_done[b], 16)
                    sp.wait_ge(out_done[b], 16 * (k + 1))
                    load_acc(4 * k + b + 4, b)
            for b in range(4):
                t = TTOK - 4 + b
                sp.wait_ge(combined, 2 * t + 2)
                sp.dma_start(out[t * P:(t + 1) * P, :], acc[b]).then_inc(out_done[b], 16)
            for b in range(4):
                sp.wait_ge(out_done[b], 16 * TTOK // 4)

        @block.gpsimd
        def _(pool):
            pool.memset(ones, 1.0).then_inc(consts_made, 1)
            pool.memset(minus_half, -0.5).then_inc(consts_made, 1)
            for b in range(BATCH):
                pool.memset(hist[b], 0.0).then_inc(consts_made, 1)
                pool.memset(Sd[b], 0.0).then_inc(consts_made, 1)
            pool.wait_ge(consts_made, CONSTS_MADE)
            pool.wait_ge(const_in, CONSTS_IN)

            def front(slot, b, it):
                n = 2 * it + b
                if slot == 11:
                    pool.wait_ge(sumsq_kept, n + 1)
                    for i in range(2):
                        pool.tensor_tensor(ssq[:, i], ssq[:, i], minus_half, ALU.pow).then_inc(rnorm, 1)
                if slot == 17:
                    pool.wait_ge(*fr.empty(n, "AT"))
                    if has(n, 1):
                        pool.wait_ge(*bk.full(n - 1, f"UT{DB - 1}"))
                    for s in range(LEVELS):
                        pool.tensor_tensor(XTr if s == 0 else CT[:, s - 1], AT,
                                           masks[:, s].unsqueeze(1).to_broadcast([P, GT, P]), ALU.mult).then_inc(masked, 1)

            def back(slot, b, it):
                n = 2 * it + b
                if slot == 0:
                    settled(pool, w_in, 16 * (n + 1))
                    wscaled = wstage[:, 0:1, :]
                    pool.tensor_scalar(wscaled, wscaled, W_SCALE, None, ALU.mult).then_inc(w_scaled, 1)
                    pool.wait_ge(w_scaled, 2 * n + 1)
                    pool.tensor_copy(piece(n, 0), wscaled).then_inc(w_scaled, 1)
                    pool.wait_ge(w_scaled, 2 * n + 2)
                    pool.tensor_tensor(piece(n, 1), wscaled, piece(n, 0), ALU.subtract).then_inc(w_split, 1)
                if slot == 14:
                    pool.wait_ge(o_mean, n + 1)
                    pool.tensor_tensor(oss, oss, minus_half, ALU.pow).then_inc(o_rms, 1)
                if slot == 18:
                    pool.wait_ge(stats2, 3 * n + 3)
                    pool.tensor_tensor(rstd2, rstd2, minus_half[:, 0:GT], ALU.pow).then_inc(rstd2_ready, 1)
                if slot == 19:
                    pool.wait_ge(x2n_ready, GT * n + GT)
                    pool.tensor_tensor(xr, xr, x2n, ALU.add).then_inc(base_ready, 1)

            def ahead(slot, b, it):
                n = 2 * it + b
                if slot == 16:
                    pool.wait_ge(stats, 3 * n + 3)
                    pool.tensor_tensor(rstd, rstd, minus_half[:, 0:GT], ALU.pow).then_inc(rstd_ready, 1)

            run_attention(pool, front, back, ahead)

            pool.memset(idx[:], 0).then_inc(rows_zeroed, 1)
            pool.wait_ge(rows_zeroed, 1)
            pool.dma_start(rows_d.rearrange("(p c) a -> p (c a)", p=P), idx[:]).then_inc(rows_out, 16)
            pool.wait_ge(rows_out, 16)
            pool.wait_ge(routed, 1)
            pool.wait_ge(route_in, 96)

            def scatter(t, b, first):
                if not first:
                    pool.wait_ge(scattered[b], 16 * TOPK * t.half)
                for c in range(TOPK):
                    pool.tensor_copy(scat[:, b, c:c + 1], adr[:, c, bass.ds(t.v, 1)]).then_inc(scat_copied, 1)
                pool.tensor_copy(scat[:, b, TOPK:], tid[:, bass.ds(t.v, 1)]).then_inc(scat_copied, 1)
                settled(pool, scat_copied, 3 * t.v + 3)
                for c in range(TOPK):
                    pool.indirect_dma_start(
                        out=rows_d, out_offset=bass.IndirectOffsetOnAxis(ap=scat[:, b, c:c + 1], axis=0),
                        in_=scat[:, b, TOPK:], in_offset=None).then_inc(scattered[b], 16)

            for b in range(2):
                scatter(Num(b, b, 0), b, True)
            with pool.Fori(1, TTOK // 2) as k:
                for b in range(2):
                    scatter(Num(2 * k + b, b, k), b, False)

            def gather(i, b, h):
                pool.wait_ge(x_turned, i + X_TILES - 1)
                if has(h, 1):
                    pool.wait_ge(x_gathered[b], 16 * XB * h)
                pool.tensor_copy(gath[:, b, :], idx[:, bass.ds(i * XB, XB)]).then_inc(gath_copied, 1)
                settled(pool, gath_copied, i + 1)
                for c in range(XB):
                    pool.indirect_dma_start(
                        out=xg[b][:, c], out_offset=None, in_=x2n_d,
                        in_offset=bass.IndirectOffsetOnAxis(ap=gath[:, b, c:c + 1], axis=0)).then_inc(x_gathered[b], 16)

            pool.wait_ge(idx_in, 16)
            for b in range(2):
                gather(b, b, 0)
            with pool.Fori(1, R_TILES // 2) as k:
                for b in range(2):
                    gather(2 * k + b, b, k)
            for i in range(R_TILES // 2 * 2, R_TILES):
                gather(i, i % 2, i // 2)

            for b in range(2):
                pool.wait_ge(y_stored[b], 16 * (X_TILES // 2 + routed_on(b)))

            def fetch(t, b, first):
                if not first:
                    pool.wait_ge(combined, 2 * t - 6)
                pool.tensor_copy(lastidx[:, b, :], pos_i[:, :, bass.ds(t, 1)].rearrange("p a b -> p (a b)")).then_inc(gath_copied, 1)
                settled(pool, gath_copied, R_TILES + t + 1)
                for c in range(TOPK):
                    pool.indirect_dma_start(
                        out=yrow[b][:, c], out_offset=None, in_=ys_d,
                        in_offset=bass.IndirectOffsetOnAxis(ap=lastidx[:, b, c:c + 1], axis=0)).then_inc(y_in[b], 16)

            for b in range(4):
                fetch(b, b, True)
            with pool.Fori(1, TTOK // 4) as k:
                for b in range(4):
                    fetch(4 * k + b, b, False)

        @block.scalar
        def _(act):
            act.wait_ge(consts_made, CONSTS_MADE)
            act.wait_ge(const_in, CONSTS_IN)

            def put(ring, n, name, dst):
                act.wait_ge(*ring.full(n, name))
                act.copy(dst, ring.bank(name)).then_inc(ring.empty(n, name)[0], 1)

            def front(slot, b, it):
                n = 2 * it + b

                def silu(m):
                    act.wait_ge(conv_step, 3 * DB * (TAPS - 1) * n + (TAPS - 1) * (m + 1))
                    act.activation(qkvT[:, m], qkvT[:, m], ACT.Silu).then_inc(silu_done, 1)
                    if m < 2 * DB:
                        act.wait_ge(silu_done, 3 * DB * n + m + 1)
                        act.activation(sqT[:, m], qkvT[:, m], ACT.Square).then_inc(squares, 1)

                def project(m):
                    if m == 0:
                        act.wait_ge(hist_saved, n + 1)
                        if has(n, 1):
                            act.wait_ge(*fr.full(n - 1, "tokV1"))
                    act.wait_ge(*fr.full(n, f"proj{m}"))
                    act.copy(pre[:, m, TAPS - 1:], fr.bank(f"proj{m}")).then_inc(pre_ready, 1)
                    act.activation(qkvT[:, m], fr.bank(f"proj{m}"), ACT.Copy,
                                   scale=cw[:, m, TAPS - 1:TAPS]).then_inc(fr.empty(n, f"proj{m}")[0], 1)

                if slot < 10:
                    m = slot // 2
                    if slot % 2:
                        project(m)
                    elif m >= 2:
                        silu(m - 2)
                if slot == 10:
                    silu(3)
                if slot == 11:
                    project(5)
                    silu(4)
                    act.wait_ge(sumsq, n + 1)
                    act.copy(ssq, ssq_ps).then_inc(sumsq_kept, 1)
                if slot == 13:
                    silu(5)
                if slot == 15:
                    for d in range(DB):
                        put(fr, n, f"KT{d}", KT[:, d])
                    for d in range(DB):
                        put(fr, n, f"KbT{d}", KbT[:, d])
                if slot == 16:
                    for d in range(DB):
                        put(fr, n, f"QT{d}", QT[:, d])
                if slot == 17:
                    put(fr, n, "AT", AT.rearrange("p k t -> p (k t)"))

            def back(slot, b, it):
                n = 2 * it + b
                if slot < 10 and slot % 2 == 0:
                    put(bk, n, f"Y{slot // 2 + 1}", Y.rearrange("p k t -> p (k t)"))
                if slot == 13:
                    act.wait_ge(o_ready, n + 1)
                    for d in range(DB):
                        act.activation(osqT[:, d], oT[:, d], ACT.Square).then_inc(o_sq, 1)
                if slot == 16:
                    for d in range(DB):
                        put(bk, n, f"oT{d}", oT[:, d])
                if slot == 18:
                    act.wait_ge(nmr2_ready, n + 1)
                    for k in range(GT):
                        act.activation(x2n[:, k], xr[:, k], ACT.Identity, bias=nmr2[:, k:k + 1],
                                       scale=rstd2[:, k:k + 1]).then_inc(x2n_ready, 1)
                if slot == 19:
                    for d in range(DB):
                        put(bk, n, f"x2nT{d}", x2nT[:, d])

            def ahead(slot, b, it):
                n = 2 * it + b
                if slot == 17:
                    act.wait_ge(nmr_ready, n + 1)
                    if has(n, 1):
                        act.wait_ge(*ah.full(n - 1, "xnT1"))
                    for k in range(GT):
                        act.activation(xn[:, k], xl[:, k], ACT.Identity, bias=nmr[:, k:k + 1],
                                       scale=rstd[:, k:k + 1]).then_inc(xn_ready, 1)
                if slot == 18:
                    for d in range(DB):
                        put(ah, n, f"xnT{d}", xnT[:, d])
                if slot == 19:
                    act.wait_ge(*ah.full(n, "beta"))
                    if has(n, 1):
                        act.wait_ge(beta_ready, n)
                    act.activation(th, ah.bank("beta")[:, 0:GT * NH], ACT.Tanh,
                                   scale=0.5).then_inc(ah.empty(n, "beta")[0], 1)

            run_attention(act, front, back, ahead)
            act.drain().then_inc(act_idle, 1)

            act.wait_ge(kept, 1)
            act.activation(scr["sc"], logits[:], ACT.Sigmoid).then_inc(scored, 1)
            act.wait_ge(route, 1)
            act.activation(scr["bl"], scr["z"], ACT.Sigmoid).then_inc(scored, 1)
            def x_high_half(t):
                b = parity(t)
                act.wait_ge(x_turned, val(t) + 1)
                if has(t, 2):
                    act.wait_ge(up_done, 4 * units_through(val(t) - 2, is_routed(t)))
                act.activation(xs[b][:, 0].rearrange("p d t -> p (d t)"), ps[:, 6, :], ACT.Copy,
                               scale=X_SCALE).then_inc(x_high, 1)

            def unit(n, b):
                def gelu(c):
                    act.wait_ge(up_done, 4 * n + c + 1)
                    act.activation(ps[:, c, :], ps[:, c, :], ACT.Gelu,
                                   scale=1.0 / (X_SCALE * W_SCALE)).then_inc(gelu_done, 1)

                def high(c):
                    act.wait_ge(gelu_done, 4 * n + c + 1)
                    act.activation(hs[b][:, 0, 2 * c:2 * c + 2].rearrange("p f t -> p (f t)"), ps[:, c, :],
                                   ACT.Copy, scale=H_SCALE).then_inc(h_high, 1)

                gelu(0)
                if has(n, 2):
                    act.wait_ge(down_done, n - 1)
                for c in range(1, 4):
                    gelu(c)
                    high(c - 1)
                high(3)

            def shared_unit(u, t):
                unit(val(u), parity(u))
                b = parity(u)
                act.wait_ge(rw_in[b], 16 * (half(u) + 1))
                act.activation(piece(val(u) + SH_PIECES, 0), wstage[:, b:b + 1, :], ACT.Copy,
                               scale=W_SCALE).then_inc(rw_high, 1)

            def nothing(*_):
                pass

            shared_order(x_high_half, shared_unit, nothing)(act)
            routed_order(act, x_high_half, lambda i: unit(unit_of_routed(i.v), i.par), nothing)

            act.wait_ge(picked, 1)
            for c in range(TOPK):
                act.activation(wtop[:, c], score_diff[:], ACT.Sigmoid, scale=1.0 - 2.0 * c).then_inc(tops_ready, 1)

        @block.tensor
        def _(pe):
            pe.wait_ge(consts_made, CONSTS_MADE)
            pe.wait_ge(const_in, CONSTS_IN)

            def fill(ring, n, name):
                if has(n, 1) or ring.at[name] >= len(ring.banks):
                    pe.wait_ge(*ring.free(n, name))
                return ring.bank(name)

            def by_tile(ring, n, name, product):
                to = fill(ring, n, name)
                for k in range(GT):
                    last = product(to[:, k * P:(k + 1) * P], k)
                last.then_inc(ring.sem_full, 1)

            def turn_back(ring, n, name, src, d):
                by_tile(ring, n, name, lambda to, k: pe.transpose(to, src[:, k, d * P:(d + 1) * P], idt[:]))

            def turn_out(ring, n, name, src, h):
                to = fill(ring, n, name)
                for k in range(2):
                    for d in range(DB):
                        last = pe.transpose(to[:, k * D + d * P:k * D + (d + 1) * P],
                                            src[:, d, (2 * h + k) * P:(2 * h + k + 1) * P], idt[:])
                last.then_inc(ring.sem_full, 1)

            def head_sums(dst, src):
                for k in range(GT):
                    for d in range(DB):
                        at = k * NH + d * (P // HD)
                        last = pe.matmul(dst[:, at:at + P // HD], src[:, d, k * P:(k + 1) * P], headsel,
                                         start=True, stop=True)
                return last

            def front(slot, b, it):
                n = 2 * it + b

                def project(m, d):
                    to = fill(fr, n, f"proj{m}") if d == 0 else fr.bank(f"proj{m}")
                    mm = pe.matmul(to, wqkv[:, d, m * P:(m + 1) * P], xnT[:, d], start=(d == 0), stop=(d == DB - 1))
                    if d == DB - 1:
                        mm.then_inc(fr.sem_full, 1)

                if slot == 0:
                    for d in range(DB):
                        pe.wait_ge(*ah.empty(n, f"xnT{d}"))
                if slot < 10:
                    project(slot // 2, slot % 2)
                if slot == 10:
                    for d in range(DB):
                        project(5, d)
                if slot == 11:
                    if has(n, 2):
                        pe.wait_ge(logits_kept, n - 1)
                    pe.wait_ge(squares, 2 * DB * (n + 1))
                    for i in range(2):
                        last = head_sums(ssq_ps[:, i], sqT[:, DB * (1 - i):DB * (2 - i)])
                    last.then_inc(sumsq, 1)
                if slot in (12, 13):
                    c, at = ("K", DB) if slot == 12 else ("Q", 0)
                    pe.wait_ge(silu_done, 3 * DB * n + at + DB)
                    for h in range(2):
                        turn_out(fr, n, f"tok{c}{h}", qkvT[:, at:at + DB], h)
                if slot == 14:
                    pe.wait_ge(silu_done, 3 * DB * (n + 1))
                    for h in range(2):
                        turn_out(fr, n, f"tokV{h}", qkvT[:, 2 * DB:], h)
                if slot == 15:
                    pe.wait_ge(*fr.empty(n, "tokK1"))
                    for d in range(DB):
                        turn_back(fr, n, f"KT{d}", Kt, d)
                    pe.wait_ge(kb_ready, n + 1)
                    for d in range(DB):
                        turn_back(fr, n, f"KbT{d}", Kb, d)
                if slot == 16:
                    pe.wait_ge(*fr.empty(n, "tokQ1"))
                    for d in range(DB):
                        turn_back(fr, n, f"QT{d}", Qt, d)
                    pe.wait_ge(*fr.empty(n, "KbT1"))
                    to = fill(fr, n, "AT")
                    for k in range(GT):
                        for d in range(DB):
                            last = pe.matmul(to[:, k * P:(k + 1) * P], KT[:, d, k * P:(k + 1) * P],
                                             KbT[:, d, k * P:(k + 1) * P], start=(d == 0), stop=(d == DB - 1))
                    last.then_inc(fr.sem_full, 1)
                if slot == 19:
                    pe.wait_ge(x0t_ready, n + 1)
                    by_tile(fr, n, "X", lambda to, k: pe.transpose(to, XTr[:, k], idt[:]))

            def back(slot, b, it):
                n = 2 * it + b
                if slot < 10:
                    s = slot // 2 + 1
                    if slot % 2 == 0:
                        pe.wait_ge(masked, LEVELS * n + s + 1)
                        pe.wait_ge(*(fr.empty(n, "X") if s == 1 else bk.empty(n, f"Z{s - 1}")))
                        by_tile(bk, n, f"Y{s}", lambda to, k: pe.matmul(to, CT[:, s - 1, k], X[:, k], start=True, stop=True))
                    else:
                        if s > 1:
                            pe.wait_ge(*bk.empty(n, f"ZT{s - 1}"))
                        pe.wait_ge(*bk.empty(n, f"Y{s}"))
                        if s < LEVELS - 1:
                            by_tile(bk, n, f"Z{s}", lambda to, k: pe.matmul(to, XTr[:, k], Y[:, k], start=True, stop=True))
                        by_tile(bk, n, f"ZT{s}", lambda to, k: pe.matmul(to, Y[:, k], XTr[:, k], start=True, stop=True))
                if slot == W_SLOT:
                    pe.wait_ge(tt_ready, n + 1)
                    for w, src in (("W", Kb), ("U", Vb)):
                        for d in range(DB):
                            by_tile(bk, n, f"{w}T{d}", lambda to, k: pe.matmul(
                                to, src[:, k, d * P:(d + 1) * P], XTr[:, k], start=True, stop=True))
                if slot == 12:
                    pe.wait_ge(qk_ready, n + 1)
                    if isinstance(n, int) and n == GROUPS - 1:
                        pe.wait_ge(logits_kept, n)
                    else:
                        pe.wait_ge(sumsq_kept, n + 2)
                    for d in range(DB):
                        own = qk[:, d, :, 0:b + 1]
                        own = own.rearrange("p a b -> p (a b)") if b + 1 == BATCH else own[:, :, 0]
                        last = pe.matmul(corr_ps[:, 0:GCH * (b + 1)], ones, own, start=(d == 0), stop=(d == DB - 1))
                    last.then_inc(corr_mm, 1)
                if slot == 14:
                    pe.wait_ge(edge_u, 4 * (n + 1))
                    pe.wait_ge(o_sq, DB * (n + 1))
                    head_sums(oss_ps, osqT).then_inc(o_sum, 1)
                    for h in range(2):
                        turn_out(bk, n, f"otok{h}", oT, h)
                if slot == 16:
                    pe.wait_ge(*bk.empty(n, "otok1"))
                    for d in range(DB):
                        turn_back(bk, n, f"oT{d}", ob, d)
                if slot == 17:
                    for d in range(DB):
                        pe.wait_ge(*bk.empty(n, f"oT{d}"))
                    pe.wait_ge(wo_scaled, DB)
                    for h in range(2):
                        to = fill(bk, n, f"attn{h}")
                        for k in range(2):
                            for d in range(DB):
                                last = pe.matmul(to[:, k * D:(k + 1) * D], oT[:, d, (2 * h + k) * P:(2 * h + k + 1) * P],
                                                 wo[:, d], start=(d == 0), stop=(d == DB - 1))
                        last.then_inc(bk.sem_full, 1)
                if slot == 19:
                    pe.wait_ge(x2n_ready, GT * (n + 1))
                    for d in range(DB):
                        turn_back(bk, n, f"x2nT{d}", x2n, d)
                    for d in range(DB):
                        pe.wait_ge(*bk.empty(n, f"x2nT{d}"))
                    pe.wait_ge(o_mean, n + 1)
                    for k in range(GT):
                        for d in range(DB):
                            last = pe.matmul(logit_ps[:, k * N_RT:(k + 1) * N_RT], x2nT[:, d, k * P:(k + 1) * P], cen[:, d],
                                             start=(d == 0), stop=(d == DB - 1))
                    last.then_inc(logit_mm, 1)

            def ahead(slot, b, it):
                n = 2 * it + b
                if slot == 18:
                    pe.wait_ge(xn_ready, GT * (n + 1))
                    for d in range(DB):
                        turn_back(ah, n, f"xnT{d}", xn, d)
                if slot == 19:
                    for d in range(DB):
                        pe.wait_ge(*ah.empty(n, f"xnT{d}"))
                    to = fill(ah, n, "beta")
                    for k in range(GT):
                        for d in range(DB):
                            last = pe.matmul(to[:, k * NH:(k + 1) * NH], xnT[:, d, k * P:(k + 1) * P], wb[:, d],
                                             start=(d == 0), stop=(d == DB - 1))
                    last.then_inc(ah.sem_full, 1)

            run_attention(pe, front, back, ahead)
            pe.drain().then_inc(pe_idle, 1)

            def rank_rows():
                pe.wait_ge(mask_ready, 1)
                pe.wait_ge(route_in, 96)
                maskf = scr["mask"].rearrange("p t e -> p (t e)")
                pe.matmul(ps[:, 7, 0:TTOK * N_RT], scr["rc"][:, 0], maskf, start=True, stop=True)
                pe.matmul(ps[:, 7, TTOK * N_RT:2 * TTOK * N_RT], scr["rc"][:, 1], maskf,
                          start=True, stop=True).then_inc(ranked, 1)

            def turn(t):
                b = parity(t)
                pe.wait_ge(*x_there(t))
                if has(t, 1):
                    pe.wait_ge(x_low, val(t))
                for d in range(DB):
                    for c in range(XB):
                        last = pe.transpose(ps[:, 6, d * XT + c * P:d * XT + (c + 1) * P],
                                            xg[b][:, c, d * P:(d + 1) * P], idt[:])
                last.then_inc(x_turned, 1)

            def up(u, t, slot):
                n, b = val(u), parity(t)
                pe.wait_ge(x_low, val(t) + 1)
                for c in range(4):
                    if has(u, 1):
                        pe.wait_ge(h_low, 4 * n - 3 + c)
                    for f in range(2):
                        cols = slice((2 * c + f) * P, (2 * c + f + 1) * P)
                        parts = [(d, hw, hx) for d in range(DB) for hw, hx in ((0, 0), (0, 1), (1, 0))]
                        for q, (d, hw, hx) in enumerate(parts):
                            last = pe.matmul(ps[:, c, f * XT:(f + 1) * XT], weight(slot, d, hw, cols), xs[b][:, hx, d],
                                             start=(q == 0), stop=(q == len(parts) - 1))
                    last.then_inc(up_done, 1)

            def down(u, slot):
                n, b = val(u), parity(u)
                pe.wait_ge(h_low, 4 * n + 4)
                if has(u, 2):
                    pe.wait_ge(y_out, n - 1)
                for c in range(XB):
                    parts = [(f, hh, hw) for f in range(FB) for hh, hw in ((0, 0), (0, 1), (1, 0))]
                    for q, (f, hh, hw) in enumerate(parts):
                        cols = slice(f % 4 * D, (f % 4 + 1) * D)
                        last = pe.matmul(ps[:, 4 + b, c * D:(c + 1) * D], hs[b][:, hh, f, c * P:(c + 1) * P],
                                         weight(slot, DB + f // 4, hw, cols), start=(q == 0), stop=(q == len(parts) - 1))
                last.then_inc(down_done, 1)

            pe.wait_ge(w_split, SH_PIECES)
            pe.wait_ge(kept, 1)

            def between(step):
                if step == 3:
                    rank_rows()

            shared_order(turn, lambda u, t: up(u, t, parity(u)), lambda u, t: down(u, parity(u)), between)(pe)

            pe.wait_ge(routed, 2)
            pe.wait_ge(rw_low, N_RT * PIECES)

            def expert_of(i):
                return pe.value_load(eid[0:1, bass.ds(val(i), 1)], min_val=N_SH * PIECES, max_val=(SLOTS - 1) * PIECES)

            def unit_of(i):
                return Num(unit_of_routed(i.v), i.par)

            routed_order(pe, turn, lambda i: up(unit_of(i), Num(i.v + X_TILES, i.par), expert_of(i)),
                         lambda i: down(unit_of(i), expert_of(i)))

        @block.vector
        def _(dve):
            dve.wait_ge(consts_made, CONSTS_MADE)
            dve.wait_ge(const_in, CONSTS_IN)
            for d in range(DB):
                dve.tensor_scalar(wo[:, d], wo[:, d], gcol[:, d:d + 1], None, ALU.mult).then_inc(wo_scaled, 1)

            def layer_stats(n, src, b6, m2, rs, counted):
                for k in range(GT):
                    last = dve.bn_stats(b6[:, k], src[:, k])
                last.then_inc(counted, 1)
                settled(dve, counted, 3 * n + 1)
                for k in range(GT):
                    last = dve.bn_aggr(m2[:, k], b6[:, k])
                last.then_inc(counted, 1)
                dve.wait_ge(counted, 3 * n + 2)
                dve.tensor_scalar(rs, m2[:, :, 1], EPS, None, ALU.add).then_inc(counted, 1)

            def by_head(a):
                return a.unsqueeze(2).to_broadcast([P, a.shape[-1], HD])

            def heads(a):
                return a.rearrange("p k (h e) -> p (k h) e", h=NH)

            def bank_heads(a):
                return a.rearrange("p (g e) -> p g e", e=HD)

            def front(slot, b, it):
                n = 2 * it + b

                def convolve(m):
                    at = 3 * DB * (TAPS - 1) * n + (TAPS - 1) * m
                    dve.wait_ge(*fr.empty(n, f"proj{m}"))
                    for t in range(TAPS - 1):
                        if t:
                            dve.wait_ge(conv_step, at + t)
                        dve.scalar_tensor_tensor(qkvT[:, m], pre[:, m, t:t + GRP], cw[:, m, t:t + 1],
                                                 qkvT[:, m], ALU.mult, ALU.add).then_inc(conv_step, 1)

                if slot == 0:
                    dve.tensor_copy(pre[:, :, 0:TAPS - 1], hist[b]).then_inc(hist_saved, 1)
                    dve.wait_ge(hist_saved, n + 1)
                if slot <= 10 and slot % 2 == 0 and slot >= 2:
                    convolve(slot // 2 - 1)
                if slot == 12:
                    convolve(5)
                    dve.tensor_copy(hist[b], pre[:, :, GRP:GRP + TAPS - 1]).then_inc(hist_set, 1)
                if slot in (12, 13):
                    c, i, to = ("K", 0, Kt) if slot == 12 else ("Q", 1, Qt)
                    dve.wait_ge(rnorm, 2 * n + i + 1)
                    for h in range(2):
                        name = f"tok{c}{h}"
                        dve.wait_ge(*fr.full(n, name))
                        dve.tensor_tensor(heads(to[:, 2 * h:2 * h + 2]), bank_heads(fr.bank(name)),
                                          by_head(ssq[:, i, 2 * NH * h:2 * NH * (h + 1)]), ALU.mult).then_inc(fr.empty(n, name)[0], 1)
                if slot == 13:
                    dve.wait_ge(*fr.empty(n, "tokK1"))
                    dve.wait_ge(beta_ready, n + 1)
                    if has(n, 1):
                        dve.wait_ge(*bk.full(n - 1, f"UT{DB - 1}"))
                    dve.tensor_tensor(heads(Kb), heads(Kt), by_head(beta[b]), ALU.mult).then_inc(kb_ready, 1)
                if slot == 14:
                    for h in range(2):
                        name = f"tokV{h}"
                        dve.wait_ge(*fr.full(n, name))
                        dve.tensor_tensor(heads(Vb[:, 2 * h:2 * h + 2]), bank_heads(fr.bank(name)),
                                          by_head(beta[b][:, 2 * NH * h:2 * NH * (h + 1)]), ALU.mult).then_inc(fr.empty(n, name)[0], 1)
                if slot == 18:
                    dve.wait_ge(masked, LEVELS * n + 1)
                    dve.tensor_tensor(XTr, XTr, idt[:].unsqueeze(1).to_broadcast([P, GT, P]), ALU.add).then_inc(x0t_ready, 1)
                if slot == 19:
                    dve.wait_ge(*fr.full(n, "X"))
                    dve.tensor_copy(X.rearrange("p k t -> p (k t)"), fr.bank("X")).then_inc(fr.empty(n, "X")[0], 1)

            def back(slot, b, it):
                n = 2 * it + b
                e = b + 1

                def chunks(a):
                    return a.rearrange("p d (c t) -> p d c t", t=CH)

                def flat(a):
                    return a.rearrange("p k t -> p (k t)")

                if slot < 10 and slot % 2:
                    s = slot // 2 + 1
                    for name, to in ((f"Z{s}", X), (f"ZT{s}", XTr)):
                        if s < LEVELS - 1 or to is XTr:
                            dve.wait_ge(*bk.full(n, name))
                            dve.tensor_tensor(flat(to), flat(to), bk.bank(name), ALU.add).then_inc(bk.empty(n, name)[0], 1)
                    if s == LEVELS - 1:
                        dve.wait_ge(*bk.empty(n, f"ZT{s}"))
                        dve.scalar_tensor_tensor(XTr, XTr, 3.0, minus2i.unsqueeze(1).to_broadcast([P, GT, P]),
                                                 ALU.mult, ALU.add).then_inc(tt_ready, 1)
                if slot == W_SLOT:
                    if has(n, 1):
                        dve.wait_ge(corr_mm, n)
                    dve.tensor_tensor(qk[:, :, :, 0:e], chunks(QT)[:, :, :, 0:e], chunks(KT)[:, :, :, 0:e],
                                      ALU.mult).then_inc(qk_ready, 1)
                    for i, w in enumerate("WU"):
                        for d in range(DB):
                            name = f"{w}T{d}"
                            dve.wait_ge(*bk.full(n, name))
                            dve.tensor_tensor(prod[:, DB * i + d], bk.bank(name), KT[:, d], ALU.mult).then_inc(products, 1)
                            dve.tensor_copy(Wc[:, i, d, :, 0:e],
                                            bk.bank(name).rearrange("p (c t) -> p c t", t=CH)[:, :, 0:e]).then_inc(bk.empty(n, name)[0], 1)
                if slot == 12:
                    dve.tensor_copy(Sd[b][:, :, 0:1], Sd[b][:, :, GCH:GCH + 1]).then_inc(carry, 1)
                    dve.wait_ge(products, 4 * n + 4)
                    dve.tensor_reduce(PR.rearrange("p a d c -> p (a d c)"),
                                      prod.rearrange("p a (c t) -> p (a c) t", t=CH), AX_X, ALU.add).then_inc(chunk_sums, 1)
                    dve.wait_ge(chunk_sums, n + 1)
                    dve.tensor_scalar(PR[:, 0], PR[:, 0], -1.0, 1.0, ALU.mult, ALU.add).then_inc(one_minus, 1)
                    dve.wait_ge(one_minus, n + 1)
                    dve.wait_ge(carry, n + 1)
                    for d in range(DB):
                        dve.tensor_tensor_scan(Sd[b][:, d, 1:GCH + 1], PR[:, 0, d], PR[:, 1, d], Sd[b][:, d, 0:1],
                                               ALU.mult, ALU.add).then_inc(scanned, 1)
                    dve.wait_ge(scanned, DB * (n + 1))
                    if has(n, 1):
                        dve.wait_ge(logit_mm, n)
                    before = Sd[b][:, :, 0:GCH].unsqueeze(3)
                    dve.tensor_tensor(chunks(oT), chunks(QT), before.to_broadcast([P, DB, GCH, CH]), ALU.mult).then_inc(edge_u, 1)
                    own = wu[:, :, :, 0:e]
                    dve.wait_ge(*bk.empty(n, "UT1"))
                    dve.tensor_tensor(own, Wc[:, 0, :, :, 0:e], before.to_broadcast([P, DB, GCH, e]), ALU.mult).then_inc(edge_u, 1)
                    dve.wait_ge(edge_u, 4 * n + 2)
                    dve.tensor_tensor(own, Wc[:, 1, :, :, 0:e], own, ALU.subtract).then_inc(edge_u, 1)
                    dve.wait_ge(edge_u, 4 * n + 3)
                    dve.wait_ge(corr_mm, n + 1)
                    dots = corr_ps[:, 0:GCH * e].rearrange("p (c t) -> p c t", t=e).unsqueeze(1)
                    dve.tensor_tensor(own, own, dots.to_broadcast([P, DB, GCH, e]), ALU.mult).then_inc(edge_u, 1)
                    dve.wait_ge(edge_u, 4 * n + 4)
                    dve.tensor_tensor(chunks(oT)[:, :, :, 0:e], chunks(oT)[:, :, :, 0:e], own, ALU.add).then_inc(o_ready, 1)
                if slot == 14:
                    dve.wait_ge(o_sum, n + 1)
                    dve.tensor_scalar(oss, oss_ps, 1.0 / HD, EPS, ALU.mult, ALU.add).then_inc(o_mean, 1)
                if slot == 15:
                    dve.wait_ge(o_rms, n + 1)
                    if has(n, 1):
                        dve.wait_ge(tokens_out[1 - b], 32 * (it + b))
                        dve.wait_ge(*bk.full(n - 1, "x2nT1"))
                    for h in range(2):
                        name = f"otok{h}"
                        dve.wait_ge(*bk.full(n, name))
                        dve.tensor_tensor(heads(ob[:, 2 * h:2 * h + 2]), bank_heads(bk.bank(name)),
                                          by_head(oss[:, 2 * NH * h:2 * NH * (h + 1)]), ALU.mult).then_inc(bk.empty(n, name)[0], 1)
                if slot == 17:
                    dve.wait_ge(xr_in[b], 16 * (it + 1))
                    for h in range(2):
                        name = f"attn{h}"
                        dve.wait_ge(*bk.full(n, name))
                        part = xr[:, 2 * h:2 * h + 2].rearrange("p k d -> p (k d)")
                        dve.tensor_tensor(part, part, bk.bank(name), ALU.add).then_inc(bk.empty(n, name)[0], 1)
                    dve.wait_ge(*bk.empty(n, "attn1"))
                    layer_stats(n, xr, bn2, mv2, rstd2, stats2)
                if slot == 18:
                    dve.wait_ge(rstd2_ready, n + 1)
                    dve.scalar_tensor_tensor(nmr2, mv2[:, :, 0], -1.0, rstd2, ALU.mult, ALU.mult).then_inc(nmr2_ready, 1)
                if slot == 19:
                    dve.wait_ge(logit_mm, n + 1)
                    dve.tensor_copy(logits[:, bass.ds(b * (TTOK // BATCH) + GT * it, GT), :],
                                    logit_ps.rearrange("p (k e) -> p k e", e=N_RT)).then_inc(logits_kept, 1)

            def ahead(slot, b, it):
                n = 2 * it + b
                if slot == 16:
                    dve.wait_ge(xl_in[b], 16 * (it + 1))
                    layer_stats(n, xl, bn, mv, rstd, stats)
                if slot == 17:
                    dve.wait_ge(rstd_ready, n + 1)
                    dve.scalar_tensor_tensor(nmr, mv[:, :, 0], -1.0, rstd, ALU.mult, ALU.mult).then_inc(nmr_ready, 1)
                if slot == 19:
                    dve.wait_ge(*ah.empty(n, "beta"))
                    dve.tensor_scalar(beta[b], th, 0.5, 0.5, ALU.mult, ALU.add).then_inc(beta_ready, 1)

            run_attention(dve, front, back, ahead)
            dve.wait_ge(logits_kept, GROUPS)
            dve.drain().then_inc(kept, 1)
            dve.wait_ge(route_in, 96)
            r = scr
            step = [0]

            def then(ins, s=route):
                step[0] += 1
                ins.then_inc(route, 1)
                dve.wait_ge(route, step[0])

            def over_tiles(a):
                return a.unsqueeze(1).to_broadcast([P, TTOK, a.shape[-1]])

            def over_experts(a):
                return a.unsqueeze(2).to_broadcast([P, a.shape[-1], N_RT])

            then(dve.tensor_tensor(r["z"], logits[:], over_tiles(r["biasc"]), ALU.add))
            then(dve.memset(r["onec"], 1.0))
            dve.wait_ge(scored, 2)

            def pick(hot):
                then(dve.tensor_reduce(r["m"], r["bl"], AX_X, ALU.max))
                then(dve.tensor_tensor(r["tmp"], r["bl"], over_experts(r["m"]), ALU.is_equal))
                then(dve.tensor_tensor(r["tmp"], r["tmp"], over_tiles(r["prefc"]), ALU.mult))
                then(dve.tensor_reduce(r["mx"], r["tmp"], AX_X, ALU.max))
                then(dve.tensor_tensor(hot, r["tmp"], over_experts(r["mx"]), ALU.is_equal))

            rank = ps[:, 7, 0:TTOK * N_RT].rearrange("p (t e) -> p t e", e=N_RT)
            count = ps[:, 7, TTOK * N_RT:2 * TTOK * N_RT].rearrange("p (t e) -> p t e", e=N_RT)

            def router(part):
                if part == 0:
                    pick(r["oh1"])
                    then(dve.scalar_tensor_tensor(r["bl"], r["oh1"], -2.0, r["bl"], ALU.mult, ALU.add))
                if part == 1:
                    pick(r["oh2"])
                    dve.tensor_tensor(r["mask"], r["oh1"], r["oh2"], ALU.add).then_inc(mask_ready, 1)
                if part == 2:
                    for c, hot in enumerate(("oh1", "oh2")):
                        then(dve.tensor_tensor(r["tmp"], r[hot], r["sc"], ALU.mult))
                        then(dve.tensor_reduce(r["s12"][:, c], r["tmp"], AX_X, ALU.add))
                    dve.tensor_tensor(score_diff[:], r["s12"][:, 0], r["s12"][:, 1], ALU.subtract).then_inc(picked, 1)
                if part == 4:
                    dve.wait_ge(ranked, 1)
                    for e in range(N_RT):
                        then(dve.tensor_tensor_scan(r["inc"][:, :, e], r["onec"], count[:, :, e], 0.0, ALU.mult, ALU.add))
                    whole = r["inc"][:, TTOK - 1, :].unsqueeze(2).to_broadcast([P, N_RT, X_TILES])
                    steps = r["kc"].unsqueeze(1).to_broadcast([P, N_RT, X_TILES])
                    then(dve.tensor_tensor(r["cmp"], whole, steps, ALU.is_gt))
                    then(dve.tensor_reduce(r["nb"], r["cmp"], AX_X, ALU.add))
                if part == 5:
                    then(dve.tensor_tensor_scan(r["tb"], r["onec"][:, 0:N_RT], r["nb"], 0.0, ALU.mult, ALU.add))
                    then(dve.tensor_tensor(r["start"], r["tb"], r["nb"], ALU.subtract))
                    then(dve.tensor_scalar(r["start"], r["start"], float(XT), None, ALU.mult))
                    then(dve.tensor_tensor(r["pos"], r["inc"], count, ALU.subtract))
                    then(dve.tensor_tensor(r["pos"], r["pos"], rank, ALU.add))
                    then(dve.tensor_tensor(r["pos"], r["pos"], over_tiles(r["start"]), ALU.add))
                if part == 6:
                    for c, hot in enumerate(("oh1", "oh2")):
                        then(dve.tensor_tensor(r["tmp"], r[hot], r["pos"], ALU.mult))
                        then(dve.tensor_reduce(r["p12"][:, c], r["tmp"], AX_X, ALU.add))
                    then(dve.tensor_copy(pos_i[:], r["p12"]))
                    then(dve.tensor_scalar(lane[:], pos_i[:], P - 1, None, ALU.bitwise_and))
                    then(dve.tensor_scalar(adr[:], pos_i[:], 7, None, ALU.logical_shift_right))
                    dve.scalar_tensor_tensor(adr[:], lane[:], float(IDX_COLS), adr[:], ALU.mult, ALU.add).then_inc(routed, 1)
                if part == 7:
                    tiles = r["tc"].unsqueeze(2).to_broadcast([P, R_TILES, N_RT])
                    ends = r["tb"].unsqueeze(1).to_broadcast([P, R_TILES, N_RT])
                    then(dve.tensor_tensor(r["cmpt"], ends, tiles, ALU.is_le))
                    then(dve.tensor_reduce(r["es"], r["cmpt"], AX_X, ALU.add))
                    then(dve.tensor_scalar(r["es"], r["es"], float(N_RT - 1), None, ALU.min))
                    dve.tensor_scalar(eid[:], r["es"], float(PIECES), float(SH_PIECES), ALU.mult, ALU.add).then_inc(routed, 1)

            def x_low_half(t):
                b = parity(t)
                dve.wait_ge(x_high, val(t) + 1)
                dve.scalar_tensor_tensor(xs[b][:, 1].rearrange("p d t -> p (d t)"), ps[:, 6, :], X_SCALE,
                                         xs[b][:, 0].rearrange("p d t -> p (d t)"), ALU.mult, ALU.subtract).then_inc(x_low, 1)

            def unit(n, b):
                for c in range(4):
                    dve.wait_ge(h_high, 4 * n + c + 1)
                    hi, lo = (hs[b][:, q, 2 * c:2 * c + 2].rearrange("p f t -> p (f t)") for q in range(2))
                    dve.scalar_tensor_tensor(lo, ps[:, c, :], H_SCALE, hi, ALU.mult, ALU.subtract).then_inc(h_low, 1)

            def shared_unit(u, t):
                n = val(u)
                unit(n, parity(u))
                dve.wait_ge(rw_high, n + 1)
                dve.scalar_tensor_tensor(piece(n + SH_PIECES, 1), wstage[:, parity(u):parity(u) + 1, :], W_SCALE,
                                         piece(n + SH_PIECES, 0), ALU.mult, ALU.subtract).then_inc(rw_low, 1)

            def y_shared(u, t):
                n, b, e = val(u), parity(t), parity(u)
                dve.wait_ge(down_done, n + 1)
                if e == 0:
                    dve.wait_ge(base_in[b], 16 * (half(t) + 1))
                    if has(t, 2):
                        dve.wait_ge(y_stored[b], 16 * half(t))
                else:
                    dve.wait_ge(y_out, n)
                flat = lambda a: a.rearrange("p k d -> p (k d)")
                dve.scalar_tensor_tensor(flat(yo[b]), ps[:, 4 + e, :], 1.0 / (H_SCALE * W_SCALE),
                                         flat(bt[b] if e == 0 else yo[b]), ALU.mult, ALU.add).then_inc(y_out, 1)

            def y_routed(i):
                n, b = unit_of_routed(i.v), i.par
                dve.wait_ge(down_done, n + 1)
                dve.wait_ge(y_stored[b], 16 * (X_TILES // 2 + i.half))
                dve.tensor_scalar(yo[b].rearrange("p k d -> p (k d)"), ps[:, 4 + b, :],
                                  1.0 / (H_SCALE * W_SCALE), None, ALU.mult).then_inc(y_out, 1)

            shared_order(x_low_half, shared_unit, y_shared, between=router)(dve)
            routed_order(dve, x_low_half, lambda i: unit(unit_of_routed(i.v), i.par), y_routed)

            dve.wait_ge(tops_ready, TOPK)

            def combine(t, b, k):
                dve.wait_ge(acc_in[b], 16 * (k + 1))
                dve.wait_ge(y_in[b], 32 * (k + 1))
                for c in range(TOPK):
                    if c:
                        dve.wait_ge(combined, 2 * t + c)
                    dve.scalar_tensor_tensor(acc[b], yrow[b][:, c], wtop[:, c, bass.ds(t, 1)], acc[b],
                                             ALU.mult, ALU.add).then_inc(combined, 1)

            with dve.Fori(0, TTOK // 4) as k:
                for b in range(4):
                    combine(4 * k + b, b, k)


def run_attention(eng, front, back, ahead):

    def tick(f=None, b=None, a=None):
        for slot in range(SLOTS_A):
            for stage, at in ((back, b), (front, f), (ahead, a)):
                if at:
                    stage(slot, *at)

    tick(a=(0, 0))
    tick(f=(0, 0), a=(1, 0))
    tick(f=(1, 0), b=(0, 0), a=(0, 1))
    with eng.Fori(0, ROUNDS - 2) as it:
        tick(f=(0, it + 1), b=(1, it), a=(1, it + 1))
        tick(f=(1, it + 1), b=(0, it + 1), a=(0, it + 2))
    r = ROUNDS - 1
    tick(f=(0, r), b=(1, r - 1), a=(1, r))
    tick(f=(1, r), b=(0, r))
    tick(b=(1, r))


def constants():
    i = np.arange(P)
    same = (i[:, None] // CH) == (i[None, :] // CH)
    masks = np.zeros((P, LEVELS, P), np.float32)
    for s in range(LEVELS):
        w = 1 << s
        joined = same & (i[:, None] // (2 * w) == i[None, :] // (2 * w))
        joined &= ((i[:, None] // w) % 2 == 0) & ((i[None, :] // w) % 2 == 1)
        masks[:, s][joined] = -1.0
    eye = np.eye(P, dtype=np.float32)
    before = np.stack([(i[:, None] < i[None, :]), np.ones((P, P))], axis=1).astype(np.float32)

    def row(a):
        return np.ascontiguousarray(np.broadcast_to(np.asarray(a, np.float32), (P, len(a))))

    return {
        "ident": eye, "lvl_masks": masks, "eye2": -2.0 * eye, "head_sel": (i[:, None] // HD == np.arange(P // HD)).astype(np.float32), "block_tri": before,
        "row_iota": row(XT * np.arange(X_TILES)), "tile_iota": row(np.arange(R_TILES)),
        "pref": row(N_RT - np.arange(N_RT)),
        "tok_id": (P * np.arange(TTOK)[None, :] + i[:, None]).astype(np.int32),
    }


def laid_out(i):
    def split(w):
        return np.ascontiguousarray(np.asarray(w).reshape(-1, P, w.shape[-1]).transpose(1, 0, 2))

    conv = np.concatenate([i[f"L0_attn_conv_{c}"].reshape(D, TAPS) for c in "qkv"])
    up = np.concatenate([i["L0_ffn_Wfc_sh"], i["L0_ffn_Wfc_r"]]).transpose(0, 2, 1)
    down = np.concatenate([i["L0_ffn_Wproj_sh"], i["L0_ffn_Wproj_r"]]).transpose(0, 2, 1)
    up = up.reshape(SLOTS, DB, P, PIECE)
    down = down.reshape(SLOTS, FB, P, D).transpose(0, 2, 1, 3).reshape(SLOTS, P, PIECES // 2, PIECE).transpose(0, 2, 1, 3)
    return {
        "x": i["L0_attn_x"].reshape(TOK, D),
        "w_qkv": split(np.concatenate([i[f"L0_attn_W{c}"] for c in "qkv"], axis=1)),
        "w_beta": split(i["L0_attn_Wb"]),
        "conv_w": split(conv),
        "g_col": split(np.tile(i["L0_attn_g"], NH)[:, None])[:, :, 0],
        "w_o": split(i["L0_attn_Wo"]),
        "cent": split(i["L0_ffn_centroids"].T),
        "bias": np.ascontiguousarray(np.broadcast_to(i["L0_ffn_routing_bias"], (P, N_RT))),
        "w_ffn": np.concatenate([up, down], axis=1).reshape(SLOTS * PIECES, P, PIECE),
    }


_ORDER = ["x", "w_qkv", "w_beta", "conv_w", "g_col", "w_o", "cent", "bias", "w_ffn",
          "ident", "lvl_masks", "eye2", "head_sel", "block_tri", "row_iota", "tile_iota", "pref", "tok_id"]


def kernel(**inputs):
    import concourse.bacc as bacc
    from concourse.bass_utils import run_bass_kernel_spmd

    arrays = {**laid_out({k: np.asarray(v) for k, v in inputs.items()}), **constants()}
    nc = bacc.Bacc("TRN2", target_bir_lowering=False, num_devices=1)
    args = [nc.dram_tensor(f"in_{n}", arrays[n].shape, mybir.dt.from_np(arrays[n].dtype), kind="ExternalInput").ap()
            for n in _ORDER]
    out = nc.dram_tensor("out", (TOK, D), F32, kind="ExternalOutput").ap()
    build(nc, *args, out)
    feed = {f"in_{n}": np.ascontiguousarray(arrays[n]) for n in _ORDER}
    r = run_bass_kernel_spmd(nc, [feed], core_ids=[0])
    return r.results[0]["out"].reshape(BATCH, SEQ, D)
```

```python
from contextlib import ExitStack

import numpy as np

import concourse.bass as bass
from concourse import mybir

ALU = mybir.AluOpType
ACT = mybir.ActivationFunctionType
F32 = mybir.dt.float32
F16 = mybir.dt.float16
I32 = mybir.dt.int32
AX_X = mybir.AxisListType.X

P = 128
BATCH, SEQ, D = 2, 2048, 256
TOK = BATCH * SEQ
NH, HD = 4, 64
CH = 64
TAPS = 4
EPS = 1e-5
DB = D // P

GRP = 512
GT = GRP // P
GROUPS = TOK // GRP
ROUNDS = GROUPS // BATCH
GCH = GRP // CH
LEVELS = 6

FF = 1024
FB = FF // P
N_SH, N_RT, TOPK = 2, 8, 2
SLOTS = N_SH + N_RT
PIECE = 1024
PIECES = 2 * DB * FF // PIECE
CONSTS_MADE = 2 + 2 * BATCH
CONSTS_IN = 16 * 10
XT = 256
XB = XT // P
X_TILES = TOK // XT
S_TILES = X_TILES // 2
S_UNITS = N_SH * S_TILES
R_TILES = TOK * TOPK // XT + N_RT - 1
TTOK = TOK // P
IDX_COLS = R_TILES * XB
COMBINES = 2 * XB * TOPK
RANK_STEP = 2
PEELED = 4
X_SCALE = 256.0
W_SCALE = 256.0
H_SCALE = 64.0


class Ring:

    def __init__(self, banks, fills, sem_full, sem_empty):
        self.banks, self.fills = banks, fills
        self.at = {name: i for i, (name, _) in enumerate(fills)}
        self.sem_full, self.sem_empty = sem_full, sem_empty
        self.count = {e: sum(o == e for _, o in fills) for e in sem_empty}
        self.rank = [sum(o == e for _, o in fills[:i]) for i, (_, e) in enumerate(fills)]

    def bank(self, name):
        return self.banks[self.at[name] % len(self.banks)]

    def full(self, n, name):
        return self.sem_full, n * len(self.fills) + self.at[name] + 1

    def empty(self, n, name):
        i = self.at[name]
        e = self.fills[i][1]
        return self.sem_empty[e], n * self.count[e] + self.rank[i] + 1

    def free(self, n, name):
        i = self.at[name]
        if i >= len(self.banks):
            return self.empty(n, self.fills[i - len(self.banks)][0])
        last = [k for k in range(len(self.fills)) if k % len(self.banks) == i % len(self.banks)][-1]
        e = self.fills[last][1]
        return self.sem_empty[e], n * self.count[e]


FRONT_FILLS = (
    [(f"proj{m}", "act") for m in range(3 * DB)]
    + [(f"tokK{h}", "dve") for h in range(2)]
    + [(f"{c}T{d}", "act") for c in ("K", "Kb") for d in range(DB)]
    + [("AT", "act")]
    + [(f"tokQ{h}", "dve") for h in range(2)]
    + [(f"QT{d}", "act") for d in range(DB)]
    + [(f"tokV{h}", "dve") for h in range(2)]
    + [("X", "dve")]
)
BACK_FILLS = (
    [(f"{w}{s}", "act" if w == "Y" else "dve")
     for s in range(1, LEVELS) for w in ("Y", "Z", "ZT") if (w, s) != ("Z", LEVELS - 1)]
    + [(f"{w}T{d}", "dve") for w in ("W", "U") for d in range(DB)]
)
TAIL_FILLS = (
    [(f"otok{h}", "dve") for h in range(2)]
    + [(f"oT{d}", "act") for d in range(DB)]
    + [(f"attn{h}", "dve") for h in range(2)]
    + [(f"x2nT{d}", "act") for d in range(DB)]
)
AHEAD_FILLS = [(f"xnT{d}", "act") for d in range(DB)] + [("beta", "act")]
SLOTS_A = 19
W_SLOT = 11


class Tile:

    def __init__(self, phase, v, par, half):
        self.phase, self.v, self.par, self.half = phase, v, par, half

    @property
    def seq(self):
        return self.v + (0, S_TILES, S_TILES + R_TILES)[self.phase]

    @property
    def rows(self):
        return self.v + (S_TILES if self.phase == 2 else 0)

    def unit(self, e=0):
        if self.phase == 1:
            return self.v + S_UNITS, self.par
        base = 0 if self.phase == 0 else S_UNITS + R_TILES
        return N_SH * self.v + (base + e), (base + e) % 2


def shared_tile(phase, v, j, h):
    return Tile(phase, v, j if phase == 0 else (S_TILES + R_TILES + j) % 2, h)


def routed_on(b):
    return (R_TILES + 1 - b) // 2


def shared_order(eng, phase, turn, up, down, between=None):
    def step(v, j, h, last=False):
        t, after = shared_tile(phase, v, j, h), shared_tile(phase, v + 1, 1 - j, h + j)
        if not last:
            turn(after)
        up(t, 1)
        down(t, 0)
        if isinstance(v, int) and between:
            between(2 * v)
        if not last:
            up(after, 0)
        down(t, 1)
        if isinstance(v, int) and between:
            between(2 * v + 1)

    turn(shared_tile(phase, 0, 0, 0))
    up(shared_tile(phase, 0, 0, 0), 0)
    peeled = PEELED if phase == 0 else 0
    for v in range(peeled):
        step(v, v % 2, v // 2)
    with eng.Fori(peeled // 2, S_TILES // 2 - 1) as k:
        for j in range(2):
            step(2 * k + j, j, k)
    for v in range(S_TILES - 2, S_TILES):
        step(v, v % 2, v // 2, last=v == S_TILES - 1)


def routed_order(eng, turn, up, down):
    def step(i, j, h, left):
        if left >= 1:
            up(Tile(1, i + 1, 1 - j, h + j))
        if left >= 2:
            turn(Tile(1, i + 2, j, h + 1))
        down(Tile(1, i, j, h))

    turn(Tile(1, 0, 0, 0))
    up(Tile(1, 0, 0, 0))
    turn(Tile(1, 1, 1, 0))
    pairs = (R_TILES - 2) // 2
    with eng.Fori(0, pairs) as k:
        for j in range(2):
            step(2 * k + j, j, k, 2)
    for i in range(2 * pairs, R_TILES):
        step(i, i % 2, i // 2, R_TILES - 1 - i)


def has(n, k):
    return not isinstance(n, int) or n >= k


def build(nc, x, w_qkv, w_beta, conv_w, g_col, w_o, cent, bias, w_ffn,
          ident, lvl_masks, eye2, head_sel, block_tri, row_iota, tile_iota, pref, tok_id, out):
    ctx = ExitStack()
    with ctx:
        def sb(name, shape, dt=F32):
            return ctx.enter_context(nc.sbuf_tensor(name, shape, dt))

        def sem(name):
            return ctx.enter_context(nc.semaphore(name))

        base_d = nc.dram_tensor("base_d", (TOK, D), F32).ap()
        x2n_d = nc.dram_tensor("x2n_d", (TOK, D), F32).ap()
        acc_d = nc.dram_tensor("acc_d", (TOK, D), F32).ap()
        ys_d = nc.dram_tensor("ys_d", (R_TILES * XT, D), F32).ap()
        rows_d = nc.dram_tensor("rows_d", (P * IDX_COLS, 1), I32).ap()

        W = sb("W", [P, SLOTS * PIECES, 2, PIECE], F16)
        arena = W[:, N_SH * PIECES:, :, :].rearrange("p a b c -> p (a b c)").bitcast(F32)
        late_room = sb("late_room", [P, 8192])
        rooms = [[arena, 0, N_RT * PIECES * PIECE], [late_room[:], 0, 8192]]

        def early(*shape):
            n = int(np.prod(shape))
            room = next(r for r in rooms if r[1] + n <= r[2])
            a = room[0][:, room[1]:room[1] + n]
            room[1] += n
            if len(shape) == 1:
                return a
            names = "abcd"[:len(shape)]
            return a.rearrange(f"p ({' '.join(names)}) -> p {' '.join(names)}",
                               **{k: s for k, s in zip(names[1:], shape[1:])})

        idt = sb("idt", [P, P])
        wstage = sb("wstage", [P, 2, PIECE])
        logits = sb("logits", [P, TTOK, N_RT])

        def carve(room, start, shape, dt=F32):
            n = int(np.prod(shape)) // (2 if dt == F16 else 1)
            a = room[:, start:start + n]
            a = a.bitcast(dt) if dt != F32 else a
            if len(shape) > 1:
                names = "abcd"[:len(shape)]
                a = a.rearrange(f"p ({' '.join(names)}) -> p {' '.join(names)}",
                                **{k: z for k, z in zip(names[1:], shape[1:])})
            return a, start + n

        late = 0
        xg, bt, yo, xs, hs = [], [], [], [], []
        for tiles, shape, dt in ((xg, (XB, D), F32), (bt, (XB, D), F32), (yo, (XB, D), F32),
                                 (xs, (2, DB, XT), F16), (hs, (2, FB, XT), F16)):
            for _ in range(2):
                tile, late = carve(late_room[:], late, shape, dt)
                tiles.append(tile)
        assert late <= 8192

        at = (N_RT - 1) * PIECES * PIECE
        scr = {}
        for name, shape in (("rc", (2, P)), ("prefc", (N_RT,)), ("biasc", (N_RT,)), ("kc", (X_TILES,)),
                            ("tc", (R_TILES,)), ("onec", (TTOK,)), ("z", (TTOK, N_RT)), ("sc", (TTOK, N_RT)),
                            ("bl", (TTOK, N_RT)), ("oh1", (TTOK, N_RT)), ("oh2", (TTOK, N_RT)),
                            ("mask", (TTOK, N_RT)), ("tmp", (TTOK, N_RT)), ("inc", (TTOK, N_RT)),
                            ("pos", (TTOK, N_RT)), ("m", (TTOK,)), ("mx", (TTOK,)), ("s12", (2, TTOK)),
                            ("p12", (2, TTOK)), ("cmp", (N_RT, X_TILES)), ("nb", (N_RT,)), ("tb", (N_RT,)),
                            ("start", (N_RT,)), ("cmpt", (R_TILES, N_RT)), ("es", (R_TILES,))):
            scr[name], at = carve(arena, at, shape)
        assert at <= N_RT * PIECES * PIECE
        score_diff = sb("score_diff", [P, TTOK])
        eid = sb("eid", [P, R_TILES], I32)
        pos_i = sb("pos_i", [P, 2, TTOK], I32)
        lane = sb("lane", [P, 2, TTOK], I32)
        adr = sb("adr", [P, 2, TTOK], I32)
        tid = sb("tid", [P, TTOK], I32)
        wtop = sb("wtop", [P, 2, TTOK])
        idx = sb("idx", [P, IDX_COLS], I32)
        scat = sb("scat", [P, 2, 3], I32)
        gath = sb("gath", [P, 2, XB], I32)

        at = 0
        acc, yrow = [], []
        for m in range(2 * XB):
            if m < XB:
                tile, at = carve(arena, at, (D,))
                acc.append(tile)
            tile, at = carve(arena, at, (TOPK, D))
            yrow.append(tile)
        lastidx = sb("lastidx", [P, 4, TOPK], I32)

        wqkv = early(DB, 3 * D)
        wo = early(DB, D)
        wb = early(DB, NH)
        cen = early(DB, N_RT)
        cw = early(3 * DB, TAPS)
        gcol = early(DB)
        masks = early(LEVELS, P)
        minus2i = early(P)
        headsel = early(P // HD)
        ones = early(P)
        minus_half = early(16)
        xl = early(GT, D)
        xr = early(GT, D)
        xnT = early(DB, GRP)
        pre = early(3 * DB, GRP + TAPS - 1)
        hist = [early(3 * DB, TAPS - 1) for _ in range(BATCH)]
        qkvT = early(3 * DB, GRP)
        sqT = early(2 * DB, GRP)
        osqT = early(DB, GRP)
        xn = early(GT, D)
        Qt = early(GT, D)
        Kt = early(GT, D)
        Kb = early(GT, D)
        Vb = early(GT, D)
        KT = early(DB, GRP)
        KbT = early(DB, GRP)
        QT = early(DB, GRP)
        AT = early(GT, P)
        CT = early(LEVELS - 1, GT, P)
        X = early(GT, P)
        XTr = early(GT, P)
        Y = early(GT, P)
        prod = early(2 * DB, GRP)
        Wc = early(2, DB, GCH, BATCH)
        PR = early(2, DB, GCH)
        Sd = [early(DB, GCH + 1) for _ in range(BATCH)]
        qk = early(DB, GCH, BATCH)
        wu = early(DB, GCH, BATCH)
        oT = early(DB, GRP)
        ob = early(GT, D)
        x2n = ob
        x2nT = oT
        bn = early(GT, 6)
        mv = early(GT, 2)
        rstd = early(GT)
        nmr = early(GT)
        bn2 = early(GT, 6)
        mv2 = early(GT, 2)
        rstd2 = early(GT)
        nmr2 = early(GT)
        ssq = early(2, GT * NH)
        th = early(GT * NH)
        beta = [early(GT * NH) for _ in range(BATCH)]
        oss = early(GT * NH)

        ps = ctx.enter_context(nc.psum_tensor("ps", [P, 8, 512], F32))
        small = ps[:, 7, :]
        corr_ps = small[:, 32:32 + GCH * BATCH]
        logit_ps = small[:, 64:64 + GT * N_RT]
        ssq_ps = small[:, 128:128 + 2 * GT * NH].rearrange("p (a t) -> p a t", a=2)
        oss_ps = small[:, 192:192 + GT * NH]

        const_in = sem("const_in")
        consts_made = sem("consts_made")
        wo_scaled = sem("wo_scaled")
        xl_in = [sem(f"xl_in{b}") for b in range(BATCH)]
        xr_in = [sem(f"xr_in{b}") for b in range(BATCH)]
        stats = sem("stats")
        rstd_ready = sem("rstd_ready")
        nmr_ready = sem("nmr_ready")
        xn_ready = sem("xn_ready")
        hist_saved = sem("hist_saved")
        hist_set = sem("hist_set")
        beta_ready = sem("beta_ready")
        pre_ready = sem("pre_ready")
        conv_step = sem("conv_step")
        silu_done = sem("silu_done")
        squares = sem("squares")
        sumsq = sem("sumsq")
        sumsq_kept = sem("sumsq_kept")
        rnorm = sem("rnorm")
        kb_ready = sem("kb_ready")
        masked = sem("masked")
        x0t_ready = sem("x0t_ready")
        tt_ready = sem("tt_ready")
        products = sem("products")
        chunk_sums = sem("chunk_sums")
        carry = sem("carry")
        one_minus = sem("one_minus")
        scanned = sem("scanned")
        qk_ready = sem("qk_ready")
        corr_mm = sem("corr_mm")
        edge_u = sem("edge_u")
        o_ready = sem("o_ready")
        o_sq = sem("o_sq")
        o_sum = sem("o_sum")
        o_mean = sem("o_mean")
        o_rms = sem("o_rms")
        stats2 = sem("stats2")
        rstd2_ready = sem("rstd2_ready")
        nmr2_ready = sem("nmr2_ready")
        x2n_ready = sem("x2n_ready")
        base_ready = sem("base_ready")
        logit_mm = sem("logit_mm")
        logits_kept = sem("logits_kept")
        tokens_out = [sem(f"tokens_out{b}") for b in range(BATCH)]
        w_in = sem("w_in")
        w_scaled = sem("w_scaled")
        w_split = sem("w_split")
        route_in = sem("route_in")
        x_loaded = [sem(f"x_loaded{b}") for b in range(2)]
        base_in = [sem(f"base_in{b}") for b in range(2)]
        x_turned = sem("x_turned")
        x_high = sem("x_high")
        x_low = sem("x_low")
        up_done = sem("up_done")
        gelu_done = sem("gelu_done")
        h_high = sem("h_high")
        h_low = sem("h_low")
        down_done = sem("down_done")
        y_out = sem("y_out")
        y_stored = [sem(f"y_stored{b}") for b in range(2)]
        rw_in = [sem(f"rw_in{b}") for b in range(2)]
        rw_high = sem("rw_high")
        rw_low = sem("rw_low")
        scored = sem("scored")
        route = sem("route")
        mask_ready = sem("mask_ready")
        ranked = sem("ranked")
        picked = sem("picked")
        tops_ready = sem("tops_ready")
        routed = sem("routed")
        rows_zeroed = sem("rows_zeroed")
        rows_out = sem("rows_out")
        x_gathered = [sem(f"x_gathered{b}") for b in range(2)]
        scat_copied = sem("scat_copied")
        scattered = [sem(f"scattered{b}") for b in range(2)]
        idx_in = sem("idx_in")
        gath_copied = sem("gath_copied")
        acc_in = [sem(f"acc_in{b}") for b in range(XB)]
        y_in = [sem(f"y_in{b}") for b in range(4)]
        combined = sem("combined")
        out_done = [sem(f"out_done{b}") for b in range(XB)]

        fr = Ring([ps[:, b, :] for b in range(3)], FRONT_FILLS, sem("front_full"),
                  {"act": sem("front_act"), "dve": sem("front_dve")})
        bk = Ring([ps[:, b, :] for b in range(3, 6)], BACK_FILLS, sem("back_full"),
                  {"act": sem("back_act"), "dve": sem("back_dve")})
        tl = Ring([ps[:, 6, :]], TAIL_FILLS, sem("tail_full"), {"act": sem("tail_act"), "dve": sem("tail_dve")})
        ah = Ring([ps[:, 6, :]], AHEAD_FILLS, sem("ahead_full"), {"act": sem("ahead_act")})
        SH_PIECES = N_SH * PIECES
        assert SH_PIECES == GROUPS

        def tokens(ap, b, it):
            return ap[bass.ds(b * SEQ + it * GRP, GRP), :].rearrange("(k p) d -> p k d", p=P)

        passed = sem("passed")
        kept, pe_idle, act_idle = sem("kept"), sem("pe_idle"), sem("act_idle")

        def rows_of(ap, t):
            return ap[bass.ds(t * XT, XT), :].rearrange("(k p) d -> p k d", p=P)

        def piece(n, half):
            return W[:, n:n + 1, half, :] if isinstance(n, int) else W[:, bass.ds(n, 1), half, :]

        def weight(slot, k, half, cols):
            if isinstance(slot, int):
                return W[:, slot * PIECES + k, half, cols]
            return W[:, bass.ds(slot + k, 1), half, cols].rearrange("p a n -> p (a n)")

        def x_there(t):
            if t.phase == 1:
                return x_gathered[t.par], 16 * XB * (t.half + 1)
            return shared_in(x_loaded[t.par], t)

        def shared_in(s, t):
            return s, 16 * (t.half + (1 if t.phase == 0 else S_TILES // 2 + 1))

        def y_stores(t):
            return t.half + (0, S_TILES // 2, S_TILES // 2 + routed_on(t.par))[t.phase]

        def ups_before(t):
            return t.unit()[0] - (N_SH if t.phase == 0 else 1)

        def settled(eng, s, value):
            eng.wait_ge(s, value)
            eng.sem_inc(passed, 1)

        block = ctx.enter_context(nc.Block())

        @block.sync
        def _(sp):
            def load_ahead(b, it):
                n = 2 * it + b
                if has(n, 1):
                    sp.wait_ge(xn_ready, GT * n)
                sp.dma_start(xl, tokens(x, b, it)).then_inc(xl_in[b], 16)

            load_ahead(0, 0)
            for dst, src in ((idt[:], ident), (wqkv, w_qkv), (cw, conv_w), (wb, w_beta), (masks, lvl_masks),
                             (minus2i, eye2), (wo, w_o), (gcol, g_col), (cen, cent), (headsel, head_sel)):
                sp.dma_start(dst, src).then_inc(const_in, 16)
            load_ahead(1, 0)

            def load_piece(n):
                sp.dma_start(wstage[:, 0, :], w_ffn[bass.ds(n, 1)].rearrange("a p n -> p (a n)")).then_inc(w_in, 16)

            load_piece(0)
            load_ahead(0, 1)

            def tick(b, it):
                n = 2 * it + b
                if has(n, 1):
                    sp.wait_ge(tokens_out[1 - b], 32 * (it + b))
                sp.dma_start(xr, tokens(x, b, it)).then_inc(xr_in[b], 16)
                if not isinstance(n, int) or n + 3 < GROUPS:
                    load_ahead(1 - b, it + 1 + b)
                if not isinstance(n, int) or n + 1 < GROUPS:
                    sp.wait_ge(w_split, n + 1)
                    load_piece(n + 1)
                sp.wait_ge(x2n_ready, GT * (n + 1))
                sp.dma_start(tokens(x2n_d, b, it), x2n).then_inc(tokens_out[b], 16)
                sp.wait_ge(base_ready, n + 1)
                sp.dma_start(tokens(base_d, b, it), xr).then_inc(tokens_out[b], 16)

            tick(0, 0)
            with sp.Fori(0, ROUNDS - 2) as it:
                tick(1, it)
                tick(0, it + 1)
            tick(1, ROUNDS - 2)
            for b in range(BATCH):
                tick(b, ROUNDS - 1)
            for b in range(BATCH):
                sp.wait_ge(tokens_out[b], 32 * ROUNDS)

            for e in (kept, pe_idle, act_idle):
                sp.wait_ge(e, 1)
            for dst, src in ((scr["rc"], block_tri), (scr["prefc"], pref), (scr["biasc"], bias),
                             (scr["kc"], row_iota), (scr["tc"], tile_iota), (tid[:], tok_id)):
                sp.dma_start(dst, src).then_inc(route_in, 16)

            def load_tile(t):
                if has(t.seq, 2):
                    sp.wait_ge(x_turned, t.seq - 1)
                sp.dma_start(xg[t.par], rows_of(x2n_d, t.rows)).then_inc(x_loaded[t.par], 16)

            def load_base(t):
                if t.phase == 2 and not has(t.v, 2):
                    sp.wait_ge(y_out, S_UNITS)
                elif has(t.v, 2):
                    sp.wait_ge(y_out, t.unit()[0] - 3)
                sp.dma_start(bt[t.par], rows_of(base_d, t.rows)).then_inc(base_in[t.par], 16)

            def load_pieces(u):
                for q in range(2):
                    if has(u, 1):
                        sp.wait_ge(rw_low, 2 * u + (q - 1))
                    src = w_ffn[bass.ds(2 * u + (SH_PIECES + q), 1)].rearrange("a p n -> p (a n)")
                    sp.dma_start(wstage[:, q, :], src).then_inc(rw_in[q], 16)

            sp.wait_ge(w_split, SH_PIECES)

            def first_half(v, j, h):
                t = shared_tile(0, v, j, h)
                if not isinstance(v, int) or v + 2 < S_TILES:
                    load_tile(shared_tile(0, v + 2, j, h + 1))
                if not isinstance(v, int) or v + 1 < S_TILES:
                    load_pieces(2 * v + 2)
                    load_pieces(2 * v + 3)
                if not isinstance(v, int) or v + 2 < S_TILES:
                    load_base(shared_tile(0, v + 2, j, h + 1))
                sp.wait_ge(y_out, 2 * v + 2)
                sp.dma_start(rows_of(acc_d, v), yo[t.par]).then_inc(y_stored[t.par], 16)

            for v in range(2):
                load_tile(shared_tile(0, v, v, 0))
                load_base(shared_tile(0, v, v, 0))
                load_pieces(v)
            with sp.Fori(0, S_TILES // 2 - 1) as k:
                for j in range(2):
                    first_half(2 * k + j, j, k)
            for v in range(S_TILES - 2, S_TILES):
                first_half(v, v % 2, v // 2)

            def store_routed(t):
                sp.wait_ge(y_out, t.unit()[0] + 1)
                dst = ys_d[bass.ds(t.v * XT, XT), :].rearrange("(k p) d -> p k d", p=P)
                sp.dma_start(dst, yo[t.par]).then_inc(y_stored[t.par], 16)

            pairs = (R_TILES - 2) // 2
            with sp.Fori(0, pairs) as k:
                for j in range(2):
                    store_routed(Tile(1, 2 * k + j, j, k))
            for i in range(2 * pairs, R_TILES):
                left = R_TILES - 1 - i
                if left < 2:
                    load_tile(shared_tile(2, 1 - left, 1 - left, 0))
                    load_base(shared_tile(2, 1 - left, 1 - left, 0))
                store_routed(Tile(1, i, i % 2, i // 2))

            def load_acc(v, j):
                sp.dma_start(acc[j], acc_d[bass.ds((2 * v + j) * P, P), :]).then_inc(acc_in[j], 16)

            for b in range(2):
                sp.wait_ge(y_stored[b], 16 * S_TILES // 2)
            for j in range(XB):
                load_acc(0, j)

            def second_half(v, j, h):
                t = shared_tile(2, v, j, h)
                if not isinstance(v, int) or v + 2 < S_TILES:
                    load_tile(shared_tile(2, v + 2, j, h + 1))
                    load_base(shared_tile(2, v + 2, j, h + 1))
                for c in range(XB):
                    sp.wait_ge(combined, COMBINES * v + TOPK * (c + 1))
                    sp.dma_start(out[bass.ds((2 * v + c) * P, P), :], acc[c]).then_inc(out_done[c], 16)
                sp.wait_ge(combined, COMBINES * v + COMBINES)
                sp.dma_start(rows_of(out, t.rows), yo[t.par]).then_inc(y_stored[t.par], 16)
                if not isinstance(v, int) or v + 1 < S_TILES:
                    for c in range(XB):
                        sp.wait_ge(out_done[c], 16 * (v + 1))
                        load_acc(v + 1, c)

            with sp.Fori(0, S_TILES // 2 - 1) as k:
                for j in range(2):
                    second_half(2 * k + j, j, k)
            for v in range(S_TILES - 2, S_TILES):
                second_half(v, v % 2, v // 2)
            for b in range(2):
                sp.wait_ge(out_done[b], 16 * S_TILES)
                sp.wait_ge(y_stored[b], 16 * (S_TILES + routed_on(b)))

        @block.gpsimd
        def _(pool):
            pool.memset(ones, 1.0).then_inc(consts_made, 1)
            pool.memset(minus_half, -0.5).then_inc(consts_made, 1)
            for b in range(BATCH):
                pool.memset(hist[b], 0.0).then_inc(consts_made, 1)
                pool.memset(Sd[b], 0.0).then_inc(consts_made, 1)
            pool.wait_ge(consts_made, CONSTS_MADE)
            pool.wait_ge(const_in, CONSTS_IN)

            def front(slot, b, it):
                n = 2 * it + b
                if slot == 11:
                    pool.wait_ge(sumsq_kept, n + 1)
                    for i in range(2):
                        pool.tensor_tensor(ssq[:, i], ssq[:, i], minus_half, ALU.pow).then_inc(rnorm, 1)
                if slot == 15:
                    pool.wait_ge(*fr.empty(n, "AT"))
                    if has(n, 1):
                        pool.wait_ge(*bk.full(n - 1, f"UT{DB - 1}"))
                    for s in range(1, LEVELS):
                        pool.tensor_tensor(CT[:, s - 1], AT, masks[:, s].unsqueeze(1).to_broadcast([P, GT, P]),
                                           ALU.mult).then_inc(masked, 1)

            def back(slot, b, it):
                n = 2 * it + b
                if slot == 12:
                    settled(pool, w_in, 16 * (n + 1))
                    wscaled = wstage[:, 0:1, :]
                    pool.tensor_scalar(wscaled, wscaled, W_SCALE, None, ALU.mult).then_inc(w_scaled, 1)
                    pool.wait_ge(w_scaled, 2 * n + 1)
                    pool.tensor_copy(piece(n, 0), wscaled).then_inc(w_scaled, 1)
                    pool.wait_ge(w_scaled, 2 * n + 2)
                    pool.tensor_tensor(piece(n, 1), wscaled, piece(n, 0), ALU.subtract).then_inc(w_split, 1)
                if slot == 16:
                    pool.wait_ge(o_mean, n + 1)
                    pool.tensor_tensor(oss, oss, minus_half, ALU.pow).then_inc(o_rms, 1)

            def tail(slot, b, it):
                n = 2 * it + b
                if slot == 5:
                    pool.wait_ge(stats2, 3 * n + 3)
                    pool.tensor_tensor(rstd2, rstd2, minus_half[:, 0:GT], ALU.pow).then_inc(rstd2_ready, 1)
                if slot == 8:
                    pool.wait_ge(x2n_ready, GT * n + GT)
                    pool.tensor_tensor(xr, xr, x2n, ALU.add).then_inc(base_ready, 1)

            def ahead(slot, b, it):
                n = 2 * it + b
                if slot == 9:
                    pool.wait_ge(stats, 3 * n + 3)
                    pool.tensor_tensor(rstd, rstd, minus_half[:, 0:GT], ALU.pow).then_inc(rstd_ready, 1)

            run_attention(pool, front, back, tail, ahead)

            pool.memset(idx[:], 0).then_inc(rows_zeroed, 1)
            pool.wait_ge(rows_zeroed, 1)
            pool.dma_start(rows_d.rearrange("(p c) a -> p (c a)", p=P), idx[:]).then_inc(rows_out, 16)
            pool.wait_ge(rows_out, 16)
            pool.wait_ge(routed, 1)
            pool.wait_ge(route_in, 96)

            def scatter(t, b, h):
                if has(h, 1):
                    pool.wait_ge(scattered[b], 16 * TOPK * h)
                for c in range(TOPK):
                    pool.tensor_copy(scat[:, b, c:c + 1], adr[:, c, bass.ds(t, 1)]).then_inc(scat_copied, 1)
                pool.tensor_copy(scat[:, b, TOPK:], tid[:, bass.ds(t, 1)]).then_inc(scat_copied, 1)
                settled(pool, scat_copied, 3 * t + 3)
                for c in range(TOPK):
                    pool.indirect_dma_start(
                        out=rows_d, out_offset=bass.IndirectOffsetOnAxis(ap=scat[:, b, c:c + 1], axis=0),
                        in_=scat[:, b, TOPK:], in_offset=None).then_inc(scattered[b], 16)

            for b in range(2):
                scatter(b, b, 0)
            with pool.Fori(1, TTOK // 2) as k:
                for b in range(2):
                    scatter(2 * k + b, b, k)
            for b in range(2):
                pool.wait_ge(scattered[b], 16 * TOPK * TTOK // 2)
            pool.dma_start(idx[:], rows_d.rearrange("(p c) a -> p (c a)", p=P)).then_inc(idx_in, 16)

            def gather(i, b, h):
                pool.wait_ge(x_turned, i + S_TILES - 1)
                if has(h, 1):
                    pool.wait_ge(x_gathered[b], 16 * XB * h)
                pool.tensor_copy(gath[:, b, :], idx[:, bass.ds(i * XB, XB)]).then_inc(gath_copied, 1)
                settled(pool, gath_copied, i + 1)
                for c in range(XB):
                    pool.indirect_dma_start(
                        out=xg[b][:, c], out_offset=None, in_=x2n_d,
                        in_offset=bass.IndirectOffsetOnAxis(ap=gath[:, b, c:c + 1], axis=0)).then_inc(x_gathered[b], 16)

            pool.wait_ge(idx_in, 16)
            for b in range(2):
                gather(b, b, 0)
            with pool.Fori(1, R_TILES // 2) as k:
                for b in range(2):
                    gather(2 * k + b, b, k)
            for i in range(R_TILES // 2 * 2, R_TILES):
                gather(i, i % 2, i // 2)

            for b in range(2):
                pool.wait_ge(y_stored[b], 16 * (S_TILES // 2 + routed_on(b)))

            def fetch(v, m):
                if has(v, 1):
                    pool.wait_ge(combined, COMBINES * v + (TOPK * (m + 1) - COMBINES))
                t = 2 * v + (m if m < XB else TTOK // 2 + m - XB)
                pool.tensor_copy(lastidx[:, m, :], pos_i[:, :, bass.ds(t, 1)].rearrange("p a b -> p (a b)")).then_inc(gath_copied, 1)
                settled(pool, gath_copied, 2 * XB * v + (R_TILES + m + 1))
                for c in range(TOPK):
                    pool.indirect_dma_start(
                        out=yrow[m][:, c], out_offset=None, in_=ys_d,
                        in_offset=bass.IndirectOffsetOnAxis(ap=lastidx[:, m, c:c + 1], axis=0)).then_inc(y_in[m], 16)

            for m in range(2 * XB):
                fetch(0, m)
            with pool.Fori(1, S_TILES) as v:
                for m in range(2 * XB):
                    fetch(v, m)

        @block.scalar
        def _(act):
            act.wait_ge(consts_made, CONSTS_MADE)
            act.wait_ge(const_in, CONSTS_IN)

            def put(ring, n, name, dst):
                act.wait_ge(*ring.full(n, name))
                act.copy(dst, ring.bank(name)).then_inc(ring.empty(n, name)[0], 1)

            def front(slot, b, it):
                n = 2 * it + b

                def silu(m):
                    act.wait_ge(conv_step, 3 * DB * (TAPS - 1) * n + (TAPS - 1) * (m + 1))
                    act.activation(qkvT[:, m], qkvT[:, m], ACT.Silu).then_inc(silu_done, 1)
                    if m < 2 * DB:
                        act.wait_ge(silu_done, 3 * DB * n + m + 1)
                        act.activation(sqT[:, m], qkvT[:, m], ACT.Square).then_inc(squares, 1)

                def project(m):
                    if m == 0:
                        act.wait_ge(hist_saved, n + 1)
                        if has(n, 1):
                            act.wait_ge(*fr.full(n - 1, "tokV1"))
                    act.wait_ge(*fr.full(n, f"proj{m}"))
                    act.copy(pre[:, m, TAPS - 1:], fr.bank(f"proj{m}")).then_inc(pre_ready, 1)
                    act.activation(qkvT[:, m], fr.bank(f"proj{m}"), ACT.Copy,
                                   scale=cw[:, m, TAPS - 1:TAPS]).then_inc(fr.empty(n, f"proj{m}")[0], 1)

                if slot < 10 and slot % 2:
                    project(slot // 2)
                    if slot >= 3:
                        silu(slot // 2 - 1)
                if slot == 10:
                    project(5)
                    act.wait_ge(sumsq, n + 1)
                    act.copy(ssq, ssq_ps).then_inc(sumsq_kept, 1)
                if slot == 11:
                    silu(4)
                if slot == 12:
                    silu(5)
                if slot == 13:
                    for name, to in (("KT", KT), ("KbT", KbT)):
                        for d in range(DB):
                            put(fr, n, f"{name}{d}", to[:, d])
                if slot == 14:
                    put(fr, n, "AT", AT.rearrange("p k t -> p (k t)"))
                if slot == 15:
                    for d in range(DB):
                        put(fr, n, f"QT{d}", QT[:, d])

            def back(slot, b, it):
                n = 2 * it + b
                if slot < 10 and slot % 2 == 0:
                    put(bk, n, f"Y{slot // 2 + 1}", Y.rearrange("p k t -> p (k t)"))
                if slot == 14:
                    act.wait_ge(o_ready, n + 1)
                    for d in range(DB):
                        act.activation(osqT[:, d], oT[:, d], ACT.Square).then_inc(o_sq, 1)

            def tail(slot, b, it):
                n = 2 * it + b
                if slot in (2, 3):
                    d = slot - 2
                    put(tl, n, f"oT{d}", oT[:, d])
                if slot == 7:
                    act.wait_ge(nmr2_ready, n + 1)
                    for k in range(GT):
                        act.activation(x2n[:, k], xr[:, k], ACT.Identity, bias=nmr2[:, k:k + 1],
                                       scale=rstd2[:, k:k + 1]).then_inc(x2n_ready, 1)
                if slot in (8, 9):
                    d = slot - 8
                    put(tl, n, f"x2nT{d}", x2nT[:, d])

            def ahead(slot, b, it):
                n = 2 * it + b
                if slot == 11:
                    act.wait_ge(nmr_ready, n + 1)
                    if has(n, 1):
                        act.wait_ge(*ah.full(n - 1, "xnT1"))
                    for k in range(GT):
                        act.activation(xn[:, k], xl[:, k], ACT.Identity, bias=nmr[:, k:k + 1],
                                       scale=rstd[:, k:k + 1]).then_inc(xn_ready, 1)
                if slot == 16:
                    for d in range(DB):
                        put(ah, n, f"xnT{d}", xnT[:, d])
                if slot == 17:
                    act.wait_ge(*ah.full(n, "beta"))
                    if has(n, 1):
                        act.wait_ge(beta_ready, n)
                    act.activation(th, ah.bank("beta")[:, 0:GT * NH], ACT.Tanh,
                                   scale=0.5).then_inc(ah.empty(n, "beta")[0], 1)

            run_attention(act, front, back, tail, ahead)
            act.drain().then_inc(act_idle, 1)

            act.wait_ge(kept, 1)
            act.activation(scr["sc"], logits[:], ACT.Sigmoid).then_inc(scored, 1)
            act.wait_ge(route, 1)
            act.activation(scr["bl"], scr["z"], ACT.Sigmoid).then_inc(scored, 1)
            def x_high_half(t):
                act.wait_ge(x_turned, t.seq + 1)
                if has(t.seq, 2):
                    act.wait_ge(up_done, 4 * ups_before(t))
                act.activation(xs[t.par][:, 0].rearrange("p d t -> p (d t)"), ps[:, 6, :], ACT.Copy,
                               scale=X_SCALE).then_inc(x_high, 1)

            def unit(n, b):
                def gelu(c):
                    act.wait_ge(up_done, 4 * n + c + 1)
                    act.activation(ps[:, c, :], ps[:, c, :], ACT.Gelu,
                                   scale=1.0 / (X_SCALE * W_SCALE)).then_inc(gelu_done, 1)

                def high(c):
                    act.wait_ge(gelu_done, 4 * n + c + 1)
                    act.activation(hs[b][:, 0, 2 * c:2 * c + 2].rearrange("p f t -> p (f t)"), ps[:, c, :],
                                   ACT.Copy, scale=H_SCALE).then_inc(h_high, 1)

                gelu(0)
                if has(n, 2):
                    act.wait_ge(down_done, n - 1)
                for c in range(1, 4):
                    gelu(c)
                    high(c - 1)
                high(3)

            def shared_unit(t, e):
                unit(*t.unit(e))
                if t.phase == 0:
                    n = t.unit(e)[0]
                    for q in range(2):
                        act.wait_ge(rw_in[q], 16 * (n + 1))
                        act.activation(piece(2 * n + (SH_PIECES + q), 0), wstage[:, q:q + 1, :], ACT.Copy,
                                       scale=W_SCALE).then_inc(rw_high, 1)

            def nothing(*_):
                pass

            shared_order(act, 0, x_high_half, shared_unit, nothing)
            routed_order(act, x_high_half, lambda t: unit(*t.unit()), nothing)

            act.wait_ge(picked, 1)
            for c in range(TOPK):
                act.activation(wtop[:, c], score_diff[:], ACT.Sigmoid, scale=1.0 - 2.0 * c).then_inc(tops_ready, 1)
            shared_order(act, 2, x_high_half, shared_unit, nothing)

        @block.tensor
        def _(pe):
            pe.wait_ge(consts_made, CONSTS_MADE)
            pe.wait_ge(const_in, CONSTS_IN)

            def fill(ring, n, name):
                if has(n, 1) or ring.at[name] >= len(ring.banks):
                    pe.wait_ge(*ring.free(n, name))
                return ring.bank(name)

            def by_tile(ring, n, name, product):
                to = fill(ring, n, name)
                for k in range(GT):
                    last = product(to[:, k * P:(k + 1) * P], k)
                last.then_inc(ring.sem_full, 1)

            def turn_back(ring, n, name, src, d):
                by_tile(ring, n, name, lambda to, k: pe.transpose(to, src[:, k, d * P:(d + 1) * P], idt[:]))

            def turn_out(ring, n, name, src, h):
                to = fill(ring, n, name)
                for k in range(2):
                    for d in range(DB):
                        last = pe.transpose(to[:, k * D + d * P:k * D + (d + 1) * P],
                                            src[:, d, (2 * h + k) * P:(2 * h + k + 1) * P], idt[:])
                last.then_inc(ring.sem_full, 1)

            def head_sums(dst, src):
                for k in range(GT):
                    for d in range(DB):
                        at = k * NH + d * (P // HD)
                        last = pe.matmul(dst[:, at:at + P // HD], src[:, d, k * P:(k + 1) * P], headsel,
                                         start=True, stop=True)
                return last

            def front(slot, b, it):
                n = 2 * it + b

                def project(m, d):
                    to = fill(fr, n, f"proj{m}") if d == 0 else fr.bank(f"proj{m}")
                    mm = pe.matmul(to, wqkv[:, d, m * P:(m + 1) * P], xnT[:, d], start=(d == 0), stop=(d == DB - 1))
                    if d == DB - 1:
                        mm.then_inc(fr.sem_full, 1)

                if slot == 0:
                    for d in range(DB):
                        pe.wait_ge(*ah.empty(n, f"xnT{d}"))
                if slot < 10:
                    project(slot // 2, slot % 2)
                if slot == 10:
                    for d in range(DB):
                        project(5, d)
                    if has(n, 2):
                        pe.wait_ge(o_mean, n - 1)
                    pe.wait_ge(squares, 2 * DB * (n + 1))
                    for i in range(2):
                        last = head_sums(ssq_ps[:, i], sqT[:, DB * (1 - i):DB * (2 - i)])
                    last.then_inc(sumsq, 1)
                if slot == 12:
                    pe.wait_ge(silu_done, 3 * DB * n + 2 * DB)
                    for h in range(2):
                        turn_out(fr, n, f"tokK{h}", qkvT[:, DB:2 * DB], h)
                if slot == 13:
                    pe.wait_ge(*fr.empty(n, "tokK1"))
                    for d in range(DB):
                        turn_back(fr, n, f"KT{d}", Kt, d)
                    pe.wait_ge(kb_ready, n + 1)
                    for d in range(DB):
                        turn_back(fr, n, f"KbT{d}", Kb, d)
                if slot == 14:
                    pe.wait_ge(*fr.empty(n, "KbT1"))
                    to = fill(fr, n, "AT")
                    for k in range(GT):
                        for d in range(DB):
                            last = pe.matmul(to[:, k * P:(k + 1) * P], KT[:, d, k * P:(k + 1) * P],
                                             KbT[:, d, k * P:(k + 1) * P], start=(d == 0), stop=(d == DB - 1))
                    last.then_inc(fr.sem_full, 1)
                    for h in range(2):
                        turn_out(fr, n, f"tokQ{h}", qkvT[:, 0:DB], h)
                if slot == 15:
                    pe.wait_ge(*fr.empty(n, "tokQ1"))
                    for d in range(DB):
                        turn_back(fr, n, f"QT{d}", Qt, d)
                    pe.wait_ge(silu_done, 3 * DB * (n + 1))
                    for h in range(2):
                        turn_out(fr, n, f"tokV{h}", qkvT[:, 2 * DB:], h)
                if slot == 17:
                    pe.wait_ge(x0t_ready, 2 * n + 2)
                    by_tile(fr, n, "X", lambda to, k: pe.transpose(to, XTr[:, k], idt[:]))

            def back(slot, b, it):
                n = 2 * it + b
                if slot < 10:
                    s = slot // 2 + 1
                    if slot % 2 == 0:
                        pe.wait_ge(masked, (LEVELS - 1) * n + s)
                        pe.wait_ge(*(fr.empty(n, "X") if s == 1 else bk.empty(n, f"Z{s - 1}")))
                        by_tile(bk, n, f"Y{s}", lambda to, k: pe.matmul(to, CT[:, s - 1, k], X[:, k], start=True, stop=True))
                    else:
                        if s > 1:
                            pe.wait_ge(*bk.empty(n, f"ZT{s - 1}"))
                        pe.wait_ge(*bk.empty(n, f"Y{s}"))
                        if s < LEVELS - 1:
                            by_tile(bk, n, f"Z{s}", lambda to, k: pe.matmul(to, XTr[:, k], Y[:, k], start=True, stop=True))
                        by_tile(bk, n, f"ZT{s}", lambda to, k: pe.matmul(to, Y[:, k], XTr[:, k], start=True, stop=True))
                if slot == W_SLOT:
                    pe.wait_ge(tt_ready, n + 1)
                    for w, src in (("W", Kb), ("U", Vb)):
                        for d in range(DB):
                            by_tile(bk, n, f"{w}T{d}", lambda to, k: pe.matmul(
                                to, src[:, k, d * P:(d + 1) * P], XTr[:, k], start=True, stop=True))
                if slot == 12:
                    pe.wait_ge(qk_ready, n + 1)
                    if has(n, 1):
                        pe.wait_ge(logits_kept, n)
                    else:
                        pe.wait_ge(sumsq_kept, 2)
                    for d in range(DB):
                        own = qk[:, d, :, 0:b + 1]
                        own = own.rearrange("p a b -> p (a b)") if b + 1 == BATCH else own[:, :, 0]
                        last = pe.matmul(corr_ps[:, 0:GCH * (b + 1)], ones, own, start=(d == 0), stop=(d == DB - 1))
                    last.then_inc(corr_mm, 1)
                if slot == 15:
                    pe.wait_ge(edge_u, 4 * (n + 1))
                    pe.wait_ge(o_sq, DB * (n + 1))
                    head_sums(oss_ps, osqT).then_inc(o_sum, 1)

            def tail(slot, b, it):
                n = 2 * it + b
                if slot in (0, 1):
                    if slot == 0:
                        last = GROUPS - 1 if isinstance(n, int) and n + 2 >= GROUPS else n + 2
                        pe.wait_ge(*ah.empty(last, "beta"))
                    turn_out(tl, n, f"otok{slot}", oT, slot)
                if slot in (2, 3):
                    pe.wait_ge(*tl.empty(n, "otok1"))
                    turn_back(tl, n, f"oT{slot - 2}", ob, slot - 2)
                if slot in (4, 5):
                    h = slot - 4
                    for d in range(DB):
                        pe.wait_ge(*tl.empty(n, f"oT{d}"))
                    pe.wait_ge(wo_scaled, DB)
                    to = fill(tl, n, f"attn{h}")
                    for k in range(2):
                        for d in range(DB):
                            last = pe.matmul(to[:, k * D:(k + 1) * D], oT[:, d, (2 * h + k) * P:(2 * h + k + 1) * P],
                                             wo[:, d], start=(d == 0), stop=(d == DB - 1))
                    last.then_inc(tl.sem_full, 1)
                if slot in (8, 9):
                    pe.wait_ge(x2n_ready, GT * (n + 1))
                    turn_back(tl, n, f"x2nT{slot - 8}", x2n, slot - 8)
                if slot == 11:
                    for d in range(DB):
                        pe.wait_ge(*tl.empty(n, f"x2nT{d}"))
                    pe.wait_ge(o_mean, n + 1)
                    if not isinstance(n, int) or n + 2 < GROUPS:
                        pe.wait_ge(sumsq_kept, n + 3)
                    for k in range(GT):
                        for d in range(DB):
                            last = pe.matmul(logit_ps[:, k * N_RT:(k + 1) * N_RT], x2nT[:, d, k * P:(k + 1) * P], cen[:, d],
                                             start=(d == 0), stop=(d == DB - 1))
                    last.then_inc(logit_mm, 1)

            def ahead(slot, b, it):
                n = 2 * it + b
                if slot == 16:
                    pe.wait_ge(xn_ready, GT * (n + 1))
                    if has(n, 3):
                        pe.wait_ge(*tl.empty(n - 3, f"x2nT{DB - 1}"))
                    for d in range(DB):
                        turn_back(ah, n, f"xnT{d}", xn, d)
                if slot == 17:
                    for d in range(DB):
                        pe.wait_ge(*ah.empty(n, f"xnT{d}"))
                    to = fill(ah, n, "beta")
                    for k in range(GT):
                        for d in range(DB):
                            last = pe.matmul(to[:, k * NH:(k + 1) * NH], xnT[:, d, k * P:(k + 1) * P], wb[:, d],
                                             start=(d == 0), stop=(d == DB - 1))
                    last.then_inc(ah.sem_full, 1)

            run_attention(pe, front, back, tail, ahead)
            pe.drain().then_inc(pe_idle, 1)

            def rank_rows():
                pe.wait_ge(mask_ready, 1)
                pe.wait_ge(route_in, 96)
                maskf = scr["mask"].rearrange("p t e -> p (t e)")
                pe.matmul(ps[:, 7, 0:TTOK * N_RT], scr["rc"][:, 0], maskf, start=True, stop=True)
                pe.matmul(ps[:, 7, TTOK * N_RT:2 * TTOK * N_RT], scr["rc"][:, 1], maskf,
                          start=True, stop=True).then_inc(ranked, 1)

            def turn(t):
                pe.wait_ge(*x_there(t))
                if has(t.seq, 1):
                    pe.wait_ge(x_low, t.seq)
                for d in range(DB):
                    for c in range(XB):
                        last = pe.transpose(ps[:, 6, d * XT + c * P:d * XT + (c + 1) * P],
                                            xg[t.par][:, c, d * P:(d + 1) * P], idt[:])
                last.then_inc(x_turned, 1)

            def up(t, e, slot):
                n = t.unit(e)[0]
                pe.wait_ge(x_low, t.seq + 1)
                for c in range(4):
                    if has(n, 1):
                        pe.wait_ge(h_low, 4 * n + (c - 3))
                    for f in range(2):
                        cols = slice((2 * c + f) * P, (2 * c + f + 1) * P)
                        parts = [(d, hw, hx) for d in range(DB) for hw, hx in ((0, 0), (0, 1), (1, 0))]
                        for q, (d, hw, hx) in enumerate(parts):
                            last = pe.matmul(ps[:, c, f * XT:(f + 1) * XT], weight(slot, d, hw, cols), xs[t.par][:, hx, d],
                                             start=(q == 0), stop=(q == len(parts) - 1))
                    last.then_inc(up_done, 1)

            def down(t, e, slot):
                n, b = t.unit(e)
                pe.wait_ge(h_low, 4 * n + 4)
                if has(n, 2):
                    pe.wait_ge(y_out, n - 1)
                for c in range(XB):
                    parts = [(f, hh, hw) for f in range(FB) for hh, hw in ((0, 0), (0, 1), (1, 0))]
                    for q, (f, hh, hw) in enumerate(parts):
                        cols = slice(f % 4 * D, (f % 4 + 1) * D)
                        last = pe.matmul(ps[:, 4 + b, c * D:(c + 1) * D], hs[b][:, hh, f, c * P:(c + 1) * P],
                                         weight(slot, DB + f // 4, hw, cols), start=(q == 0), stop=(q == len(parts) - 1))
                last.then_inc(down_done, 1)

            pe.wait_ge(w_split, SH_PIECES)
            pe.wait_ge(kept, 1)

            def between(step):
                if step == RANK_STEP:
                    rank_rows()

            def shared_up(t, e):
                up(t, e, e)

            def shared_down(t, e):
                down(t, e, e)

            shared_order(pe, 0, turn, shared_up, shared_down, between)

            pe.wait_ge(routed, 2)
            pe.wait_ge(rw_low, N_RT * PIECES)

            def expert_of(t):
                return pe.value_load(eid[0:1, bass.ds(t.v, 1)], min_val=N_SH * PIECES, max_val=(SLOTS - 1) * PIECES)

            routed_order(pe, turn, lambda t: up(t, 0, expert_of(t)), lambda t: down(t, 0, expert_of(t)))
            shared_order(pe, 2, turn, shared_up, shared_down)

        @block.vector
        def _(dve):
            dve.wait_ge(consts_made, CONSTS_MADE)
            dve.wait_ge(const_in, CONSTS_IN)
            for d in range(DB):
                dve.tensor_scalar(wo[:, d], wo[:, d], gcol[:, d:d + 1], None, ALU.mult).then_inc(wo_scaled, 1)

            def layer_stats(n, src, b6, m2, rs, counted):
                for k in range(GT):
                    last = dve.bn_stats(b6[:, k], src[:, k])
                last.then_inc(counted, 1)
                settled(dve, counted, 3 * n + 1)
                for k in range(GT):
                    last = dve.bn_aggr(m2[:, k], b6[:, k])
                last.then_inc(counted, 1)
                dve.wait_ge(counted, 3 * n + 2)
                dve.tensor_scalar(rs, m2[:, :, 1], EPS, None, ALU.add).then_inc(counted, 1)

            def by_head(a):
                return a.unsqueeze(2).to_broadcast([P, a.shape[-1], HD])

            def heads(a):
                return a.rearrange("p k (h e) -> p (k h) e", h=NH)

            def bank_heads(a):
                return a.rearrange("p (g e) -> p g e", e=HD)

            def front(slot, b, it):
                n = 2 * it + b

                def convolve(m):
                    at = 3 * DB * (TAPS - 1) * n + (TAPS - 1) * m
                    dve.wait_ge(*fr.empty(n, f"proj{m}"))
                    for t in range(TAPS - 1):
                        if t:
                            dve.wait_ge(conv_step, at + t)
                        dve.scalar_tensor_tensor(qkvT[:, m], pre[:, m, t:t + GRP], cw[:, m, t:t + 1],
                                                 qkvT[:, m], ALU.mult, ALU.add).then_inc(conv_step, 1)

                if slot == 0:
                    dve.tensor_copy(pre[:, :, 0:TAPS - 1], hist[b]).then_inc(hist_saved, 1)
                    dve.wait_ge(hist_saved, n + 1)
                if slot <= 10 and slot % 2 == 0 and slot >= 2:
                    convolve(slot // 2 - 1)
                if slot == 11:
                    convolve(5)
                    dve.tensor_copy(hist[b], pre[:, :, GRP:GRP + TAPS - 1]).then_inc(hist_set, 1)
                if slot in (12, 14):
                    c, i, to = ("K", 0, Kt) if slot == 12 else ("Q", 1, Qt)
                    dve.wait_ge(rnorm, 2 * n + i + 1)
                    for h in range(2):
                        name = f"tok{c}{h}"
                        dve.wait_ge(*fr.full(n, name))
                        dve.tensor_tensor(heads(to[:, 2 * h:2 * h + 2]), bank_heads(fr.bank(name)),
                                          by_head(ssq[:, i, 2 * NH * h:2 * NH * (h + 1)]), ALU.mult).then_inc(fr.empty(n, name)[0], 1)
                if slot == 12:
                    dve.wait_ge(*fr.empty(n, "tokK1"))
                    dve.wait_ge(beta_ready, n + 1)
                    if has(n, 1):
                        dve.wait_ge(*bk.full(n - 1, f"UT{DB - 1}"))
                    dve.tensor_tensor(heads(Kb), heads(Kt), by_head(beta[b]), ALU.mult).then_inc(kb_ready, 1)
                if slot == 15:
                    dve.wait_ge(*fr.empty(n, "AT"))
                    dve.tensor_tensor(XTr, AT, masks[:, 0].unsqueeze(1).to_broadcast([P, GT, P]), ALU.mult).then_inc(x0t_ready, 1)
                    dve.wait_ge(x0t_ready, 2 * n + 1)
                    dve.tensor_tensor(XTr, XTr, idt[:].unsqueeze(1).to_broadcast([P, GT, P]), ALU.add).then_inc(x0t_ready, 1)
                    for h in range(2):
                        name = f"tokV{h}"
                        dve.wait_ge(*fr.full(n, name))
                        dve.tensor_tensor(heads(Vb[:, 2 * h:2 * h + 2]), bank_heads(fr.bank(name)),
                                          by_head(beta[b][:, 2 * NH * h:2 * NH * (h + 1)]), ALU.mult).then_inc(fr.empty(n, name)[0], 1)
                if slot == 17:
                    dve.wait_ge(*fr.full(n, "X"))
                    dve.tensor_copy(X.rearrange("p k t -> p (k t)"), fr.bank("X")).then_inc(fr.empty(n, "X")[0], 1)

            def back(slot, b, it):
                n = 2 * it + b
                e = b + 1

                def chunks(a):
                    return a.rearrange("p d (c t) -> p d c t", t=CH)

                def flat(a):
                    return a.rearrange("p k t -> p (k t)")

                if slot < 10 and slot % 2:
                    s = slot // 2 + 1
                    for name, to in ((f"Z{s}", X), (f"ZT{s}", XTr)):
                        if s < LEVELS - 1 or to is XTr:
                            dve.wait_ge(*bk.full(n, name))
                            dve.tensor_tensor(flat(to), flat(to), bk.bank(name), ALU.add).then_inc(bk.empty(n, name)[0], 1)
                    if s == LEVELS - 1:
                        dve.wait_ge(*bk.empty(n, f"ZT{s}"))
                        dve.scalar_tensor_tensor(XTr, XTr, 3.0, minus2i.unsqueeze(1).to_broadcast([P, GT, P]),
                                                 ALU.mult, ALU.add).then_inc(tt_ready, 1)
                if slot == W_SLOT:
                    if has(n, 1):
                        dve.wait_ge(corr_mm, n)
                    dve.tensor_tensor(qk[:, :, :, 0:e], chunks(QT)[:, :, :, 0:e], chunks(KT)[:, :, :, 0:e],
                                      ALU.mult).then_inc(qk_ready, 1)
                    for i, w in enumerate("WU"):
                        for d in range(DB):
                            name = f"{w}T{d}"
                            dve.wait_ge(*bk.full(n, name))
                            dve.tensor_tensor(prod[:, DB * i + d], bk.bank(name), KT[:, d], ALU.mult).then_inc(products, 1)
                            dve.tensor_copy(Wc[:, i, d, :, 0:e],
                                            bk.bank(name).rearrange("p (c t) -> p c t", t=CH)[:, :, 0:e]).then_inc(bk.empty(n, name)[0], 1)
                if slot == 13:
                    dve.tensor_copy(Sd[b][:, :, 0:1], Sd[b][:, :, GCH:GCH + 1]).then_inc(carry, 1)
                    dve.wait_ge(products, 4 * n + 4)
                    dve.tensor_reduce(PR.rearrange("p a d c -> p (a d c)"),
                                      prod.rearrange("p a (c t) -> p (a c) t", t=CH), AX_X, ALU.add).then_inc(chunk_sums, 1)
                    dve.wait_ge(chunk_sums, n + 1)
                    dve.tensor_scalar(PR[:, 0], PR[:, 0], -1.0, 1.0, ALU.mult, ALU.add).then_inc(one_minus, 1)
                    dve.wait_ge(one_minus, n + 1)
                    dve.wait_ge(carry, n + 1)
                    for d in range(DB):
                        dve.tensor_tensor_scan(Sd[b][:, d, 1:GCH + 1], PR[:, 0, d], PR[:, 1, d], Sd[b][:, d, 0:1],
                                               ALU.mult, ALU.add).then_inc(scanned, 1)
                    dve.wait_ge(scanned, DB * (n + 1))
                    if has(n, 1):
                        dve.wait_ge(logit_mm, n)
                    before = Sd[b][:, :, 0:GCH].unsqueeze(3)
                    dve.tensor_tensor(chunks(oT), chunks(QT), before.to_broadcast([P, DB, GCH, CH]), ALU.mult).then_inc(edge_u, 1)
                    own = wu[:, :, :, 0:e]
                    dve.wait_ge(*bk.empty(n, "UT1"))
                    dve.tensor_tensor(own, Wc[:, 0, :, :, 0:e], before.to_broadcast([P, DB, GCH, e]), ALU.mult).then_inc(edge_u, 1)
                    dve.wait_ge(edge_u, 4 * n + 2)
                    dve.tensor_tensor(own, Wc[:, 1, :, :, 0:e], own, ALU.subtract).then_inc(edge_u, 1)
                    dve.wait_ge(edge_u, 4 * n + 3)
                    dve.wait_ge(corr_mm, n + 1)
                    dots = corr_ps[:, 0:GCH * e].rearrange("p (c t) -> p c t", t=e).unsqueeze(1)
                    dve.tensor_tensor(own, own, dots.to_broadcast([P, DB, GCH, e]), ALU.mult).then_inc(edge_u, 1)
                    dve.wait_ge(edge_u, 4 * n + 4)
                    dve.tensor_tensor(chunks(oT)[:, :, :, 0:e], chunks(oT)[:, :, :, 0:e], own, ALU.add).then_inc(o_ready, 1)
                if slot == 15:
                    dve.wait_ge(o_sum, n + 1)
                    dve.tensor_scalar(oss, oss_ps, 1.0 / HD, EPS, ALU.mult, ALU.add).then_inc(o_mean, 1)

            def tail(slot, b, it):
                n = 2 * it + b
                if slot in (0, 1):
                    if slot == 0:
                        dve.wait_ge(o_rms, n + 1)
                        if has(n, 1):
                            dve.wait_ge(tokens_out[1 - b], 32 * (it + b))
                            dve.wait_ge(*tl.full(n - 1, "x2nT1"))
                    h, name = slot, f"otok{slot}"
                    dve.wait_ge(*tl.full(n, name))
                    dve.tensor_tensor(heads(ob[:, 2 * h:2 * h + 2]), bank_heads(tl.bank(name)),
                                      by_head(oss[:, 2 * NH * h:2 * NH * (h + 1)]), ALU.mult).then_inc(tl.empty(n, name)[0], 1)
                if slot in (4, 5):
                    if slot == 4:
                        dve.wait_ge(xr_in[b], 16 * (it + 1))
                    h, name = slot - 4, f"attn{slot - 4}"
                    dve.wait_ge(*tl.full(n, name))
                    part = xr[:, 2 * h:2 * h + 2].rearrange("p k d -> p (k d)")
                    dve.tensor_tensor(part, part, tl.bank(name), ALU.add).then_inc(tl.empty(n, name)[0], 1)
                if slot == 5:
                    dve.wait_ge(*tl.empty(n, "attn1"))
                    layer_stats(n, xr, bn2, mv2, rstd2, stats2)
                if slot == 6:
                    dve.wait_ge(rstd2_ready, n + 1)
                    dve.scalar_tensor_tensor(nmr2, mv2[:, :, 0], -1.0, rstd2, ALU.mult, ALU.mult).then_inc(nmr2_ready, 1)
                if slot == 12:
                    dve.wait_ge(logit_mm, n + 1)
                    dve.tensor_copy(logits[:, bass.ds(b * (TTOK // BATCH) + GT * it, GT), :],
                                    logit_ps.rearrange("p (k e) -> p k e", e=N_RT)).then_inc(logits_kept, 1)

            def ahead(slot, b, it):
                n = 2 * it + b
                if slot == 8:
                    dve.wait_ge(xl_in[b], 16 * (it + 1))
                    layer_stats(n, xl, bn, mv, rstd, stats)
                if slot == 10:
                    dve.wait_ge(rstd_ready, n + 1)
                    dve.scalar_tensor_tensor(nmr, mv[:, :, 0], -1.0, rstd, ALU.mult, ALU.mult).then_inc(nmr_ready, 1)
                if slot == 18:
                    dve.wait_ge(*ah.empty(n, "beta"))
                    dve.tensor_scalar(beta[b], th, 0.5, 0.5, ALU.mult, ALU.add).then_inc(beta_ready, 1)

            run_attention(dve, front, back, tail, ahead)
            dve.wait_ge(logits_kept, GROUPS)
            dve.drain().then_inc(kept, 1)
            dve.wait_ge(route_in, 96)
            r = scr
            step = [0]

            def then(ins, s=route):
                step[0] += 1
                ins.then_inc(route, 1)
                dve.wait_ge(route, step[0])

            def over_tiles(a):
                return a.unsqueeze(1).to_broadcast([P, TTOK, a.shape[-1]])

            def over_experts(a):
                return a.unsqueeze(2).to_broadcast([P, a.shape[-1], N_RT])

            then(dve.tensor_tensor(r["z"], logits[:], over_tiles(r["biasc"]), ALU.add))
            then(dve.memset(r["onec"], 1.0))
            dve.wait_ge(scored, 2)

            def pick(hot):
                then(dve.tensor_reduce(r["m"], r["bl"], AX_X, ALU.max))
                then(dve.tensor_tensor(r["tmp"], r["bl"], over_experts(r["m"]), ALU.is_equal))
                then(dve.tensor_tensor(r["tmp"], r["tmp"], over_tiles(r["prefc"]), ALU.mult))
                then(dve.tensor_reduce(r["mx"], r["tmp"], AX_X, ALU.max))
                then(dve.tensor_tensor(hot, r["tmp"], over_experts(r["mx"]), ALU.is_equal))

            rank = ps[:, 7, 0:TTOK * N_RT].rearrange("p (t e) -> p t e", e=N_RT)
            count = ps[:, 7, TTOK * N_RT:2 * TTOK * N_RT].rearrange("p (t e) -> p t e", e=N_RT)

            def router(part):
                if part == 0:
                    pick(r["oh1"])
                    then(dve.scalar_tensor_tensor(r["bl"], r["oh1"], -2.0, r["bl"], ALU.mult, ALU.add))
                if part == 1:
                    pick(r["oh2"])
                    dve.tensor_tensor(r["mask"], r["oh1"], r["oh2"], ALU.add).then_inc(mask_ready, 1)
                if part == 2:
                    for c, hot in enumerate(("oh1", "oh2")):
                        then(dve.tensor_tensor(r["tmp"], r[hot], r["sc"], ALU.mult))
                        then(dve.tensor_reduce(r["s12"][:, c], r["tmp"], AX_X, ALU.add))
                    dve.tensor_tensor(score_diff[:], r["s12"][:, 0], r["s12"][:, 1], ALU.subtract).then_inc(picked, 1)
                if part == 3:
                    dve.wait_ge(ranked, 1)
                    for e in range(N_RT):
                        then(dve.tensor_tensor_scan(r["inc"][:, :, e], r["onec"], count[:, :, e], 0.0, ALU.mult, ALU.add))
                    whole = r["inc"][:, TTOK - 1, :].unsqueeze(2).to_broadcast([P, N_RT, X_TILES])
                    steps = r["kc"].unsqueeze(1).to_broadcast([P, N_RT, X_TILES])
                    then(dve.tensor_tensor(r["cmp"], whole, steps, ALU.is_gt))
                    then(dve.tensor_reduce(r["nb"], r["cmp"], AX_X, ALU.add))
                if part == 4:
                    then(dve.tensor_tensor_scan(r["tb"], r["onec"][:, 0:N_RT], r["nb"], 0.0, ALU.mult, ALU.add))
                    then(dve.tensor_tensor(r["start"], r["tb"], r["nb"], ALU.subtract))
                    then(dve.tensor_scalar(r["start"], r["start"], float(XT), None, ALU.mult))
                    then(dve.tensor_tensor(r["pos"], r["inc"], count, ALU.subtract))
                    then(dve.tensor_tensor(r["pos"], r["pos"], rank, ALU.add))
                    then(dve.tensor_tensor(r["pos"], r["pos"], over_tiles(r["start"]), ALU.add))
                if part == 5:
                    for c, hot in enumerate(("oh1", "oh2")):
                        then(dve.tensor_tensor(r["tmp"], r[hot], r["pos"], ALU.mult))
                        then(dve.tensor_reduce(r["p12"][:, c], r["tmp"], AX_X, ALU.add))
                    then(dve.tensor_copy(pos_i[:], r["p12"]))
                    then(dve.tensor_scalar(lane[:], pos_i[:], P - 1, None, ALU.bitwise_and))
                    then(dve.tensor_scalar(adr[:], pos_i[:], 7, None, ALU.logical_shift_right))
                    dve.scalar_tensor_tensor(adr[:], lane[:], float(IDX_COLS), adr[:], ALU.mult, ALU.add).then_inc(routed, 1)
                if part == 6:
                    tiles = r["tc"].unsqueeze(2).to_broadcast([P, R_TILES, N_RT])
                    ends = r["tb"].unsqueeze(1).to_broadcast([P, R_TILES, N_RT])
                    then(dve.tensor_tensor(r["cmpt"], ends, tiles, ALU.is_le))
                    then(dve.tensor_reduce(r["es"], r["cmpt"], AX_X, ALU.add))
                    then(dve.tensor_scalar(r["es"], r["es"], float(N_RT - 1), None, ALU.min))
                    dve.tensor_scalar(eid[:], r["es"], float(PIECES), float(SH_PIECES), ALU.mult, ALU.add).then_inc(routed, 1)

            def x_low_half(t):
                dve.wait_ge(x_high, t.seq + 1)
                hi, lo = (xs[t.par][:, q].rearrange("p d t -> p (d t)") for q in range(2))
                dve.scalar_tensor_tensor(lo, ps[:, 6, :], X_SCALE, hi, ALU.mult, ALU.subtract).then_inc(x_low, 1)

            def unit(n, b):
                for c in range(4):
                    dve.wait_ge(h_high, 4 * n + c + 1)
                    hi, lo = (hs[b][:, q, 2 * c:2 * c + 2].rearrange("p f t -> p (f t)") for q in range(2))
                    dve.scalar_tensor_tensor(lo, ps[:, c, :], H_SCALE, hi, ALU.mult, ALU.subtract).then_inc(h_low, 1)

            def shared_unit(t, e):
                unit(*t.unit(e))
                if t.phase == 0:
                    n = t.unit(e)[0]
                    for q in range(2):
                        dve.wait_ge(rw_high, 2 * n + (q + 1))
                        dve.scalar_tensor_tensor(piece(2 * n + (SH_PIECES + q), 1), wstage[:, q:q + 1, :], W_SCALE,
                                                 piece(2 * n + (SH_PIECES + q), 0), ALU.mult, ALU.subtract).then_inc(rw_low, 1)

            def combine(v, m, sums, t):
                dve.wait_ge(y_in[m], 32 * (v + 1))
                for c in range(TOPK):
                    if c:
                        dve.wait_ge(combined, COMBINES * v + (TOPK * m + c))
                    dve.scalar_tensor_tensor(sums, yrow[m][:, c], wtop[:, c, bass.ds(t, 1)], sums,
                                             ALU.mult, ALU.add).then_inc(combined, 1)

            def y_shared(t, e):
                n, b = t.unit(e)
                dve.wait_ge(down_done, n + 1)
                if e == 0:
                    dve.wait_ge(*shared_in(base_in[t.par], t))
                    if t.phase or has(t.v, 2):
                        dve.wait_ge(y_stored[t.par], 16 * y_stores(t))
                else:
                    dve.wait_ge(y_out, n)
                flat = lambda a: a.rearrange("p k d -> p (k d)")
                dve.scalar_tensor_tensor(flat(yo[t.par]), ps[:, 4 + b, :], 1.0 / (H_SCALE * W_SCALE),
                                         flat(bt[t.par] if e == 0 else yo[t.par]), ALU.mult, ALU.add).then_inc(y_out, 1)
                if t.phase == 2 and e == 0:
                    for j in range(XB):
                        dve.wait_ge(acc_in[j], 16 * (t.v + 1))
                        combine(t.v, j, acc[j], 2 * t.v + j)
                if t.phase == 2 and e == 1:
                    dve.wait_ge(y_out, n + 1)
                    for j in range(XB):
                        combine(t.v, XB + j, yo[t.par][:, j], 2 * t.v + (TTOK // 2 + j))

            def y_routed(t):
                n, b = t.unit()
                dve.wait_ge(down_done, n + 1)
                dve.wait_ge(y_stored[b], 16 * y_stores(t))
                dve.tensor_scalar(yo[b].rearrange("p k d -> p (k d)"), ps[:, 4 + b, :],
                                  1.0 / (H_SCALE * W_SCALE), None, ALU.mult).then_inc(y_out, 1)

            shared_order(dve, 0, x_low_half, shared_unit, y_shared, between=router)
            routed_order(dve, x_low_half, lambda t: unit(*t.unit()), y_routed)
            dve.wait_ge(tops_ready, TOPK)
            shared_order(dve, 2, x_low_half, shared_unit, y_shared)


def run_attention(eng, front, back, tail, ahead):

    def tick(t=None, b=None, f=None, a=None):
        for slot in range(SLOTS_A):
            for stage, at in ((back, b), (tail, t), (front, f), (ahead, a)):
                if at:
                    stage(slot, *at)

    tick(a=(0, 0))
    tick(f=(0, 0), a=(1, 0))
    tick(b=(0, 0), f=(1, 0), a=(0, 1))
    tick(t=(0, 0), b=(1, 0), f=(0, 1), a=(1, 1))
    with eng.Fori(0, ROUNDS - 2) as it:
        tick(t=(1, it), b=(0, it + 1), f=(1, it + 1), a=(0, it + 2))
        tick(t=(0, it + 1), b=(1, it + 1), f=(0, it + 2), a=(1, it + 2))
    r = ROUNDS - 1
    tick(t=(1, r - 1), b=(0, r), f=(1, r))
    tick(t=(0, r), b=(1, r))
    tick(t=(1, r))


def constants():
    i = np.arange(P)
    same = (i[:, None] // CH) == (i[None, :] // CH)
    masks = np.zeros((P, LEVELS, P), np.float32)
    for s in range(LEVELS):
        w = 1 << s
        joined = same & (i[:, None] // (2 * w) == i[None, :] // (2 * w))
        joined &= ((i[:, None] // w) % 2 == 0) & ((i[None, :] // w) % 2 == 1)
        masks[:, s][joined] = -1.0
    eye = np.eye(P, dtype=np.float32)
    before = np.stack([(i[:, None] < i[None, :]), np.ones((P, P))], axis=1).astype(np.float32)

    def row(a):
        return np.ascontiguousarray(np.broadcast_to(np.asarray(a, np.float32), (P, len(a))))

    return {
        "ident": eye, "lvl_masks": masks, "eye2": -2.0 * eye, "head_sel": (i[:, None] // HD == np.arange(P // HD)).astype(np.float32), "block_tri": before,
        "row_iota": row(XT * np.arange(X_TILES)), "tile_iota": row(np.arange(R_TILES)),
        "pref": row(N_RT - np.arange(N_RT)),
        "tok_id": (P * np.arange(TTOK)[None, :] + i[:, None]).astype(np.int32),
    }


def laid_out(i):
    def split(w):
        return np.ascontiguousarray(np.asarray(w).reshape(-1, P, w.shape[-1]).transpose(1, 0, 2))

    conv = np.concatenate([i[f"L0_attn_conv_{c}"].reshape(D, TAPS) for c in "qkv"])
    up = np.concatenate([i["L0_ffn_Wfc_sh"], i["L0_ffn_Wfc_r"]]).transpose(0, 2, 1)
    down = np.concatenate([i["L0_ffn_Wproj_sh"], i["L0_ffn_Wproj_r"]]).transpose(0, 2, 1)
    up = up.reshape(SLOTS, DB, P, PIECE)
    down = down.reshape(SLOTS, FB, P, D).transpose(0, 2, 1, 3).reshape(SLOTS, P, PIECES // 2, PIECE).transpose(0, 2, 1, 3)
    return {
        "x": i["L0_attn_x"].reshape(TOK, D),
        "w_qkv": split(np.concatenate([i[f"L0_attn_W{c}"] for c in "qkv"], axis=1)),
        "w_beta": split(i["L0_attn_Wb"]),
        "conv_w": split(conv),
        "g_col": split(np.tile(i["L0_attn_g"], NH)[:, None])[:, :, 0],
        "w_o": split(i["L0_attn_Wo"]),
        "cent": split(i["L0_ffn_centroids"].T),
        "bias": np.ascontiguousarray(np.broadcast_to(i["L0_ffn_routing_bias"], (P, N_RT))),
        "w_ffn": np.concatenate([up, down], axis=1).reshape(SLOTS * PIECES, P, PIECE),
    }


_ORDER = ["x", "w_qkv", "w_beta", "conv_w", "g_col", "w_o", "cent", "bias", "w_ffn",
          "ident", "lvl_masks", "eye2", "head_sel", "block_tri", "row_iota", "tile_iota", "pref", "tok_id"]


def kernel(**inputs):
    import concourse.bacc as bacc
    from concourse.bass_utils import run_bass_kernel_spmd

    arrays = {**laid_out({k: np.asarray(v) for k, v in inputs.items()}), **constants()}
    nc = bacc.Bacc("TRN2", target_bir_lowering=False, num_devices=1)
    args = [nc.dram_tensor(f"in_{n}", arrays[n].shape, mybir.dt.from_np(arrays[n].dtype), kind="ExternalInput").ap()
            for n in _ORDER]
    out = nc.dram_tensor("out", (TOK, D), F32, kind="ExternalOutput").ap()
    build(nc, *args, out)
    feed = {f"in_{n}": np.ascontiguousarray(arrays[n]) for n in _ORDER}
    r = run_bass_kernel_spmd(nc, [feed], core_ids=[0])
    return r.results[0]["out"].reshape(BATCH, SEQ, D)
```
